# Optimizing a Trainium2 kernel written in Bass

```python
import numpy as np
import jax
import jax.numpy as jnp

def _softmax(x, axis=-1):
    return jax.nn.softmax(x, axis=axis)

def _gelu(x):
    return jax.nn.gelu(x, approximate=True)

def _silu(x):
    return jax.nn.silu(x)

def _sigmoid(x):
    return jax.nn.sigmoid(x)

def _layernorm(x, axis=-1, eps=1e-05):
    m = jnp.mean(x, axis=axis, keepdims=True)
    v = jnp.var(x, axis=axis, keepdims=True)
    return (x - m) / jnp.sqrt(v + eps)

def _scatter_add(tgt, idx, src, axis=0):
    return tgt.at[idx].add(src)

def _segment_sum(src, seg, n):
    return jax.ops.segment_sum(src, seg, n)
kernel_name = 'mk_decoder_postln_d2_seqx_r8_f0a696'

def setup_inputs(seed: int=0):
    np.random.seed(seed)
    _w = jnp.asarray

    def _rec_inputs():
        import jax
        import jax.numpy as jnp
        _rk = jax.random.key(seed)
        x = -0.000125 + 0.9999 * jax.random.normal(jax.random.fold_in(_rk, 1), (2, 256, 256), jnp.float32)
        _lenS = 256 - jax.random.randint(jax.random.fold_in(_rk, 7), (2,), 0, max(1, 256 // 4) + 1, jnp.int32)
        _lenS2 = 512 - jax.random.randint(jax.random.fold_in(_rk, 8), (2,), 0, max(1, 512 // 4) + 1, jnp.int32)
        _ctx_2048P = jax.random.normal(jax.random.fold_in(_rk, 11), (2, 16, 256), jnp.float32)
        _ctx_2048c = jax.random.dirichlet(jax.random.fold_in(_rk, 511), 0.3 * jnp.ones((16,), jnp.float32), (2, 512))
        _ctx_2048t = jnp.einsum('bsk,bkd->bsd', _ctx_2048c, _ctx_2048P)
        _ctx_2048t = _ctx_2048t * jax.lax.rsqrt(jnp.mean(jnp.square(_ctx_2048t)) + 1e-12) * 0.953939
        ctx_2048 = -0.000514642 + 1.00011 * (_ctx_2048t + 0.3 * jax.random.normal(jax.random.fold_in(_rk, 611), (2, 512, 256), jnp.float32))
        _validS = jnp.arange(256)[None, :] < _lenS[:, None]
        _validS2 = jnp.arange(512)[None, :] < _lenS2[:, None]
        _causal = jnp.tril(jnp.ones((256, 256), dtype=bool))
        mask_BxS2_bk0 = jnp.logical_not(jnp.broadcast_to(_validS2[:, :], (2, 512)))
        return (x, ctx_2048, mask_BxS2_bk0)
    x, ctx_2048, mask_BxS2_bk0 = _rec_inputs()

    def _L0_attn_setup():
        import jax, jax.numpy as jnp
        import numpy as np
        B, L, D, H = (4, 512, 256, 16)
        HD = D // H
        EPS = 1e-09

        def phi(x):
            return jax.nn.elu(x) + 1.0
        key = jax.random.key(seed)
        k1, k2, k3 = jax.random.split(key, 3)
        x = jax.random.normal(k1, (B, L, D), dtype=jnp.float32)
        W_qkv = jax.random.normal(k2, (3 * D, D), dtype=jnp.float32) * D ** (-0.5)
        W_out = jax.random.normal(k3, (D, D), dtype=jnp.float32) * D ** (-0.5)
        return {'x': x, 'W_qkv': W_qkv, 'W_out': W_out}
    _L0_attn_all = _L0_attn_setup()
    _L0_attn_in = {k: v for k, v in _L0_attn_all.items() if k in ('W_qkv', 'W_out')}
    del _L0_attn_all

    def _L0_xattn_setup():
        import jax, jax.numpy as jnp
        import numpy as np
        key = jax.random.key(seed)
        k1, k2, k3 = jax.random.split(key, 3)
        B, S, D, M = (8, 256, 256, 128)
        hidden_states = jax.random.normal(k1, (B, S, D), dtype=jnp.float32)
        memory_tokens = jax.random.normal(k2, (B, M, D), dtype=jnp.float32)
        memory_mask = jax.random.randint(k3, (B, M), 0, 2).astype(jnp.bool_)
        return {'hidden_states': hidden_states, 'memory_tokens': memory_tokens, 'memory_mask': memory_mask}
    _L0_xattn_all = _L0_xattn_setup()
    _L0_xattn_in = {k: v for k, v in _L0_xattn_all.items() if k in ()}
    del _L0_xattn_all

    def _L0_ffn_setup():
        import jax, jax.numpy as jnp
        import numpy as np
        TOP_K = 2
        key = jax.random.key(seed)
        ks = jax.random.split(key, 7)
        B, S, H = (2, 256, 256)
        E, A, NS = (8, 64, 2048)
        x = jax.random.normal(ks[0], (B, S, H), jnp.float32)
        gate_w = jax.random.normal(ks[1], (E, H), jnp.float32) * 0.01
        W = jax.random.normal(ks[2], (H, H), jnp.float32) * 0.02
        atoms = jax.random.normal(ks[3], (A, NS), jnp.float32) * 0.02
        expert_atom_weights = jax.random.normal(ks[4], (E, A), jnp.float32) * 0.1
        importance = jax.random.normal(ks[5], (E, NS), jnp.float32) * 0.1
        mask_idx = jax.random.randint(ks[6], (NS,), 0, H * H, jnp.int32)
        return dict(x=x, gate_w=gate_w, W=W, atoms=atoms, expert_atom_weights=expert_atom_weights, importance=importance, mask_idx=mask_idx)
    _L0_ffn_all = _L0_ffn_setup()
    _L0_ffn_in = {k: v for k, v in _L0_ffn_all.items() if k in ('gate_w', 'W', 'atoms', 'expert_atom_weights', 'importance', 'mask_idx')}
    del _L0_ffn_all

    def _L1_attn_setup():
        import jax, jax.numpy as jnp
        import numpy as np
        N_HEADS = 32
        WINDOW = 128

        def _sliding_window_attention(x, Wq, Wk, Wv, Wo, n_heads=N_HEADS, window=WINDOW):
            B, T, D = x.shape
            H, dk = (n_heads, D // n_heads)
            bs = window
            assert T % bs == 0
            nb = T // bs

            def heads(y):
                return y.reshape(B, T, H, dk).transpose(0, 2, 1, 3)
            q = heads(x @ Wq.T)
            k = heads(x @ Wk.T)
            v = heads(x @ Wv.T)
            qb = q.reshape(B, H, nb, bs, dk)
            zpad = jnp.zeros((B, H, bs, dk), dtype=x.dtype)
            kp = jnp.concatenate([zpad, k], axis=2).reshape(B, H, nb + 1, bs, dk)
            vp = jnp.concatenate([zpad, v], axis=2).reshape(B, H, nb + 1, bs, dk)
            kw = jnp.concatenate([kp[:, :, :-1], kp[:, :, 1:]], axis=3)
            vw = jnp.concatenate([vp[:, :, :-1], vp[:, :, 1:]], axis=3)
            scale = 1.0 / np.sqrt(dk).astype(np.float32)
            scores = jnp.einsum('bhnrd,bhncd->bhnrc', qb, kw) * scale
            i = jnp.arange(nb)[:, None, None]
            r = jnp.arange(bs)[None, :, None]
            c = jnp.arange(2 * bs)[None, None, :]
            dist = bs + r - c
            key_global = i * bs - bs + c
            valid = (dist >= 0) & (dist <= window) & (key_global >= 0)
            scores = jnp.where(valid[None, None], scores, jnp.finfo(scores.dtype).min)
            probs = jax.nn.softmax(scores, axis=-1)
            out = jnp.einsum('bhnrc,bhncd->bhnrd', probs, vw)
            out = out.reshape(B, H, T, dk).transpose(0, 2, 1, 3).reshape(B, T, D)
            return out @ Wo.T
        key = jax.random.key(seed)
        ks = jax.random.split(key, 5)
        B, T, D = (2, 512, 256)
        w_std = 0.02
        return {'x': jax.random.normal(ks[0], (B, T, D), dtype=jnp.float32), 'Wq': jax.random.normal(ks[1], (D, D), dtype=jnp.float32) * w_std, 'Wk': jax.random.normal(ks[2], (D, D), dtype=jnp.float32) * w_std, 'Wv': jax.random.normal(ks[3], (D, D), dtype=jnp.float32) * w_std, 'Wo': jax.random.normal(ks[4], (D, D), dtype=jnp.float32) * w_std}
    _L1_attn_all = _L1_attn_setup()
    _L1_attn_in = {k: v for k, v in _L1_attn_all.items() if k in ('Wq', 'Wk', 'Wv', 'Wo')}
    del _L1_attn_all

    def _L1_xattn_setup():
        import jax, jax.numpy as jnp
        import numpy as np
        D_MODEL = 256
        NUM_HEADS = 16
        HEAD_DIM = D_MODEL // NUM_HEADS

        def _fq_sym(x, axis):
            s = jnp.max(jnp.abs(x), axis=axis, keepdims=True) / 127.0
            s = jnp.maximum(s, 1e-08)
            q = jnp.clip(jnp.round(x / s), -127.0, 127.0) * s
            return x + jax.lax.stop_gradient(q - x)

        def _fq_unsigned(x, axis):
            s = jnp.max(x, axis=axis, keepdims=True) / 255.0
            s = jnp.maximum(s, 1e-08)
            q = jnp.clip(jnp.round(x / s), 0.0, 255.0) * s
            return x + jax.lax.stop_gradient(q - x)
        key = jax.random.key(seed)
        ks = jax.random.split(key, 8)
        B, N, M, C = (2, 256, 64, D_MODEL)
        return {'x': jax.random.normal(ks[0], (B, N, C), jnp.float32), 'cond': jax.random.normal(ks[1], (B, M, C), jnp.float32), 'Wq': jax.random.normal(ks[2], (C, C), jnp.float32) * 0.02, 'bq': jnp.zeros((C,), jnp.float32), 'Wkv': jax.random.normal(ks[3], (C, 2 * C), jnp.float32) * 0.02, 'bkv': jnp.zeros((2 * C,), jnp.float32), 'Wp': jax.random.normal(ks[4], (C, C), jnp.float32) * 0.02, 'bp': jnp.zeros((C,), jnp.float32)}
    _L1_xattn_all = _L1_xattn_setup()
    _L1_xattn_in = {k: v for k, v in _L1_xattn_all.items() if k in ('Wq', 'bq', 'Wkv', 'bkv', 'Wp', 'bp')}
    del _L1_xattn_all

    def _L1_ffn_setup():
        import jax, jax.numpy as jnp
        import numpy as np
        TOPK = 6
        CAP = 128
        ROUTE_SCALE = 1.0
        key = jax.random.key(seed)
        k = jax.random.split(key, 6)
        B, T, C = (2, 256, 256)
        E, H, HS = (64, 32, 64)
        std = 0.01
        return {'x': jax.random.normal(k[0], (B, T, C), jnp.float32), 'w_gate': jax.random.normal(k[1], (C, E), jnp.float32) * std, 'w_shared_up': jax.random.normal(k[2], (C, 2 * HS), jnp.float32) * std, 'w_shared_down': jax.random.normal(k[3], (HS, C), jnp.float32) * std, 'w_up': jax.random.normal(k[4], (E, C, 2 * H), jnp.float32) * std, 'w_down': jax.random.normal(k[5], (E, H, C), jnp.float32) * std}
    _L1_ffn_all = _L1_ffn_setup()
    _L1_ffn_in = {k: v for k, v in _L1_ffn_all.items() if k in ('w_gate', 'w_shared_up', 'w_shared_down', 'w_up', 'w_down')}
    del _L1_ffn_all
    return {'x': x, 'ctx_2048': ctx_2048, 'mask_BxS2_bk0': mask_BxS2_bk0, 'L0_attn_W_qkv': _L0_attn_in['W_qkv'], 'L0_attn_W_out': _L0_attn_in['W_out'], 'L0_ffn_gate_w': _L0_ffn_in['gate_w'], 'L0_ffn_W': _L0_ffn_in['W'], 'L0_ffn_atoms': _L0_ffn_in['atoms'], 'L0_ffn_expert_atom_weights': _L0_ffn_in['expert_atom_weights'], 'L0_ffn_importance': _L0_ffn_in['importance'], 'L0_ffn_mask_idx': _L0_ffn_in['mask_idx'], 'L1_attn_Wq': _L1_attn_in['Wq'], 'L1_attn_Wk': _L1_attn_in['Wk'], 'L1_attn_Wv': _L1_attn_in['Wv'], 'L1_attn_Wo': _L1_attn_in['Wo'], 'L1_xattn_Wq': _L1_xattn_in['Wq'], 'L1_xattn_bq': _L1_xattn_in['bq'], 'L1_xattn_Wkv': _L1_xattn_in['Wkv'], 'L1_xattn_bkv': _L1_xattn_in['bkv'], 'L1_xattn_Wp': _L1_xattn_in['Wp'], 'L1_xattn_bp': _L1_xattn_in['bp'], 'L1_ffn_w_gate': _L1_ffn_in['w_gate'], 'L1_ffn_w_shared_up': _L1_ffn_in['w_shared_up'], 'L1_ffn_w_shared_down': _L1_ffn_in['w_shared_down'], 'L1_ffn_w_up': _L1_ffn_in['w_up'], 'L1_ffn_w_down': _L1_ffn_in['w_down']}

def reference(x, ctx_2048, mask_BxS2_bk0, L0_attn_W_qkv, L0_attn_W_out, L0_ffn_gate_w, L0_ffn_W, L0_ffn_atoms, L0_ffn_expert_atom_weights, L0_ffn_importance, L0_ffn_mask_idx, L1_attn_Wq, L1_attn_Wk, L1_attn_Wv, L1_attn_Wo, L1_xattn_Wq, L1_xattn_bq, L1_xattn_Wkv, L1_xattn_bkv, L1_xattn_Wp, L1_xattn_bp, L1_ffn_w_gate, L1_ffn_w_shared_up, L1_ffn_w_shared_down, L1_ffn_w_up, L1_ffn_w_down):
    import jax
    import jax.numpy as jnp

    def _L0_attn_ref(x, W_qkv, W_out):
        import jax, jax.numpy as jnp
        import numpy as np
        B, L, D, H = (4, 512, 256, 16)
        HD = D // H
        EPS = 1e-09

        def phi(x):
            return jax.nn.elu(x) + 1.0
        b, l, d = x.shape
        qkv = x @ W_qkv.T
        q, k, v = jnp.split(qkv, 3, axis=-1)
        q = q.reshape(b, l, H, HD).transpose(0, 2, 1, 3)
        k = k.reshape(b, l, H, HD).transpose(0, 2, 1, 3)
        v = v.reshape(b, l, H, HD).transpose(0, 2, 1, 3)
        q = phi(q)
        k = phi(k)
        kv_cumsum = jnp.cumsum(k * v, axis=2)
        k_cumsum = jnp.cumsum(k, axis=2)
        out = q * kv_cumsum / (q * k_cumsum + EPS)
        out = out.transpose(0, 2, 1, 3).reshape(b, l, d)
        return out @ W_out.T * HD ** (-0.5)

    def _L0_xattn_ref(hidden_states, memory_tokens, memory_mask):
        import jax, jax.numpy as jnp
        import numpy as np
        B, S, D = hidden_states.shape
        scale = 1.0 / jnp.sqrt(jnp.asarray(D, hidden_states.dtype))
        scores = jnp.einsum('bsd,bmd->bsm', hidden_states, memory_tokens) * scale
        neg_inf = jnp.asarray(-1e+30, scores.dtype)
        scores = jnp.where(memory_mask[:, None, :], scores, neg_inf)
        attn = jax.nn.softmax(scores, axis=-1)
        readout = jnp.einsum('bsm,bmd->bsd', attn, memory_tokens)
        valid_b = jnp.any(memory_mask, axis=-1)
        out = jnp.where(valid_b[:, None, None], readout, jnp.zeros_like(readout))
        return out

    def _L0_ffn_ref(x, gate_w, W, atoms, expert_atom_weights, importance, mask_idx):
        import jax, jax.numpy as jnp
        import numpy as np
        TOP_K = 2
        B, S, H = x.shape
        xt = x.reshape(-1, H)
        logits = jnp.clip(xt @ gate_w.T, -50.0, 50.0)
        top_w, top_idx = jax.lax.top_k(logits, TOP_K)
        rw = jax.nn.softmax(top_w, axis=-1)
        deltas = jax.nn.softmax(expert_atom_weights, axis=-1) @ atoms
        weighted = deltas * jax.nn.sigmoid(importance)
        rows = mask_idx // H
        cols = mask_idx % H
        vals = jnp.einsum('tk,tks->ts', rw, weighted[top_idx])
        xg = xt[:, cols]
        contrib = jax.ops.segment_sum((xg * vals).T, rows, num_segments=H)
        out = xt @ W.T + contrib.T
        return out.reshape(B, S, H)

    def _L1_attn_ref(x, Wq, Wk, Wv, Wo):
        import jax, jax.numpy as jnp
        import numpy as np
        N_HEADS = 32
        WINDOW = 128

        def _sliding_window_attention(x, Wq, Wk, Wv, Wo, n_heads=N_HEADS, window=WINDOW):
            B, T, D = x.shape
            H, dk = (n_heads, D // n_heads)
            bs = window
            assert T % bs == 0
            nb = T // bs

            def heads(y):
                return y.reshape(B, T, H, dk).transpose(0, 2, 1, 3)
            q = heads(x @ Wq.T)
            k = heads(x @ Wk.T)
            v = heads(x @ Wv.T)
            qb = q.reshape(B, H, nb, bs, dk)
            zpad = jnp.zeros((B, H, bs, dk), dtype=x.dtype)
            kp = jnp.concatenate([zpad, k], axis=2).reshape(B, H, nb + 1, bs, dk)
            vp = jnp.concatenate([zpad, v], axis=2).reshape(B, H, nb + 1, bs, dk)
            kw = jnp.concatenate([kp[:, :, :-1], kp[:, :, 1:]], axis=3)
            vw = jnp.concatenate([vp[:, :, :-1], vp[:, :, 1:]], axis=3)
            scale = 1.0 / np.sqrt(dk).astype(np.float32)
            scores = jnp.einsum('bhnrd,bhncd->bhnrc', qb, kw) * scale
            i = jnp.arange(nb)[:, None, None]
            r = jnp.arange(bs)[None, :, None]
            c = jnp.arange(2 * bs)[None, None, :]
            dist = bs + r - c
            key_global = i * bs - bs + c
            valid = (dist >= 0) & (dist <= window) & (key_global >= 0)
            scores = jnp.where(valid[None, None], scores, jnp.finfo(scores.dtype).min)
            probs = jax.nn.softmax(scores, axis=-1)
            out = jnp.einsum('bhnrc,bhncd->bhnrd', probs, vw)
            out = out.reshape(B, H, T, dk).transpose(0, 2, 1, 3).reshape(B, T, D)
            return out @ Wo.T
        return _sliding_window_attention(x, Wq, Wk, Wv, Wo)

    def _L1_xattn_ref(x, cond, Wq, bq, Wkv, bkv, Wp, bp):
        import jax, jax.numpy as jnp
        import numpy as np
        D_MODEL = 256
        NUM_HEADS = 16
        HEAD_DIM = D_MODEL // NUM_HEADS

        def _fq_sym(x, axis):
            s = jnp.max(jnp.abs(x), axis=axis, keepdims=True) / 127.0
            s = jnp.maximum(s, 1e-08)
            q = jnp.clip(jnp.round(x / s), -127.0, 127.0) * s
            return x + jax.lax.stop_gradient(q - x)

        def _fq_unsigned(x, axis):
            s = jnp.max(x, axis=axis, keepdims=True) / 255.0
            s = jnp.maximum(s, 1e-08)
            q = jnp.clip(jnp.round(x / s), 0.0, 255.0) * s
            return x + jax.lax.stop_gradient(q - x)
        B, N, C = x.shape
        H, hd = (NUM_HEADS, HEAD_DIM)
        q = (x @ Wq + bq).reshape(1, B * N, H, hd)
        kv = (cond @ Wkv + bkv).reshape(1, -1, 2, H, hd)
        k, v = (kv[:, :, 0], kv[:, :, 1])
        scale = 1.0 / np.sqrt(hd).astype(np.float32)
        q = jnp.transpose(q * scale, (0, 2, 1, 3))
        k = jnp.transpose(k, (0, 2, 1, 3))
        v = jnp.transpose(v, (0, 2, 1, 3))
        q = _fq_sym(q, axis=-1)
        k = _fq_sym(k, axis=-1)
        v = _fq_sym(v, axis=2)
        attn = jnp.einsum('bhqd,bhkd->bhqk', q, k)
        attn = jax.nn.softmax(attn.astype(jnp.float32), axis=-1)
        attn = _fq_unsigned(attn, axis=-1)
        out = jnp.einsum('bhqk,bhkd->bhqd', attn, v)
        out = jnp.transpose(out, (0, 2, 1, 3)).reshape(B, N, C)
        return out @ Wp + bp

    def _L1_ffn_ref(x, w_gate, w_shared_up, w_shared_down, w_up, w_down):
        import jax, jax.numpy as jnp
        import numpy as np
        TOPK = 6
        CAP = 128
        ROUTE_SCALE = 1.0
        B, T, C = x.shape
        E = w_gate.shape[1]
        x_flat = x.reshape(-1, C)
        N = x_flat.shape[0]
        su = x_flat @ w_shared_up
        y_s, g_s = jnp.split(su, 2, axis=-1)
        shared = jax.nn.silu(g_s) * y_s @ w_shared_down
        scores = jax.nn.sigmoid(x_flat @ w_gate)
        _, topk_idx = jax.lax.top_k(scores, TOPK)
        w = jnp.take_along_axis(scores, topk_idx, axis=-1)
        w = w / w.sum(-1, keepdims=True) * ROUTE_SCALE
        flat_e = topk_idx.reshape(-1)
        oh = jax.nn.one_hot(flat_e, E, dtype=jnp.int32)
        pos = jnp.take_along_axis(jnp.cumsum(oh, axis=0), flat_e[:, None], axis=1)[:, 0] - 1
        valid = pos < CAP
        pos_c = jnp.where(valid, pos, CAP - 1)
        token_ids = jnp.repeat(jnp.arange(N), TOPK)
        x_disp = jnp.zeros((E, CAP, C), x.dtype).at[flat_e, pos].set(x_flat[token_ids], mode='drop')
        up = jnp.einsum('ecd,edh->ech', x_disp, w_up)
        g_r, v_r = jnp.split(up, 2, axis=-1)
        h_r = jax.nn.silu(g_r) * v_r
        out_r = jnp.einsum('ech,ehd->ecd', h_r, w_down)
        y_ts = out_r[flat_e, pos_c]
        y_ts = jnp.where(valid[:, None], y_ts, 0.0)
        routed = (y_ts.reshape(N, TOPK, C) * w[:, :, None]).sum(axis=1)
        return (shared + routed).reshape(B, T, C)
    x = _layernorm(x + _L0_attn_ref(x, L0_attn_W_qkv, L0_attn_W_out), axis=-1)
    x = _layernorm(x + _L0_xattn_ref(x, ctx_2048, mask_BxS2_bk0), axis=-1)
    x = _layernorm(x + _L0_ffn_ref(x, L0_ffn_gate_w, L0_ffn_W, L0_ffn_atoms, L0_ffn_expert_atom_weights, L0_ffn_importance, L0_ffn_mask_idx), axis=-1)
    x = _layernorm(x + _L1_attn_ref(x, L1_attn_Wq, L1_attn_Wk, L1_attn_Wv, L1_attn_Wo), axis=-1)
    x = _layernorm(x + _L1_xattn_ref(x, ctx_2048, L1_xattn_Wq, L1_xattn_bq, L1_xattn_Wkv, L1_xattn_bkv, L1_xattn_Wp, L1_xattn_bp), axis=-1)
    x = _layernorm(x + _L1_ffn_ref(x, L1_ffn_w_gate, L1_ffn_w_shared_up, L1_ffn_w_shared_down, L1_ffn_w_up, L1_ffn_w_down), axis=-1)
    return x

_drawn_inputs = setup_inputs


def setup_inputs(seed=0):
    import zlib

    import numpy as np

    out = dict(_drawn_inputs(seed))
    spreads = {'L1_xattn_bq': (0.0, 2.0), 'L1_xattn_bkv': (0.0, 0.274), 'L1_xattn_bp': (0.0, 0.1)}
    factors = {'L0_ffn_gate_w': 8.0,
     'L0_ffn_atoms': 8.0,
     'L0_ffn_expert_atom_weights': 8.0,
     'L0_ffn_importance': 24.077,
     'L1_attn_Wq': 8.0,
     'L1_attn_Wk': 8.0,
     'L1_xattn_Wq': 8.0,
     'L1_ffn_w_gate': 8.0,
     'L1_ffn_w_shared_up': 8.0,
     'L1_ffn_w_shared_down': 8.0,
     'L1_ffn_w_up': 8.0,
     'L1_ffn_w_down': 8.0}
    for name, (base, spread) in spreads.items():
        noise = np.random.default_rng([zlib.crc32(name.encode()), seed]).standard_normal(out[name].shape)
        drawn = base * np.exp(spread * noise) if base else spread * noise
        out[name] = jnp.asarray(drawn.astype(out[name].dtype))
    for name, factor in factors.items():
        out[name] = (out[name] * factor).astype(out[name].dtype)
    return out
```

```python
import math
from contextlib import ExitStack

import numpy as np
import concourse.bass as bass
from concourse import mybir
from concourse.alu_op_type import AluOpType as ALU

ACT = mybir.ActivationFunctionType
AX = mybir.AxisListType
F32 = mybir.dt.float32
BF16 = mybir.dt.bfloat16
I32 = mybir.dt.int32
I16 = mybir.dt.int16
U32 = mybir.dt.uint32
U8 = mybir.dt.uint8

P = 128
B, S, D = 2, 256, 256
N = B * S
TT = N // P
DC = D // P
M = 512
MT = M // P
KT = B * MT
EPS_LN = 1e-5
EPS_LIN = 1e-9
E0, NA, NS = 8, 64, 2048
SJ = NS // P
H1, DH1 = 32, 8
HU = 4
UC = P // (HU * DH1)
HX, DHX = 16, 16
KW = 64
E1, HE, HS, TOPK, CAP = 64, 32, 64, 6, 128
EG = P // HE
NG = E1 // EG
MASKED = -1.0e30
LOWEST = -3.0e38
ROUND = 12582912.0
STAGES = 6
NORM_AT = 9


def build(nc, t, out):
    with ExitStack() as ctx:
        def sb(name, shape, dt=F32):
            return ctx.enter_context(nc.sbuf_tensor(name, shape, dt))

        sems = {}

        def sem(name):
            if name not in sems:
                sems[name] = ctx.enter_context(nc.semaphore(name))
            return sems[name]

        ps = ctx.enter_context(nc.psum_tensor("ps", [P, 8 * 512], F32))

        def bank(k, n=1):
            return ps[:, 512 * k:512 * (k + n)]

        x_tok = [sb("x_even", [P, TT, D]), sb("x_odd", [P, TT, D])]
        xT = [sb("xT_even", [P, DC, N]), sb("xT_odd", [P, DC, N])]
        res = sb("res", [P, TT, D])
        stats = sb("stats", [P, TT, 6])
        meanvar = sb("meanvar", [P, TT, 2])
        var_eps = sb("var_eps", [P, TT])
        rstd = sb("rstd", [P, TT])
        minus_half = sb("minus_half", [P, TT])
        w_qkv0 = sb("w_qkv0", [P, DC, 3 * D])
        w_out0 = sb("w_out0", [P, DC, D])
        ctxT = sb("ctxT", [P, DC, B * M])
        ctx_tok = sb("ctx_tok", [P, KT, D])
        mask_u8 = sb("mask_u8", [P, B, M], U8)
        mask_add = sb("mask_add", [P, B, M])
        valid = sb("valid", [P, B])
        w_ffn0 = sb("w_ffn0", [P, DC, D])
        w_router0 = sb("w_router0", [P, DC, E0])
        wq1 = sb("wq1", [P, DC, D])
        wk1 = sb("wk1", [P, DC, D])
        wv1 = sb("wv1", [P, DC, D])
        wo1 = sb("wo1", [P, DC, D])
        wqx = sb("wqx", [P, DC, D])
        wkvx = sb("wkvx", [P, DC, 2 * D])
        wpx = sb("wpx", [P, DC, D])
        bqx = sb("bqx", [P, D])
        bkx = sb("bkx", [P, D])
        bpx = sb("bpx", [P, D])
        bvx = sb("bvx", [P, DC])
        w_router1 = sb("w_router1", [P, DC, E1])
        w_su = sb("w_su", [P, DC, 2 * HS])
        w_sd = sb("w_sd", [HS, D])
        ident = sb("ident", [P, P])
        ident_b = sb("ident_b", [P, P], BF16)
        tri_b = sb("tri_b", [P, P], BF16)
        ones_b = sb("ones_b", [P, P], BF16)
        keep_state = sb("keep_state", [P, N])
        iota_row = sb("iota_row", [P, D])
        part_id = sb("part_id", [P, DC])
        win_own = sb("win_own", [P, HU, P], BF16)
        win_prev = sb("win_prev", [P, HU, P], BF16)
        head_of = sb("head_of", [P, UC, HU])
        head_sel = sb("head_sel", [P, HU])
        head_rows = sb("head_rows", [H1, D])
        small = sb("small", [P, 2048])

        area = {"a": sb("area_a", [P, 12288]), "b": sb("area_b", [P, 14336])}
        taken = {"small": 0}
        area["small"] = small

        def carve(where, at, shape, dt=F32, rows=P):
            words = math.prod(shape) * mybir.dt.size(dt) // 4
            assert at + words <= area[where].shape[1], (where, at, shape)
            v = area[where][0:rows, at:at + words]
            if dt != F32:
                v = v.bitcast(dt)
            if len(shape) == 2:
                v = v.rearrange("p (a b) -> p a b", a=shape[0])
            if len(shape) == 3:
                v = v.rearrange("p (a b c) -> p a b c", a=shape[0], b=shape[1])
            return v

        def tiny(shape, dt=F32):
            v = carve("small", taken["small"], shape, dt)
            taken["small"] += (math.prod(shape) * mybir.dt.size(dt) + 3) // 4
            return v

        exp_kq = carve("a", 0, [2, N])
        relu_kq = carve("a", 2 * N, [2, N])
        phi_k = carve("a", 4 * N, [N])
        kv = carve("a", 5 * N, [N])
        kv_sum = carve("a", 6 * N, [N])
        k_sum = carve("a", 7 * N, [N])
        phi_q = carve("a", 8 * N, [N])
        den = carve("a", 9 * N, [N])
        num = carve("a", 10 * N, [N])
        lin = carve("a", 11 * N, [DC, N])
        s2 = carve("a", 13 * N, [TT, M])
        p2 = carve("a", 0, [TT, M])
        pT2 = carve("a", 4 * M, [TT, MT, P])
        mx2, nb2, z2, rz2 = tiny([TT]), tiny([TT]), tiny([TT]), tiny([TT])
        atoms = carve("b", 0, [NS], rows=NA)
        idx_row = carve("b", NS, [NS], I32)
        col_hot = carve("b", 2 * NS, [DC, NS])
        row_hot = carve("b", 4 * NS, [SJ, D])
        weighted = carve("b", 4 * NS + SJ * D, [NS], rows=E0)
        idx_col = sb("idx_col", [P, SJ], I32)
        row_id = tiny([SJ])
        mix = tiny([NA])[0:E0]
        mix_z = tiny([3])[0:E0]
        mixT = tiny([E0])[0:NA]
        vals = carve("a", 0, [2, N])
        prod = carve("a", 2 * N, [2, N])
        logit0, top0 = tiny([TT, E0]), tiny([TT, 8])
        idx0, idx0f = tiny([TT, 8], U32), tiny([TT, 8])
        gap0, exp0, w20, w10 = tiny([TT]), tiny([TT]), tiny([TT]), tiny([TT])
        hot0, hot1, gate0 = tiny([TT, E0]), tiny([TT, E0]), tiny([TT, E0])
        gate0T = carve("a", 4 * N, [N], rows=E0)
        qT1 = carve("a", 0, [DC, N])
        kT1 = carve("a", 2 * N, [DC, HU, N])
        v1 = carve("a", 10 * N, [TT * H1 // HU * HU, HU * DH1])
        p1 = carve("a", 18 * N, [2, HU * 2 * P])
        pT1 = carve("b", 8 * N, [2, HU * 2 * P])
        attT1 = carve("b", 12 * N, [2, DC, P])
        rzT1 = carve("b", 13 * N, [P], rows=H1)
        nmx1, z1, rz1 = tiny([2, HU]), tiny([TT, H1]), tiny([TT, H1])
        kstack = carve("b", 0, [2, HX * KW], BF16)
        kTx = carve("b", HX * KW, [HX // 2, B * M], BF16)
        base = HX * KW + HX // 2 * B * M // 2
        qTx = carve("b", base, [HX // 2, N], BF16)
        qstack = carve("b", base + HX // 4 * N, [TT, HX * KW], BF16)
        base += HX // 4 * N + TT * HX * KW // 2
        ivT = carve("b", base, [DC, B * M], BF16)
        iv = carve("b", base + B * M, [KT, D], BF16)
        base += B * M + KT * D // 2
        px = carve("b", base, [2, B * M], I16)
        pTx = carve("b", base + B * M, [2, KT * P], BF16)
        base += 2 * B * M
        kx = carve("a", 0, [2, D])
        kr = carve("a", 2 * D, [2, D])
        ks = carve("a", 4 * D, [2, D])
        kres = carve("a", 6 * D, [2, D])
        vTx = carve("a", 8 * D, [DC, B * M])
        vr = carve("a", 8 * D + 2 * B * M, [B * M])
        qx = carve("a", 8 * D + 3 * B * M, [TT, D])
        attx = sb("attx", [P, 2, D])
        attTx = sb("attTx", [P, 2, DC, P])
        kam, ksc, krs = tiny([KT, HX]), tiny([KT, HX]), tiny([KT, HX])
        vam, vsc, vrs = tiny([DC]), tiny([DC]), tiny([DC])
        qam, qsc, qrs = tiny([TT, HX]), tiny([TT, HX]), tiny([TT, HX])
        nqs = tiny([TT, HX])
        mxx, nbx = tiny([TT * HX]), tiny([TT * HX])
        zx, rzx = tiny([TT, HX]), tiny([TT, HX])
        w_up = carve("a", 0, [DC, 2, E1 * HE])
        w_down = carve("a", DC * E1 * 2 * HE, [NG, D])
        spread = sb("spread", [E1, NG * P])
        gate1T = carve("b", 0, [N], rows=E1)
        silu = carve("b", N, [2, N])
        gated = carve("b", 3 * N, [2, N])
        hidden = carve("b", 5 * N, [2, N])
        shared = carve("b", 7 * N, [N], rows=HS)
        score1 = carve("b", 8 * N, [TT, E1])
        hot = carve("b", 8 * N + TT * E1, [TOPK, E1])
        picked = carve("b", 8 * N + TT * E1 + TOPK * E1, [TT, E1])
        picked_b = carve("b", 8 * N + 2 * TT * E1 + TOPK * E1, [TT, E1], BF16)
        gate1 = carve("b", 8 * N + 3 * TT * E1 + TOPK * E1, [TT, E1])
        top1, idx1, idx1f = tiny([TT, 8]), tiny([TT, 8], U32), tiny([TT, 8])
        sum1, rsum1 = tiny([TT]), tiny([TT])

        def proj(i):
            return bank(6 + i // 2)[:, D * (i % 2):D * (i % 2) + D]

        def pTx_ready(eng, u):
            if u % 3 < 2:
                eng.wait_ge(sem("pTx_dve"), u // 3 * 2 + u % 3 + 1)
            else:
                eng.wait_ge(sem("pTx_act"), u // 3 + 1)

        def unit_s1(u):
            return bank(2 * (u % 2), 2).rearrange("p (b j k) -> p b j k", b=2, j=HU)

        def unit_p1(u):
            return p1[:, u % 2].rearrange("p (j b k) -> p j b k", b=2, j=HU)

        def unit_pT1(u):
            return pT1[:, u % 2].rearrange("p (j b q) -> p j b q", b=2, j=HU)

        block = ctx.enter_context(nc.Block())

        def linker(eng, name):
            count = [0]

            def link(ins):
                count[0] += 1
                ins.then_inc(sem(name), 1)
                eng.wait_ge(sem(name), count[0])
            return link

        @block.sync
        def _(sp):
            def load(name, dst, src):
                sp.dma_start(dst, src).then_inc(sem("in_" + name), 16)

            two = "(c p) n -> p c n"
            load("xT", xT[0][:], t["xT"].rearrange(two, p=P))
            load("w_qkv0", w_qkv0[:], t["w_qkv0"].rearrange(two, p=P))
            load("x", x_tok[0][:], t["x"].rearrange("(i p) d -> p i d", p=P))
            load("w_out0", w_out0[:], t["w_out0"].rearrange(two, p=P))
            load("ctxT", ctxT[:], t["ctxT"].rearrange(two, p=P))
            load("ctx", ctx_tok[:], t["ctx"].rearrange("(k p) d -> p k d", p=P))
            load("w_ffn0", w_ffn0[:], t["w_ffn0"].rearrange(two, p=P))
            load("wq1", wq1[:], t["wq1"].rearrange(two, p=P))
            load("wk1", wk1[:], t["wk1"].rearrange(two, p=P))
            load("wv1", wv1[:], t["wv1"].rearrange(two, p=P))
            load("wo1", wo1[:], t["wo1"].rearrange(two, p=P))
            load("wqx", wqx[:], t["wqx"].rearrange(two, p=P))
            load("wkvx", wkvx[:], t["wkvx"].rearrange(two, p=P))
            load("wpx", wpx[:], t["wpx"].rearrange(two, p=P))
            load("bqx", bqx[:], t["bqx"])
            load("bkx", bkx[:], t["bkx"])
            load("bpx", bpx[:], t["bpx"])
            load("bvx", bvx[:], t["bvx"])
            load("w_router1", w_router1[:], t["w_router1"].rearrange(two, p=P))
            load("w_su", w_su[:], t["w_su"].rearrange(two, p=P))
            load("w_sd", w_sd[:], t["w_sd"])
            if STAGES >= 6:
                sp.wait_ge(sem("iv_ready"), DC)
                sp.wait_ge(sem("kstack_ready"), KT)
                sp.wait_ge(sem("qstack_ready"), 1)
                load("w_up", w_up.rearrange("p c k h -> p (c k h)"), t["w_up"])
                load("w_down", w_down, t["w_down"].rearrange("(g p) d -> p g d", p=P))
            for i in range(TT):
                sp.wait_ge(sem(f"x_ready{STAGES}"), i + 1)
                sp.dma_start(out[i * P:(i + 1) * P, :], x_tok[STAGES % 2][:, i, :]).then_inc(sem("out_done"), 16)
            sp.wait_ge(sem("out_done"), 16 * TT)

        @block.gpsimd
        def _(pool):
            link = linker(pool, "pool_chain")

            def load(name, dst, src):
                pool.dma_start(dst, src).then_inc(sem("in_" + name), 16)

            load("mask", mask_u8[:], t["mask"])
            load("idx_row", idx_row, t["idx_row"])
            load("idx_col", idx_col[:], t["idx"].rearrange("(p j) -> p j", j=SJ))
            load("mix", mix, t["mix"])
            load("imp", weighted, t["imp"])
            load("atoms", atoms, t["atoms"])
            load("w_router0", w_router0[:], t["w_router0"].rearrange("(c p) n -> p c n", p=P))

            pool.memset(minus_half[:], -0.5)
            pool.memset(keep_state[:], 1.0)
            pool.memset(ident[:], 0.0)
            pool.memset(ident_b[:], 0.0)
            pool.memset(tri_b[:], 1.0)
            pool.memset(ones_b[:], 1.0)
            pool.memset(win_own[:], 0.0)
            pool.memset(win_prev[:], 0.0)
            pool.memset(head_of[:], 1.0)
            pool.memset(head_rows[:], 1.0)
            link(pool.memset(spread[:], 1.0))
            link(pool.memset(keep_state[:, S:S + 1], 0.0))

            def select(buf, pattern, base, mult, op, fill):
                return pool.affine_select(out=buf, in_=buf, compare_op=op, fill=fill, base=base,
                                          pattern=pattern, channel_multiplier=mult)

            link(select(ident[:], [[-1, P]], 0, 1, ALU.not_equal, 1.0))
            link(select(ident_b[:], [[-1, P]], 0, 1, ALU.not_equal, 1.0))
            pool.iota(iota_row[:], [[1, D]], base=0, channel_multiplier=0, allow_small_or_imprecise_dtypes=True)
            link(pool.iota(part_id[:], [[P, DC]], base=0, channel_multiplier=1, allow_small_or_imprecise_dtypes=True))
            link(select(tri_b[:], [[1, P]], 0, -1, ALU.is_ge, 0.0))
            link(select(win_own[:], [[0, HU], [-1, P]], 0, 1, ALU.is_ge, MASKED))
            link(select(win_prev[:], [[0, HU], [1, P]], 0, -1, ALU.is_ge, MASKED))
            span = [[-HU * DH1, UC], [-DH1, HU]]
            link(select(head_of[:], span, 0, 1, ALU.is_ge, 0.0))
            link(select(head_of[:], [[HU * DH1, UC], [DH1, HU]], DH1 - 1, -1, ALU.is_ge, 0.0))
            link(select(head_rows[:], [[1, D]], 0, -DH1, ALU.is_ge, 0.0))
            link(select(head_rows[:], [[-1, D]], DH1 - 1, DH1, ALU.is_ge, 0.0))
            link(select(spread[:], [[1, NG * P]], 0, -HE, ALU.is_ge, 0.0))
            link(select(spread[:], [[-1, NG * P]], HE - 1, HE, ALU.is_ge, 0.0))
            pool.sem_inc(sem("const_ready"), 1)

            def linear_numerator(c):
                pool.wait_ge(sem("sums_ready"), c + 1)
                if c:
                    pool.wait_ge(sem("lin_ready"), c)
                pool.tensor_tensor(out=num, in0=phi_q, in1=kv_sum, op=ALU.mult).then_inc(sem("num_ready"), 1)

            def inverse_deviation(n, i):
                pool.wait_ge(sem(f"var_ready{n}"), i + 1)
                link(pool.tensor_scalar(var_eps[:, i:i + 1], meanvar[:, i, 1:2], EPS_LN, None, ALU.add))
                pool.tensor_tensor(out=rstd[:, i:i + 1], in0=var_eps[:, i:i + 1], in1=minus_half[:, i:i + 1],
                                   op=ALU.pow).then_inc(sem(f"rstd_ready{n}"), 1)

            for c in range(DC):
                linear_numerator(c)
            for n in range(1, STAGES + 1):
                if n == 5:
                    for u in range(TT * HX):
                        pool.wait_ge(sem("maxx_ready"), u + 1)
                        pool.tensor_scalar(nbx[:, u:u + 1], mxx[:, u:u + 1], nqs[:, u // HX, u % HX:u % HX + 1],
                                           math.log(255.0), ALU.mult, ALU.add).then_inc(sem("biasx_ready"), 1)
                        if u > HX and u % HX == NORM_AT - 2:
                            inverse_deviation(5, u // HX - 1)
                for i in range(TT - 1 if n == 5 else 0, TT):
                    inverse_deviation(n, i)
                if n == 3 and STAGES > 3:
                    pool.wait_ge(sem("x_ready3"), TT)
                    pool.memset(v1, 0.0).then_inc(sem("v1_cleared"), 1)

        @block.scalar
        def _(act):
            link = linker(act, "act_chain")

            act.wait_ge(sem("in_imp"), 16)
            act.activation(weighted, weighted, ACT.Sigmoid).then_inc(sem("imp_ready"), 1)
            act.wait_ge(sem("mixmax_ready"), 1)
            act.activation(mix, mix, ACT.Exp, bias=mix_z[:, 0:1], accum_out=mix_z[:, 1:2]).then_inc(sem("mixexp_ready"), 1)
            act.wait_ge(sem("mixT_ps"), 1)
            act.activation(mixT, bank(7)[0:NA, 0:E0], ACT.Copy).then_inc(sem("mixT_ready"), 1)

            for c in range(DC):
                act.wait_ge(sem("qkv_ps"), c + 1)
                if c:
                    act.wait_ge(sem("phi_ready"), c)
                for m, b in ((0, 3 * c), (1, 3 * c + 2)):
                    act.activation(exp_kq[:, m, :], bank(b), ACT.Exp)
                    act.activation(relu_kq[:, m, :], bank(b), ACT.Relu).then_inc(sem("exp_ready"), 1)

            def to_xT(n):
                for i in range(TT):
                    act.wait_ge(sem(f"xT_ps{n}"), i + 1)
                    slot = bank(4 + i % 2)[:, 0:D].rearrange("p (c t) -> p c t", c=DC)
                    act.activation(xT[n % 2][:, :, i * P:(i + 1) * P], slot, ACT.Copy).then_inc(sem(f"xT_ready{n}"), 1)

            def stage2():
                for i in range(TT):
                    act.wait_ge(sem("nb2_ready"), i + 1)
                    act.activation(p2[:, i, :], s2[:, i, :], ACT.Exp, bias=nb2[:, i:i + 1], scale=1.0 / 16,
                                   accum_out=z2[:, i:i + 1]).then_inc(sem("p2_ready"), 1)
                    if i:
                        evac2(i - 1)
                evac2(TT - 1)

            def evac2(i):
                act.wait_ge(sem("pT2_ps"), i + 1)
                act.activation(pT2[:, i].rearrange("p k q -> p (k q)"), bank(4 + i % 2), ACT.Copy).then_inc(sem("pT2_ready"), 1)

            def stage3():
                act.wait_ge(sem("gap0_ready"), 1)
                act.activation(exp0, gap0, ACT.Exp).then_inc(sem("exp0_ready"), 1)
                act.wait_ge(sem("gate0T_ps"), 1)
                act.activation(gate0T, bank(0)[0:E0, :], ACT.Copy).then_inc(sem("gate0T_ready"), 1)
                for j in range(SJ):
                    act.wait_ge(sem("vals_ps"), j + 1)
                    if j >= 2:
                        act.wait_ge(sem("prod_ready"), j - 1)
                    act.activation(vals[:, j % 2, :], bank(3 + j % 2 * 2), ACT.Copy).then_inc(sem("vals_ready"), 1)

            def stage4():
                for c in range(DC):
                    act.wait_ge(sem("qk1_ps"), 2 * c + 1)
                    act.activation(qT1[:, c, :], bank(2 * c), ACT.Copy, scale=DH1 ** -0.5).then_inc(sem("qT1_ready"), 1)
                    act.wait_ge(sem("qk1_ps"), 2 * c + 2)
                    act.wait_ge(sem("head_sel_ready"), 1)
                    for j in range(HU):
                        a = act.activation(kT1[:, c, j, :], bank(2 * c + 1), ACT.Copy, scale=head_sel[:, j:j + 1])
                    a.then_inc(sem("kT1_ready"), 1)
                for u in range(TT * H1 // HU):
                    i, g = divmod(u, H1 // HU)
                    nk = 1 + i % 2
                    act.wait_ge(sem("max1_ready"), u + 1)
                    if u >= 2:
                        act.wait_ge(sem("pT1_ps"), u - 1)
                    for j in range(HU):
                        a = act.activation(unit_p1(u)[:, j, 0:nk, :], unit_s1(u)[:, 0:nk, j, :], ACT.Exp,
                                           bias=nmx1[:, u % 2, j:j + 1],
                                           accum_out=z1[:, i, HU * g + j:HU * g + j + 1])
                    a.then_inc(sem("p1_ready"), 1)

            def stage5():
                for c in range(DC):
                    act.wait_ge(sem("vTx_ps"), c + 1)
                    act.wait_ge(sem("in_bvx"), 16)
                    act.activation(vTx[:, c, :], bank(2 + 2 * c, 2), ACT.Identity, bias=bvx[:, c:c + 1]).then_inc(sem("vTx_ready"), 1)
                for c in range(HX // 2):
                    act.wait_ge(sem("qTx_ps"), c + 1)
                    act.activation(qTx[:, c, :], bank(6 + c % 2)[:, 0:N // 2].bitcast(BF16), ACT.Copy).then_inc(sem("qTx_ready"), 1)
                for u in range(TT * HX):
                    i, h = divmod(u, HX)
                    act.wait_ge(sem("biasx_ready"), u + 1)
                    if u >= 2:
                        act.wait_ge(sem("pTx_ps"), u - 1)
                    act.activation(px[:, u % 2, :], bank(2 * (u % 2), 2), ACT.Exp, bias=nbx[:, u:u + 1],
                                   scale=qsc[:, i, h:h + 1], accum_out=zx[:, i, h:h + 1]).then_inc(sem("px_ready"), 1)
                    if u % 3 == 0 and u:
                        evac_px(u - 1)
                    if h == 4 and i:
                        evac_attx(i - 1)
                evac_attx(TT - 1)

            def evac_px(u):
                act.wait_ge(sem("pTx_ps"), u + 1)
                if u >= 2:
                    act.wait_ge(sem("ox_ps"), u - 1)
                act.activation(pTx[:, u % 2, :], bank(4 + u % 2).bitcast(I16), ACT.Copy).then_inc(sem("pTx_act"), 1)

            def evac_attx(i):
                act.wait_ge(sem("attTx_ps"), i + 1)
                for c in range(DC):
                    a = act.activation(attTx[:, i % 2, c, :], bank(6 + i % 2)[:, D + c * P:D + (c + 1) * P], ACT.Copy,
                                       scale=vsc[:, c:c + 1])
                a.then_inc(sem("attTx_ready"), 1)

            def stage6():
                act.wait_ge(sem("score1_ps"), 1)
                act.activation(score1.rearrange("p i e -> p (i e)"), bank(0)[:, 0:TT * E1], ACT.Sigmoid).then_inc(sem("score1_ready"), 1)
                act.wait_ge(sem("gate1T_ps"), 1)
                act.activation(gate1T, bank(5)[0:E1, :], ACT.Copy).then_inc(sem("gate1T_ready"), 1)
                for g in range(NG + 1):
                    act.wait_ge(sem("up_ps"), g + 1)
                    if g >= 2:
                        act.wait_ge(sem("hidden_ready"), g - 1)
                    rows = P if g < NG else HS
                    act.activation(silu[0:rows, g % 2, :], bank(g % 2)[0:rows, :], ACT.Silu).then_inc(sem("silu_ready"), 1)

            unit = [None, None, stage2, stage3, stage4, stage5, stage6]
            for n in range(1, STAGES + 1):
                if n > 1:
                    unit[n]()
                if n < STAGES:
                    to_xT(n)

        @block.tensor
        def _(pe):
            def dense(dst, lhsT, rhs, start=True, stop=True, **kw):
                for c in range(DC):
                    mm = pe.matmul(dst, lhsT(c), rhs(c), start=start and c == 0, stop=stop and c == DC - 1, **kw)
                return mm

            pe.wait_ge(sem("const_ready"), 1)
            pe.wait_ge(sem("mix_ready"), 1)
            pe.transpose(bank(7)[0:NA, 0:E0], mix, ident[0:E0, 0:E0]).then_inc(sem("mixT_ps"), 1)
            pe.wait_ge(sem("mixT_ready"), 1)
            pe.wait_ge(sem("in_atoms"), 16)
            for k in range(NS // 512):
                if k >= 2:
                    pe.wait_ge(sem("weighted_ready"), k - 1)
                pe.matmul(bank(6 + k % 2)[0:E0, :], mixT, atoms[:, 512 * k:512 * (k + 1)],
                          start=True, stop=True).then_inc(sem("delta_ps"), 1)

            pe.wait_ge(sem("in_xT"), 16)
            pe.wait_ge(sem("in_w_qkv0"), 16)
            for c in range(DC):
                for k, m in enumerate((1, 2, 0)):
                    mm = dense(bank(3 * c + k), lambda d: w_qkv0[:, d, D * m + P * c:D * m + P * (c + 1)],
                               lambda d: xT[0][:, d, :])
                mm.then_inc(sem("qkv_ps"), 1)
            pe.wait_ge(sem("lin_ready"), DC)
            pe.wait_ge(sem("in_w_out0"), 16)
            pe.wait_ge(sem("weighted_ready"), NS // 512)
            for i in range(TT):
                dense(proj(i), lambda c: lin[:, c, i * P:(i + 1) * P], lambda c: w_out0[:, c, :]).then_inc(sem("proj1"), 1)

            def transpose_x(n):
                for i in range(TT):
                    pe.wait_ge(sem(f"x_ready{n}"), i + 1)
                    if i >= 2:
                        pe.wait_ge(sem(f"xT_ready{n}"), i - 1)
                    for c in range(DC):
                        mm = pe.transpose(bank(4 + i % 2)[:, c * P:(c + 1) * P], x_tok[n % 2][:, i, c * P:(c + 1) * P], ident[:])
                    mm.then_inc(sem(f"xT_ps{n}"), 1)

            def tile_of(n, i):
                return lambda c: xT[n % 2][:, c, i * P:(i + 1) * P]

            def stage2():
                pe.wait_ge(sem("in_ctxT"), 16)
                for i in range(TT):
                    b = i // (TT // B)
                    pe.wait_ge(sem("xT_ready1"), i + 1)
                    dense(bank(i), tile_of(1, i), lambda c: ctxT[:, c, b * M:(b + 1) * M]).then_inc(sem("s2_ps"), 1)
                pe.wait_ge(sem("in_ctx"), 16)
                pe.wait_ge(sem("xT_ready1"), TT)
                for i in range(TT + 1):
                    if i < TT:
                        pe.wait_ge(sem("p2_ready"), i + 1)
                        if i >= 2:
                            pe.wait_ge(sem("pT2_ready"), i - 1)
                        for k in range(MT):
                            mm = pe.transpose(bank(4 + i % 2)[:, k * P:(k + 1) * P], p2[:, i, k * P:(k + 1) * P], ident[:])
                        mm.then_inc(sem("pT2_ps"), 1)
                    if i:
                        b = (i - 1) // (TT // B)
                        pe.wait_ge(sem("pT2_ready"), i)
                        for k in range(MT):
                            mm = pe.matmul(proj(i - 1), pT2[:, i - 1, k, :], ctx_tok[:, b * MT + k, :],
                                           start=k == 0, stop=k == MT - 1)
                        mm.then_inc(sem("proj2"), 1)

            def stage3():
                pe.wait_ge(sem("in_w_router0"), 16)
                pe.wait_ge(sem("in_w_ffn0"), 16)
                for i in range(TT):
                    pe.wait_ge(sem("xT_ready2"), i + 1)
                    mm = dense(bank(0)[:, E0 * i:E0 * (i + 1)], tile_of(2, i), lambda c: w_router0[:, c, :])
                mm.then_inc(sem("logit0_ps"), 1)
                for i in range(TT):
                    dense(proj(i), tile_of(2, i), lambda c: w_ffn0[:, c, :], start=i % 2 == 0, stop=False,
                          skip_group_check=True)
                pe.wait_ge(sem("hot_ready"), 1)

                def gather(j):
                    if j >= 2:
                        pe.wait_ge(sem("prod_ready"), j - 1)
                    dense(bank(2 if j % 2 else 1), lambda c: col_hot[:, c, j:NS:SJ], lambda c: xT[0][:, c, :])

                def values(j):
                    if j >= 2:
                        pe.wait_ge(sem("vals_ready"), j - 1)
                    pe.matmul(bank(3 + j % 2 * 2), weighted[:, j:NS:SJ], gate0T, start=True, stop=True).then_inc(sem("vals_ps"), 1)

                gather(0)
                gather(1)
                pe.wait_ge(sem("gate0_ready"), 1)
                for i in range(TT):
                    mm = pe.transpose(bank(0)[0:E0, i * P:(i + 1) * P], gate0[:, i, :], ident[:])
                mm.then_inc(sem("gate0T_ps"), 1)
                pe.wait_ge(sem("gate0T_ready"), 1)
                values(0)
                values(1)
                for j in range(SJ):
                    pe.wait_ge(sem("prod_ready"), j + 1)
                    for i in range(TT):
                        mm = pe.matmul(proj(i), prod[:, j % 2, i * P:(i + 1) * P], row_hot[:, j, :],
                                       start=False, stop=j == SJ - 1, skip_group_check=True)
                        if j == SJ - 1:
                            mm.then_inc(sem("proj3"), 1)
                    if j < SJ - 1:
                        mm.then_inc(sem("prod_used"), 1)
                    if j + 2 < SJ:
                        gather(j + 2)
                        values(j + 2)

            def stage4():
                for w in ("wq1", "wk1", "wv1"):
                    pe.wait_ge(sem("in_" + w), 16)
                pe.wait_ge(sem("xT_ready3"), TT)
                for c in range(DC):
                    for k, w in ((0, wq1), (1, wk1)):
                        dense(bank(2 * c + k), lambda d: w[:, d, c * P:(c + 1) * P], lambda d: xT[1][:, d, :]).then_inc(sem("qk1_ps"), 1)
                for i in range(TT):
                    dense(bank(4 + i // 2)[:, D * (i % 2):D * (i % 2) + D], tile_of(3, i), lambda d: wv1[:, d, :]).then_inc(sem("v1_ps"), 1)
                units = TT * H1 // HU

                def scores(u):
                    i, g8 = divmod(u, H1 // HU)
                    c, g = divmod(g8, UC)
                    rows = slice(g * HU * DH1, (g + 1) * HU * DH1)
                    if u >= 2:
                        pe.wait_ge(sem("p1_ready"), u - 1)
                    nk = 1 + i % 2
                    for b in range(nk):
                        kt = i - nk + 1 + b
                        dst = unit_s1(u)[:, b]
                        pe.matmul(dst, qT1[rows, c, i * P:(i + 1) * P], kT1[rows, c, :, kt * P:(kt + 1) * P], start=True, stop=False)
                        mm = pe.matmul(dst, ident_b[:], (win_own if kt == i else win_prev)[:], start=False, stop=True)
                    mm.then_inc(sem("s1_ps"), 1)

                def turn(u):
                    i, g8 = divmod(u, H1 // HU)
                    nk = 1 + i % 2
                    pe.wait_ge(sem("p1_ready"), u + 1)
                    if u:
                        pe.wait_ge(sem("pT1_ready"), u)
                    for j in range(HU):
                        for b in range(nk):
                            at = (2 * j + b) * P
                            mm = pe.transpose(bank(4, 2)[:, at:at + P], unit_p1(u)[:, j, b, :], ident[:])
                    mm.then_inc(sem("pT1_ps"), 1)

                def apply(u):
                    i, g8 = divmod(u, H1 // HU)
                    nk = 1 + i % 2
                    pe.wait_ge(sem("pT1_ready"), u + 1)
                    if u % UC == 0 and u:
                        pe.wait_ge(sem("sums1_out"), u // UC)
                    dst = bank(6)[0:HU * DH1, u % UC * P:(u % UC + 1) * P]
                    for j in range(HU):
                        for b in range(nk):
                            kt = i - nk + 1 + b
                            mm = pe.matmul(dst, v1[:, (kt * (H1 // HU) + g8) * HU + j, :], unit_pT1(u)[:, j, b, :],
                                           start=j == 0 and b == 0, stop=j == HU - 1 and b == nk - 1)
                    mm.then_inc(sem("o1_ps"), 1)

                def turn_z(i):
                    pe.wait_ge(sem("rz1_ready"), i + 1)
                    if i:
                        pe.wait_ge(sem("res4_ready"), i)
                    pe.transpose(bank(7)[0:H1, 0:P], rz1[:, i, :], ident[:]).then_inc(sem("rzT1_ps"), 1)

                def spread_z(i):
                    pe.wait_ge(sem("rzT1_ready"), i + 1)
                    for c in range(DC):
                        mm = pe.matmul(bank(7)[:, (1 + c) * P:(2 + c) * P], head_rows[:, c * P:(c + 1) * P], rzT1,
                                       start=True, stop=True)
                    mm.then_inc(sem("zf1_ps"), 1)

                def project(i):
                    pe.wait_ge(sem("att1_ready"), i + 1)
                    dense(bank(7)[:, 0:D], lambda c: attT1[:, i % 2, c, :], lambda c: wo1[:, c, :]).then_inc(sem("proj4"), 1)

                pe.wait_ge(sem("in_wo1"), 16)
                pe.wait_ge(sem("qT1_ready"), DC)
                pe.wait_ge(sem("kT1_ready"), DC)
                pe.wait_ge(sem("v1_ready"), TT // 2)
                per = H1 // HU
                scores(0)
                for u in range(units + 1):
                    if u + 1 < units:
                        scores(u + 1)
                    if u < units:
                        turn(u)
                    if u % per == 1 and u > per:
                        turn_z(u // per - 1)
                    if u % per == 2 and u > per:
                        spread_z(u // per - 1)
                    if u % per == 4 and u > per:
                        project(u // per - 1)
                    if u:
                        apply(u - 1)
                turn_z(TT - 1)
                spread_z(TT - 1)
                project(TT - 1)

            def turn_keys(k):
                pe.wait_ge(sem("kstack_ready"), k + 1)
                if k >= 2:
                    pe.wait_ge(sem("kTx_ready"), k - 1)
                for c in range(HX // 2):
                    mm = pe.transpose(bank(6 + k % 2).bitcast(BF16)[:, c * P:(c + 1) * P],
                                      kstack[:, k % 2, c * P:(c + 1) * P], ident_b[:])
                mm.then_inc(sem("kTx_ps"), 1)

            def stage5():
                pe.wait_ge(sem("in_wkvx"), 16)
                for k in range(KT):
                    if k >= 2:
                        pe.wait_ge(sem("kx_ready"), k - 1)
                    dense(bank(k % 2)[:, 0:D], lambda d: ctxT[:, d, k * P:(k + 1) * P], lambda d: wkvx[:, d, 0:D]).then_inc(sem("kx_ps"), 1)
                    if k:
                        turn_keys(k - 1)
                turn_keys(KT - 1)
                for c in range(DC):
                    for half in range(2):
                        if c == 1 and half == 0:
                            pe.wait_ge(sem("xT_ready4"), TT)
                        mm = dense(bank(2 + 2 * c + half), lambda d: wkvx[:, d, D + c * P:D + (c + 1) * P],
                                   lambda d: ctxT[:, d, half * 512:(half + 1) * 512])
                    mm.then_inc(sem("vTx_ps"), 1)
                pe.wait_ge(sem("in_wqx"), 16)
                pe.wait_ge(sem("xT_ready4"), TT)
                pe.wait_ge(sem("kx_ready"), KT)
                for i in range(TT):
                    dense(bank(i // 2)[:, D * (i % 2):D * (i % 2) + D], tile_of(4, i), lambda d: wqx[:, d, :]).then_inc(sem("qx_ps"), 1)
                pe.wait_ge(sem("kTx_ready"), KT)
                pe.wait_ge(sem("qstack_ready"), 1)
                for c in range(HX // 2):
                    if c >= 2:
                        pe.wait_ge(sem("qTx_ready"), c - 1)
                    for i in range(TT):
                        mm = pe.transpose(bank(6 + c % 2).bitcast(BF16)[:, i * P:(i + 1) * P],
                                          qstack[:, i, c * P:(c + 1) * P], ident_b[:])
                    mm.then_inc(sem("qTx_ps"), 1)
                pe.wait_ge(sem("qTx_ready"), HX // 2)
                for c in range(DC):
                    pe.wait_ge(sem("iv_ready"), c + 1)
                    for k in range(KT):
                        mm = pe.transpose(bank(6 + c).bitcast(BF16)[:, k * P:(k + 1) * P], ivT[:, c, k * P:(k + 1) * P], ident_b[:])
                    mm.then_inc(sem("iv_ps"), 1)
                pe.wait_ge(sem("ivtok_ready"), DC)
                pe.wait_ge(sem("vTx_ready"), DC)
                pe.wait_ge(sem("qx_ready"), TT // 2)
                units = TT * HX

                def scores(u):
                    i, h = divmod(u, HX)
                    if u >= 2:
                        pe.wait_ge(sem("px_ready"), u - 1)
                    rows = slice(KW * (h % 2), KW * (h % 2) + 3 * DHX)
                    for half in range(2):
                        mm = pe.matmul(bank(2 * (u % 2) + half), qTx[rows, h // 2, i * P:(i + 1) * P],
                                       kTx[rows, h // 2, half * 512:(half + 1) * 512], start=True, stop=True)
                    mm.then_inc(sem("sx_ps"), 1)

                def turn(u):
                    pe.wait_ge(sem("px_ready"), u + 1)
                    if u >= 2:
                        pTx_ready(pe, u - 2)
                    for k in range(KT):
                        mm = pe.transpose(bank(4 + u % 2).bitcast(BF16)[:, k * P:(k + 1) * P],
                                          px[:, u % 2, k * P:(k + 1) * P].bitcast(BF16), ident_b[:])
                    mm.then_inc(sem("pTx_ps"), 1)

                def apply(u):
                    i, h = divmod(u, HX)
                    pTx_ready(pe, u)
                    for k in range(KT):
                        mm = pe.matmul(bank(6 + i % 2)[:, h * DHX:(h + 1) * DHX], pTx[:, u % 2, k * P:(k + 1) * P],
                                       iv[:, k, h * DHX:(h + 1) * DHX], start=k == 0, stop=k == KT - 1)
                    mm.then_inc(sem("ox_ps"), 1)

                def project_a(i):
                    pe.wait_ge(sem("attx_ready"), i + 1)
                    for c in range(DC):
                        mm = pe.transpose(bank(6 + i % 2)[:, D + c * P:D + (c + 1) * P], attx[:, i % 2, c * P:(c + 1) * P], ident[:])
                    mm.then_inc(sem("attTx_ps"), 1)

                def project_b(i):
                    pe.wait_ge(sem("attTx_ready"), i + 1)
                    dense(bank(6 + i % 2)[:, 0:D], lambda c: attTx[:, i % 2, c, :], lambda c: wpx[:, c, :]).then_inc(sem("proj5"), 1)

                pe.wait_ge(sem("in_wpx"), 16)
                scores(0)
                scores(1)
                for u in range(units + 1):
                    if u + 2 < units:
                        scores(u + 2)
                    if u < units:
                        turn(u)
                    if u > HX and u % HX == 3:
                        project_a(u // HX - 1)
                    if u > HX and u % HX == 5:
                        project_b(u // HX - 1)
                    if u % HX == 1 and u > 2 * HX:
                        pe.wait_ge(sem("res5_ready"), u // HX - 1)
                    if u:
                        apply(u - 1)
                project_a(TT - 1)
                project_b(TT - 1)

            def stage6():
                pe.wait_ge(sem("in_w_router1"), 16)
                for i in range(TT):
                    pe.wait_ge(sem("xT_ready5"), i + 1)
                    mm = dense(bank(0)[:, E1 * i:E1 * (i + 1)], tile_of(5, i), lambda c: w_router1[:, c, :])
                mm.then_inc(sem("score1_ps"), 1)
                pe.wait_ge(sem("picked_ready"), TT)
                for i in range(TT):
                    for k in range(i + 1):
                        mm = pe.matmul(bank(1)[:, E1 * i:E1 * (i + 1)], (tri_b if k == i else ones_b)[:], picked_b[:, k, :],
                                       start=k == 0, stop=k == i)
                mm.then_inc(sem("count_ps"), 1)
                pe.wait_ge(sem("gate1_ready"), 1)
                for i in range(TT):
                    mm = pe.transpose(bank(5)[0:E1, i * P:(i + 1) * P], gate1[:, i, :], ident[:])
                mm.then_inc(sem("gate1T_ps"), 1)
                for w in ("w_su", "w_sd", "w_up", "w_down"):
                    pe.wait_ge(sem("in_" + w), 16)
                pe.wait_ge(sem("gate1T_ready"), 1)

                def up(g):
                    if g >= 2:
                        pe.wait_ge(sem("hidden_ready"), g - 1)
                    xs = lambda c: xT[1][:, c, :]
                    if g < NG:
                        rows = slice(P * g, P * (g + 1))
                        dense(bank(g % 2), lambda c: w_up[:, c, 0, rows], xs)
                        dense(bank(2 + g % 2), lambda c: w_up[:, c, 1, rows], xs)
                        mm = pe.matmul(bank(4 + g % 2), spread[:, g * P:(g + 1) * P], gate1T, start=True, stop=True)
                    else:
                        dense(bank(g % 2)[0:HS, :], lambda c: w_su[:, c, HS:2 * HS], xs)
                        mm = dense(bank(2 + g % 2)[0:HS, :], lambda c: w_su[:, c, 0:HS], xs)
                    mm.then_inc(sem("up_ps"), 1)

                def down(g):
                    pe.wait_ge(sem("hidden_ready"), g + 1)
                    for i in range(TT):
                        tile = slice(i * P, (i + 1) * P)
                        if g < NG:
                            mm = pe.matmul(proj(i), hidden[:, g % 2, tile], w_down[:, g, :],
                                           start=g == 0 and i % 2 == 0, stop=False, skip_group_check=True)
                        else:
                            mm = pe.matmul(proj(i), shared[:, tile], w_sd[:], start=False, stop=True, skip_group_check=True)
                            mm.then_inc(sem("proj6"), 1)
                    if g < NG:
                        mm.then_inc(sem("hidden_used"), 1)

                up(0)
                for g in range(NG + 1):
                    if g < NG:
                        up(g + 1)
                    down(g)

            unit = [None, None, stage2, stage3, stage4, stage5, stage6]
            for n in range(1, STAGES + 1):
                if n > 1:
                    unit[n]()
                if n < STAGES:
                    transpose_x(n)

        @block.vector
        def _(dve):
            link = linker(dve, "dve_chain")
            TS, TTN, STT = dve.tensor_scalar, dve.tensor_tensor, dve.scalar_tensor_tensor

            dve.wait_ge(sem("in_mix"), 16)
            dve.tensor_reduce(mix_z[:, 0:1], mix, AX.X, ALU.max, negate=True).then_inc(sem("mixmax_ready"), 1)
            dve.wait_ge(sem("mixexp_ready"), 1)
            link(dve.reciprocal(mix_z[:, 2:3], mix_z[:, 1:2]))
            TS(mix, mix, mix_z[:, 2:3], None, ALU.mult).then_inc(sem("mix_ready"), 1)
            dve.wait_ge(sem("in_mask"), 16)
            link(TS(mask_add[:], mask_u8[:], 1.0, None, ALU.min))
            link(dve.tensor_reduce(valid[:], mask_add[:], AX.X, ALU.max))
            link(TS(mask_add[:], mask_add[:], -1.0, -16 * MASKED, ALU.add, ALU.mult))
            dve.wait_ge(sem("const_ready"), 1)
            link(dve.tensor_reduce(head_sel[:], head_of[:].rearrange("p g j -> p j g"), AX.X, ALU.add))
            dve.sem_inc(sem("head_sel_ready"), 1)
            dve.wait_ge(sem("in_idx_row"), 16)
            dve.wait_ge(sem("in_idx_col"), 16)
            link(TS(idx_row, idx_row, D - 1, None, ALU.bitwise_and))
            link(TS(idx_col[:], idx_col[:], D.bit_length() - 1, None, ALU.logical_shift_right))
            link(dve.tensor_copy(row_id, idx_col[:]))
            for c in range(DC):
                link(TS(col_hot[:, c, :], idx_row, part_id[:, c:c + 1], None, ALU.is_equal))
            for j in range(SJ):
                link(TS(row_hot[:, j, :], iota_row[:], row_id[:, j:j + 1], None, ALU.is_equal))
            dve.wait_ge(sem("imp_ready"), 1)
            for k in range(NS // 512):
                dve.wait_ge(sem("delta_ps"), k + 1)
                w = weighted[:, 512 * k:512 * (k + 1)]
                TTN(out=w, in0=bank(6 + k % 2)[0:E0, :], in1=w, op=ALU.mult).then_inc(sem("weighted_ready"), 1)
            dve.wait_ge(sem("weighted_ready"), NS // 512)
            dve.sem_inc(sem("hot_ready"), 1)

            for c in range(DC):
                dve.wait_ge(sem("exp_ready"), 2 * c + 1)
                link(STT(out=phi_k, in0=exp_kq[:, 0, :], scalar=1.0, in1=relu_kq[:, 0, :], op0=ALU.min, op1=ALU.add))
                link(TTN(out=kv, in0=phi_k, in1=bank(3 * c + 1), op=ALU.mult))
                if c:
                    dve.wait_ge(sem("num_ready"), c)
                dve.tensor_tensor_scan(kv_sum, keep_state[:], kv, 0.0, ALU.mult, ALU.add)
                link(dve.tensor_tensor_scan(k_sum, keep_state[:], phi_k, 0.0, ALU.mult, ALU.add))
                dve.wait_ge(sem("exp_ready"), 2 * c + 2)
                STT(out=phi_q, in0=exp_kq[:, 1, :], scalar=1.0, in1=relu_kq[:, 1, :], op0=ALU.min,
                    op1=ALU.add).then_inc(sem("phi_ready"), 1)
                dve.wait_ge(sem("phi_ready"), c + 1)
                dve.sem_inc(sem("sums_ready"), 1)
                link(TTN(out=den, in0=phi_q, in1=k_sum, op=ALU.mult))
                link(TS(den, den, EPS_LIN, None, ALU.add))
                link(dve.reciprocal(den, den))
                dve.wait_ge(sem("num_ready"), c + 1)
                TTN(out=lin[:, c, :], in0=num, in1=den, op=ALU.mult).then_inc(sem("lin_ready"), 1)

            def norm_stats(n, i):
                link(dve.bn_stats(stats[:, i, :], res[:, i, :]))
                dve.bn_aggr(meanvar[:, i, :], stats[:, i, :]).then_inc(sem(f"var_ready{n}"), 1)

            def norm_scale(n, i):
                dve.wait_ge(sem(f"rstd_ready{n}"), i + 1)
                TS(x_tok[n % 2][:, i, :], res[:, i, :], meanvar[:, i, 0:1], rstd[:, i:i + 1],
                   ALU.subtract, ALU.mult).then_inc(sem(f"x_ready{n}"), 1)

            def norm(n, residual):
                for i in range(TT):
                    residual(i)
                    norm_stats(n, i)
                    if i:
                        norm_scale(n, i - 1)
                norm_scale(n, TT - 1)

            def projected(n, i):
                dve.wait_ge(sem(f"proj{n}"), 2 * (i // 2) + 2)

            def residual1(i):
                projected(1, i)
                dve.wait_ge(sem("in_x"), 16)
                link(STT(out=res[:, i, :], in0=proj(i), scalar=16 ** -0.5, in1=x_tok[0][:, i, :], op0=ALU.mult, op1=ALU.add))

            def stage2():
                for i in range(TT):
                    dve.wait_ge(sem("s2_ps"), i + 1)
                    link(dve.tensor_tensor_reduce(s2[:, i, :], bank(i), mask_add[:, i // (TT // B), :], 1.0, LOWEST,
                                                  ALU.add, ALU.max, mx2[:, i:i + 1]))
                    TS(nb2[:, i:i + 1], mx2[:, i:i + 1], -1.0 / 16, None, ALU.mult).then_inc(sem("nb2_ready"), 1)
                for i in range(TT):
                    dve.wait_ge(sem("p2_ready"), i + 1)
                    link(dve.reciprocal(rz2[:, i:i + 1], z2[:, i:i + 1]))
                    link(TS(rz2[:, i:i + 1], rz2[:, i:i + 1], valid[:, i // (TT // B):i // (TT // B) + 1], None, ALU.mult))

            def residual2(i):
                projected(2, i)
                link(STT(out=res[:, i, :], in0=proj(i), scalar=rz2[:, i:i + 1], in1=x_tok[1][:, i, :], op0=ALU.mult, op1=ALU.add))

            def residual(n):
                def add(i):
                    projected(n, i)
                    link(TTN(out=res[:, i, :], in0=proj(i), in1=x_tok[(n - 1) % 2][:, i, :], op=ALU.add))
                return add

            def stage3():
                dve.wait_ge(sem("logit0_ps"), 1)
                link(TS(logit0.rearrange("p i e -> p (i e)"), bank(0)[:, 0:TT * E0], -50.0, 50.0, ALU.max, ALU.min))
                for i in range(TT):
                    link(dve.max(top0[:, i, :], logit0[:, i, :]))
                for i in range(TT):
                    link(dve.max_index(idx0[:, i, :], top0[:, i, :], logit0[:, i, :]))
                TTN(out=gap0, in0=top0[:, :, 1], in1=top0[:, :, 0], op=ALU.subtract).then_inc(sem("gap0_ready"), 1)
                link(dve.tensor_copy(idx0f, idx0))
                ids = iota_row[:, 0:E0].unsqueeze(1).broadcast_to([P, TT, E0])
                for k, hot_k in ((0, hot0), (1, hot1)):
                    link(TTN(out=hot_k, in0=idx0f[:, :, k:k + 1].broadcast_to([P, TT, E0]), in1=ids, op=ALU.is_equal))
                dve.wait_ge(sem("exp0_ready"), 1)
                link(TS(w10, exp0, 1.0, None, ALU.add))
                link(dve.reciprocal(w10, w10))
                link(TTN(out=w20, in0=w10, in1=exp0, op=ALU.mult))
                for hot_k, w in ((hot0, w10), (hot1, w20)):
                    link(TTN(out=hot_k, in0=hot_k, in1=w.unsqueeze(2).broadcast_to([P, TT, E0]), op=ALU.mult))
                TTN(out=gate0, in0=hot0, in1=hot1, op=ALU.add).then_inc(sem("gate0_ready"), 1)
                for j in range(SJ):
                    dve.wait_ge(sem("vals_ready"), j + 1)
                    if j >= 2:
                        dve.wait_ge(sem("prod_used"), j - 1)
                    TTN(out=prod[:, j % 2, :], in0=bank(2 if j % 2 else 1), in1=vals[:, j % 2, :],
                        op=ALU.mult).then_inc(sem("prod_ready"), 1)

            def stage4():
                dve.wait_ge(sem("v1_cleared"), 1)
                units_v = v1.rearrange("p (t j) w -> p t j w", j=HU)
                for k in range(TT // 2):
                    dve.wait_ge(sem("v1_ps"), 2 * k + 2)
                    heads = bank(4 + k).rearrange("p (t j d) -> p t j d", j=HU, d=DH1)
                    for j in range(HU):
                        v = dve.tensor_copy(units_v[:, 2 * k * (H1 // HU):2 * (k + 1) * (H1 // HU), j, j * DH1:(j + 1) * DH1],
                                            heads[:, :, j, :])
                    v.then_inc(sem("v1_ready"), 1)

                def maxima(u):
                    nk = 1 + u // (H1 // HU) % 2
                    dve.wait_ge(sem("s1_ps"), u + 1)
                    if u >= 2:
                        dve.wait_ge(sem("p1_ready"), u - 1)
                    dve.tensor_reduce(nmx1[:, u % 2, :], unit_s1(u)[:, 0:nk].rearrange("p b j k -> p j b k"), AX.XY, ALU.max,
                                      negate=True).then_inc(sem("max1_ready"), 1)

                def evacuate(u):
                    nk = 1 + u // (H1 // HU) % 2
                    dve.wait_ge(sem("pT1_ps"), u + 1)
                    if u >= 2:
                        dve.wait_ge(sem("o1_ps"), u - 1)
                    src = bank(4, 2).rearrange("p (j b q) -> p j b q", b=2, j=HU)[:, :, 0:nk, :]
                    dve.tensor_copy(unit_pT1(u)[:, :, 0:nk, :], src).then_inc(sem("pT1_ready"), 1)

                def invert_z(i):
                    dve.wait_ge(sem("p1_ready"), H1 // HU * (i + 1))
                    dve.reciprocal(rz1[:, i, :], z1[:, i, :]).then_inc(sem("rz1_ready"), 1)

                def take_sums(k):
                    dve.wait_ge(sem("o1_ps"), UC * (k + 1))
                    i, c = divmod(k, DC)
                    for g in range(UC):
                        o = dve.tensor_copy(attT1[g * HU * DH1:(g + 1) * HU * DH1, i % 2, c, :],
                                            bank(6)[0:HU * DH1, g * P:(g + 1) * P])
                    o.then_inc(sem("sums1_out"), 1)

                def take_z(i):
                    dve.wait_ge(sem("rzT1_ps"), i + 1)
                    dve.tensor_copy(rzT1, bank(7)[0:H1, 0:P]).then_inc(sem("rzT1_ready"), 1)

                def normalise(i):
                    dve.wait_ge(sem("zf1_ps"), i + 1)
                    dve.wait_ge(sem("sums1_out"), DC * (i + 1))
                    a = attT1[:, i % 2].rearrange("p c q -> p (c q)")
                    TTN(out=a, in0=bank(7)[:, P:P + D], in1=a, op=ALU.mult).then_inc(sem("att1_ready"), 1)

                def add(i):
                    dve.wait_ge(sem("proj4"), i + 1)
                    TTN(out=res[:, i, :], in0=bank(7)[:, 0:D], in1=x_tok[1][:, i, :], op=ALU.add).then_inc(sem("res4_ready"), 1)
                    dve.wait_ge(sem("res4_ready"), i + 1)

                per = H1 // HU
                units = TT * per
                maxima(0)
                for u in range(units):
                    i = u // per - 1
                    if u % UC == 1 and u > UC:
                        take_sums(u // UC - 1)
                    if i >= 0 and u % per == 2:
                        take_z(i)
                    if i >= 0 and u % per == 3:
                        normalise(i)
                    if u + 1 < units:
                        maxima(u + 1)
                    evacuate(u)
                    if i >= 0 and u % per == 0:
                        invert_z(i)
                    if i >= 0 and u % per == 5:
                        add(i)
                        norm_stats(4, i)
                    if i >= 0 and u % per == 6:
                        norm_scale(4, i)
                invert_z(TT - 1)
                take_sums(TT * DC - 1)
                take_z(TT - 1)
                normalise(TT - 1)
                add(TT - 1)
                norm_stats(4, TT - 1)
                norm_scale(4, TT - 1)

            def stage5():
                def quantise(am, sc, rs):
                    link(TS(sc, am, 1.0 / 127, 1e-8, ALU.mult, ALU.max))
                    link(dve.reciprocal(rs, sc))

                def nearest(z):
                    link(TS(z, z, ROUND, ROUND, ALU.add, ALU.subtract))
                    link(TS(z, z, 127.0, -127.0, ALU.min, ALU.max))

                link(dve.memset(kstack, 0.0))
                link(dve.memset(qstack, 0.0))
                for k in range(KT):
                    s = k % 2
                    dve.wait_ge(sem("kx_ps"), k + 1)
                    dve.wait_ge(sem("in_bkx"), 16)
                    TTN(out=kx[:, s, :], in0=bank(s)[:, 0:D], in1=bkx[:], op=ALU.add).then_inc(sem("kx_ready"), 1)
                    dve.wait_ge(sem("kx_ready"), k + 1)
                    heads = kx[:, s, :].rearrange("p (h d) -> p h d", h=HX)
                    link(dve.tensor_reduce(kam[:, k, :], heads, AX.X, ALU.max, apply_absolute_value=True))
                    quantise(kam[:, k, :], ksc[:, k, :], krs[:, k, :])
                    r = kr[:, s, :].rearrange("p (h d) -> p h d", h=HX)
                    link(TTN(out=r, in0=heads, in1=krs[:, k, :].unsqueeze(2).broadcast_to([P, HX, DHX]), op=ALU.mult))
                    nearest(kr[:, s, :])
                    z = ks[:, s, :].rearrange("p (h d) -> p h d", h=HX)
                    link(TTN(out=z, in0=r, in1=ksc[:, k, :].unsqueeze(2).broadcast_to([P, HX, DHX]), op=ALU.mult))
                    rest = kres[:, s, :].rearrange("p (h d) -> p h d", h=HX)
                    if k >= 2:
                        dve.wait_ge(sem("kTx_ps"), k - 1)
                    part = kstack[:, s, :].rearrange("p (h w) -> p h w", h=HX)
                    link(dve.tensor_copy(part[:, :, 0:DHX], z))
                    link(TTN(out=rest, in0=z, in1=part[:, :, 0:DHX], op=ALU.subtract))
                    link(dve.tensor_copy(part[:, :, DHX:2 * DHX], rest))
                    TTN(out=part[:, :, 2 * DHX:3 * DHX], in0=rest, in1=part[:, :, DHX:2 * DHX],
                        op=ALU.subtract).then_inc(sem("kstack_ready"), 1)
                    if k:
                        copy_kT(k - 1)
                copy_kT(KT - 1)
                for c in range(DC):
                    dve.wait_ge(sem("vTx_ready"), c + 1)
                    link(dve.tensor_reduce(vam[:, c:c + 1], vTx[:, c, :], AX.X, ALU.max, apply_absolute_value=True))
                    quantise(vam[:, c:c + 1], vsc[:, c:c + 1], vrs[:, c:c + 1])
                    link(TS(vr, vTx[:, c, :], vrs[:, c:c + 1], ROUND, ALU.mult, ALU.add))
                    link(TS(vr, vr, ROUND, 127.0, ALU.subtract, ALU.min))
                    TS(ivT[:, c, :], vr, -127.0, None, ALU.max).then_inc(sem("iv_ready"), 1)
                    dve.wait_ge(sem("iv_ready"), c + 1)
                dve.wait_ge(sem("in_bqx"), 16)
                for i in range(0, TT, 2):
                    dve.wait_ge(sem("qx_ps"), i + 2)
                    TTN(out=qx[:, i:i + 2, :], in0=bank(i // 2).rearrange("p (i d) -> p i d", i=2),
                        in1=bqx[:].unsqueeze(1).broadcast_to([P, 2, D]), op=ALU.add).then_inc(sem("qx_ready"), 1)
                dve.wait_ge(sem("qx_ready"), TT // 2)
                flat = qx.rearrange("p i d -> p (i d)")
                link(TS(flat, flat, DHX ** -0.5, None, ALU.mult))
                heads = flat.rearrange("p (h d) -> p h d", d=DHX)
                qam_, qsc_, qrs_ = (z.rearrange("p i h -> p (i h)") for z in (qam, qsc, qrs))
                link(dve.tensor_reduce(qam_, heads, AX.X, ALU.max, apply_absolute_value=True))
                quantise(qam_, qsc_, qrs_)
                link(TS(nqs.rearrange("p i h -> p (i h)"), qsc_, -1.0, None, ALU.mult))
                link(TTN(out=heads, in0=heads, in1=qrs_.unsqueeze(2).broadcast_to([P, TT * HX, DHX]), op=ALU.mult))
                nearest(flat)
                stack = qstack.rearrange("p i (h w) -> p (i h) w", w=KW)
                for k in range(3):
                    q = dve.tensor_copy(stack[:, :, k * DHX:(k + 1) * DHX], heads)
                q.then_inc(sem("qstack_ready"), 1)
                for c in range(DC):
                    dve.wait_ge(sem("iv_ps"), c + 1)
                    dve.tensor_copy(iv[:, :, c * P:(c + 1) * P],
                                    bank(6 + c).bitcast(BF16).rearrange("p (k d) -> p k d", k=KT)).then_inc(sem("ivtok_ready"), 1)
                dve.wait_ge(sem("in_bpx"), 16)
                link(TTN(out=x_tok[0][:], in0=x_tok[0][:], in1=bpx[:].unsqueeze(1).broadcast_to([P, TT, D]), op=ALU.add))

                def maximum(u):
                    dve.wait_ge(sem("sx_ps"), u + 1)
                    dve.tensor_reduce(mxx[:, u:u + 1], bank(2 * (u % 2), 2), AX.X, ALU.max).then_inc(sem("maxx_ready"), 1)

                def evacuate(u):
                    dve.wait_ge(sem("pTx_ps"), u + 1)
                    if u >= 2:
                        dve.wait_ge(sem("ox_ps"), u - 1)
                    dve.tensor_copy(pTx[:, u % 2, :], bank(4 + u % 2).bitcast(I16)).then_inc(sem("pTx_dve"), 1)

                def normalise(i):
                    dve.wait_ge(sem("px_ready"), HX * (i + 1))
                    link(dve.reciprocal(rzx[:, i, :], zx[:, i, :]))
                    dve.wait_ge(sem("ox_ps"), HX * (i + 1))
                    TTN(out=attx[:, i % 2, :].rearrange("p (h d) -> p h d", h=HX),
                        in0=bank(6 + i % 2)[:, 0:D].rearrange("p (h d) -> p h d", h=HX),
                        in1=rzx[:, i, :].unsqueeze(2).broadcast_to([P, HX, DHX]), op=ALU.mult).then_inc(sem("attx_ready"), 1)

                def add(i):
                    dve.wait_ge(sem("proj5"), i + 1)
                    TTN(out=res[:, i, :], in0=bank(6 + i % 2)[:, 0:D], in1=x_tok[0][:, i, :], op=ALU.add).then_inc(sem("res5_ready"), 1)
                    dve.wait_ge(sem("res5_ready"), i + 1)

                units = TT * HX
                maximum(0)
                maximum(1)
                for u in range(units):
                    if u + 2 < units:
                        maximum(u + 2)
                    if u % 3 < 2:
                        evacuate(u)
                    if u >= HX:
                        i = u // HX - 1
                        if u % HX == 1:
                            normalise(i)
                        if u % HX == 5:
                            add(i)
                            norm_stats(5, i)
                        if u % HX == NORM_AT:
                            norm_scale(5, i)
                normalise(TT - 1)
                add(TT - 1)
                norm_stats(5, TT - 1)
                norm_scale(5, TT - 1)

            def copy_kT(k):
                dve.wait_ge(sem("kTx_ps"), k + 1)
                dve.tensor_copy(kTx[:, :, k * P:(k + 1) * P],
                                bank(6 + k % 2).bitcast(BF16).rearrange("p (c t) -> p c t", c=HX // 2)).then_inc(sem("kTx_ready"), 1)

            def stage6():
                dve.wait_ge(sem("score1_ready"), 1)
                ids = iota_row[:, 0:E1].unsqueeze(1).broadcast_to([P, TOPK, E1])
                for i in range(TT):
                    link(dve.max(top1[:, i, :], score1[:, i, :]))
                for i in range(TT):
                    link(dve.max_index(idx1[:, i, :], top1[:, i, :], score1[:, i, :]))
                link(dve.tensor_copy(idx1f, idx1))
                link(dve.tensor_reduce(sum1, top1[:, :, 0:TOPK], AX.X, ALU.add))
                link(dve.reciprocal(rsum1, sum1))
                for i in range(TT):
                    link(TTN(out=hot, in0=idx1f[:, i, 0:TOPK].unsqueeze(2).broadcast_to([P, TOPK, E1]), in1=ids, op=ALU.is_equal))
                    link(dve.tensor_reduce(picked[:, i, :], hot.rearrange("p k e -> p e k"), AX.X, ALU.add))
                    dve.tensor_copy(picked_b[:, i, :], picked[:, i, :]).then_inc(sem("picked_ready"), 1)
                link(TTN(out=gate1, in0=picked, in1=score1, op=ALU.mult))
                link(TTN(out=gate1, in0=gate1, in1=rsum1.unsqueeze(2).broadcast_to([P, TT, E1]), op=ALU.mult))
                dve.wait_ge(sem("count_ps"), 1)
                flat = gate1.rearrange("p i e -> p (i e)")
                STT(out=flat, in0=bank(1)[:, 0:TT * E1], scalar=float(CAP), in1=flat, op0=ALU.is_le, op1=ALU.mult).then_inc(sem("gate1_ready"), 1)
                for g in range(NG + 1):
                    s = g % 2
                    dve.wait_ge(sem("silu_ready"), g + 1)
                    if g < NG:
                        link(TTN(out=gated[:, s, :], in0=bank(2 + s), in1=silu[:, s, :], op=ALU.mult))
                        if g >= 2:
                            dve.wait_ge(sem("hidden_used"), g - 1)
                        TTN(out=hidden[:, s, :], in0=bank(4 + s), in1=gated[:, s, :], op=ALU.mult).then_inc(sem("hidden_ready"), 1)
                    else:
                        TTN(out=shared, in0=bank(2 + s)[0:HS, :], in1=silu[0:HS, s, :], op=ALU.mult).then_inc(sem("hidden_ready"), 1)

            work = [None, None, stage2, stage3, stage4, stage5, stage6]
            adds = [None, residual1, residual2, residual(3), None, None, residual(6)]
            for n in range(1, STAGES + 1):
                if n > 1:
                    work[n]()
                if adds[n]:
                    norm(n, adds[n])


def _layout(a):
    def rows(v, shape):
        return np.broadcast_to(v, (P,) + shape)

    x = a["x"].reshape(N, D)
    ctx = a["ctx_2048"].reshape(B * M, D)
    idx = a["L0_ffn_mask_idx"]
    return {
        "x": x, "xT": x.T, "w_qkv0": a["L0_attn_W_qkv"].T, "w_out0": a["L0_attn_W_out"].T,
        "ctx": ctx, "ctxT": ctx.T, "mask": rows(a["mask_BxS2_bk0"], (B, M)),
        "w_router0": a["L0_ffn_gate_w"].T, "w_ffn0": a["L0_ffn_W"].T, "atoms": a["L0_ffn_atoms"],
        "mix": a["L0_ffn_expert_atom_weights"], "imp": a["L0_ffn_importance"],
        "idx": idx, "idx_row": rows(idx, (NS,)),
        "wq1": a["L1_attn_Wq"].T, "wk1": a["L1_attn_Wk"].T, "wv1": a["L1_attn_Wv"].T, "wo1": a["L1_attn_Wo"].T,
        "wqx": a["L1_xattn_Wq"], "wkvx": a["L1_xattn_Wkv"], "wpx": a["L1_xattn_Wp"],
        "bqx": rows(a["L1_xattn_bq"], (D,)), "bkx": rows(a["L1_xattn_bkv"][0:D], (D,)),
        "bvx": a["L1_xattn_bkv"][D:2 * D].reshape(DC, P).T, "bpx": rows(a["L1_xattn_bp"], (D,)),
        "w_router1": a["L1_ffn_w_gate"], "w_su": a["L1_ffn_w_shared_up"], "w_sd": a["L1_ffn_w_shared_down"],
        "w_up": a["L1_ffn_w_up"].reshape(E1, DC, P, 2, HE).transpose(2, 1, 3, 0, 4).reshape(P, -1), "w_down": a["L1_ffn_w_down"].reshape(E1 * HE, D),
    }


def kernel(**inputs):
    import numpy as _np
    import concourse.bacc as _bacc
    from concourse import mybir as _mybir
    from concourse.bass_utils import run_bass_kernel_spmd as _run

    nc = _bacc.Bacc("TRN2", target_bir_lowering=False, num_devices=1)
    arrays, tensors = {}, {}
    for name, a in _layout({k: _np.asarray(v) for k, v in inputs.items()}).items():
        a = _np.ascontiguousarray(a)
        arrays[f"in_{name}_dram"] = a
        tensors[name] = nc.dram_tensor(f"in_{name}_dram", a.shape, _mybir.dt.from_np(a.dtype), kind="ExternalInput").ap()
    out = nc.dram_tensor("out_0_dram", (N, D), _mybir.dt.float32, kind="ExternalOutput").ap()
    build(nc, tensors, out)
    r = _run(nc, [arrays], core_ids=[0])
    return r.results[0]["out_0_dram"].reshape(B, S, D)
```

```python
import math
from contextlib import ExitStack

import numpy as np
import concourse.bass as bass
from concourse import mybir
from concourse.alu_op_type import AluOpType as ALU

ACT = mybir.ActivationFunctionType
AX = mybir.AxisListType
F32 = mybir.dt.float32
BF16 = mybir.dt.bfloat16
I32 = mybir.dt.int32
I16 = mybir.dt.int16
U32 = mybir.dt.uint32
U8 = mybir.dt.uint8

P = 128
B, S, D = 2, 256, 256
N = B * S
TT = N // P
DC = D // P
M = 512
MT = M // P
KT = B * MT
EPS_LN = 1e-5
EPS_LIN = 1e-9
E0, NA, NS = 8, 64, 2048
SJ = NS // P
H1, DH1 = 32, 8
HU = 4
UC = P // (HU * DH1)
HX, DHX = 16, 16
PAIR = 2 * DHX
KW = 64
E1, HE, HS, TOPK, CAP = 64, 32, 64, 6, 128
EG = P // HE
NG = E1 // EG
MASKED = -1.0e30
LOWEST = -3.0e38
ROUND = 12582912.0
STAGES = 6
PX = 3
SHARE = ((2, 5, 7), 8)
TURN_AT = 1
VALUES_AT = (5, 11)
NORM_AT = 9


def build(nc, t, out):
    with ExitStack() as ctx:
        def sb(name, shape, dt=F32):
            return ctx.enter_context(nc.sbuf_tensor(name, shape, dt))

        sems = {}

        def sem(name):
            if name not in sems:
                sems[name] = ctx.enter_context(nc.semaphore(name))
            return sems[name]

        ps = ctx.enter_context(nc.psum_tensor("ps", [P, 8 * 512], F32))

        def bank(k, n=1):
            return ps[:, 512 * k:512 * (k + n)]

        x_tok = [sb("x_even", [P, TT, D]), sb("x_odd", [P, TT, D])]
        xT = [sb("xT_even", [P, DC, N]), sb("xT_odd", [P, DC, N])]
        res = sb("res", [P, TT, D])
        stats = sb("stats", [P, TT, 6])
        meanvar = sb("meanvar", [P, TT, 2])
        var_eps = sb("var_eps", [P, TT])
        rstd = sb("rstd", [P, TT])
        minus_half = sb("minus_half", [P, TT])
        w_qkv0 = sb("w_qkv0", [P, DC, 3 * D])
        w_out0 = sb("w_out0", [P, DC, D])
        ctxT = sb("ctxT", [P, DC, B * M])
        ctx_tok = sb("ctx_tok", [P, KT, D])
        mask_u8 = sb("mask_u8", [P, B, M], U8)
        mask_add = sb("mask_add", [P, B, M])
        valid = sb("valid", [P, B])
        w_ffn0 = sb("w_ffn0", [P, DC, D])
        w_router0 = sb("w_router0", [P, DC, E0])
        wq1 = sb("wq1", [P, DC, D])
        wk1 = sb("wk1", [P, DC, D])
        wv1 = sb("wv1", [P, DC, D])
        wo1 = sb("wo1", [P, DC, D])
        wqx = sb("wqx", [P, DC, D])
        wkvx = sb("wkvx", [P, DC, 2 * D])
        wpx = sb("wpx", [P, DC, D])
        bqx = sb("bqx", [P, D])
        bkx = sb("bkx", [P, D])
        bpx = sb("bpx", [P, D])
        bvx = sb("bvx", [P, DC])
        w_router1 = sb("w_router1", [P, DC, E1])
        w_su = sb("w_su", [P, DC, 2 * HS])
        w_sd = sb("w_sd", [HS, D])
        ident = sb("ident", [P, P])
        ident_b = sb("ident_b", [P, P], BF16)
        tri_b = sb("tri_b", [P, P], BF16)
        ones_b = sb("ones_b", [P, P], BF16)
        keep_state = sb("keep_state", [P, N])
        iota_row = sb("iota_row", [P, D])
        part_id = sb("part_id", [P, DC])
        win_own = sb("win_own", [P, HU, P], BF16)
        win_prev = sb("win_prev", [P, HU, P], BF16)
        zero = sb("zero", [P, 1])
        head_of = sb("head_of", [P, UC, HU])
        head_sel = sb("head_sel", [P, HU])
        head_rows = sb("head_rows", [H1, D])
        small = sb("small", [P, 2048])

        area = {"a": sb("area_a", [P, 12288]), "b": sb("area_b", [P, 14336])}
        taken = {"small": 0}
        area["small"] = small

        def carve(where, at, shape, dt=F32, rows=P):
            words = math.prod(shape) * mybir.dt.size(dt) // 4
            assert at + words <= area[where].shape[1], (where, at, shape)
            v = area[where][0:rows, at:at + words]
            if dt != F32:
                v = v.bitcast(dt)
            if len(shape) == 2:
                v = v.rearrange("p (a b) -> p a b", a=shape[0])
            if len(shape) == 3:
                v = v.rearrange("p (a b c) -> p a b c", a=shape[0], b=shape[1])
            return v

        def tiny(shape, dt=F32):
            v = carve("small", taken["small"], shape, dt)
            taken["small"] += (math.prod(shape) * mybir.dt.size(dt) + 3) // 4
            return v

        exp_kq = carve("a", 0, [2, N])
        relu_kq = carve("a", 2 * N, [2, N])
        phi_k = carve("a", 4 * N, [N])
        kv = carve("a", 5 * N, [N])
        kv_sum = carve("a", 6 * N, [N])
        k_sum = carve("a", 7 * N, [N])
        phi_q = carve("a", 8 * N, [N])
        den = carve("a", 9 * N, [N])
        num = carve("a", 10 * N, [N])
        lin = carve("a", 11 * N, [DC, N])
        s2 = carve("a", 8 * N, [TT, M])
        p2 = carve("a", 0, [TT, M])
        pT2 = carve("a", 4 * M, [TT, MT, P])
        mx2, nb2, z2, rz2 = tiny([TT]), tiny([TT]), tiny([TT]), tiny([TT])
        atoms = carve("b", 0, [NS], rows=NA)
        idx_row = carve("b", NS, [NS], I32)
        col_hot = carve("b", 2 * NS, [DC, NS])
        row_hot = carve("b", 4 * NS, [SJ, D])
        weighted = carve("b", 4 * NS + SJ * D, [NS], rows=E0)
        idx_col = sb("idx_col", [P, SJ], I32)
        row_id = tiny([SJ])
        mix = tiny([NA])[0:E0]
        mix_z = tiny([3])[0:E0]
        mixT = tiny([E0])[0:NA]
        vals = carve("a", 0, [2, N])
        prod = carve("a", 2 * N, [2, N])
        logit0, top0 = tiny([TT, E0]), tiny([TT, 8])
        idx0, idx0f = tiny([TT, 8], U32), tiny([TT, 8])
        gap0, exp0, w20, w10 = tiny([TT]), tiny([TT]), tiny([TT]), tiny([TT])
        hot0, hot1, gate0 = tiny([TT, E0]), tiny([TT, E0]), tiny([TT, E0])
        gate0T = carve("a", 4 * N, [N], rows=E0)
        qT1 = carve("a", 0, [DC, N])
        kT1 = carve("a", 2 * N, [DC, HU, N])
        v1 = carve("a", 10 * N, [TT * H1 // HU * HU, HU * DH1])
        p1 = carve("a", 18 * N, [2, HU * 2 * P])
        pT1 = carve("b", 8 * N, [2, HU * 2 * P])
        attT1 = carve("b", 12 * N, [2, DC, P])
        rzT1 = carve("b", 13 * N, [P], rows=H1)
        nmx1, z1, rz1 = tiny([2, HU]), tiny([TT, H1]), tiny([TT, H1])
        vTx = carve("a", 13 * N, [DC, B * M])
        kx = carve("a", 17 * N, [KT, D])
        kr = carve("a", 5 * N, [2, D])
        ks = carve("a", 6 * N, [2, D])
        kres = carve("a", 7 * N, [2, D])
        kstack = carve("a", 8 * N, [2, HX * KW], BF16)
        vr = carve("a", 10 * N, [B * M])
        ivT = carve("a", 22 * N, [DC, B * M], BF16)
        kTx = carve("b", 0, [HX // 2, B * M], BF16)
        px = carve("b", 8 * N, [PX, B * M], I16)
        ivh = carve("b", 14 * N, [KT * HX, PAIR], BF16)
        qstack = carve("b", 18 * N, [TT, HX * KW], BF16)
        qTx = carve("b", 22 * N, [HX // 2, N], BF16)
        qx = carve("a", 10 * N, [TT, D])
        pair_rows = sb("pair_rows", [HX, D])
        rzTx = sb("rzTx", [HX, P])
        attTx = sb("attTx", [P, 2, DC, P])
        kam, ksc, krs = tiny([KT, HX]), tiny([KT, HX]), tiny([KT, HX])
        vam, vsc, vrs = tiny([DC]), tiny([DC]), tiny([DC])
        qam, qsc, qrs = tiny([TT, HX]), tiny([TT, HX]), tiny([TT, HX])
        mxx, nbx = tiny([TT * HX]), tiny([TT * HX])
        zx, rzx = tiny([TT, HX]), tiny([TT, HX])
        sx = carve("a", DC * E1 * 2 * HE, [3, B * M])
        pTx = carve("a", DC * E1 * 2 * HE + 3 * B * M, [2, KT * P], BF16)
        w_up = carve("a", 0, [DC, 2, E1 * HE])
        w_down = carve("a", DC * E1 * 2 * HE, [NG, D])
        spread = sb("spread", [E1, NG * P])
        gate1T = carve("b", 0, [N], rows=E1)
        silu = carve("b", N, [2, N])
        gated = carve("b", 3 * N, [2, N])
        hidden = carve("b", 5 * N, [2, N])
        shared = carve("b", 7 * N, [N], rows=HS)
        score1 = carve("b", 8 * N, [TT, E1])
        hot = carve("b", 8 * N + TT * E1, [TOPK, E1])
        picked = carve("b", 8 * N + TT * E1 + TOPK * E1, [TT, E1])
        picked_b = carve("b", 8 * N + 2 * TT * E1 + TOPK * E1, [TT, E1], BF16)
        gate1 = carve("b", 8 * N + 3 * TT * E1 + TOPK * E1, [TT, E1])
        top1, idx1, idx1f = tiny([TT, 8]), tiny([TT, 8], U32), tiny([TT, 8])
        sum1, rsum1 = tiny([TT]), tiny([TT])

        def proj(i):
            return bank(6 + i // 2)[:, D * (i % 2):D * (i % 2) + D]

        def by_scalar(u):
            return u % SHARE[1] in SHARE[0]

        def pTx_ready(eng, u):
            by_act = by_scalar(u)
            eng.wait_ge(sem("pTx_act" if by_act else "pTx_dve"), sum(by_scalar(k) == by_act for k in range(u + 1)))

        def unit_s1(u):
            return bank(2 * (u % 2), 2).rearrange("p (b j k) -> p b j k", b=2, j=HU)

        def unit_p1(u):
            return p1[:, u % 2].rearrange("p (j b k) -> p j b k", b=2, j=HU)

        def unit_pT1(u):
            return pT1[:, u % 2].rearrange("p (j b q) -> p j b q", b=2, j=HU)

        block = ctx.enter_context(nc.Block())

        def linker(eng, name):
            count = [0]

            def link(ins):
                count[0] += 1
                ins.then_inc(sem(name), 1)
                eng.wait_ge(sem(name), count[0])
            return link

        @block.sync
        def _(sp):
            def load(name, dst, src, of=None):
                sp.dma_start(dst, src).then_inc(sem("in_" + (of or name)), 16)

            two = "(c p) n -> p c n"
            load("xT", xT[0][:], t["xT"].rearrange(two, p=P))
            load("w_qkv0", w_qkv0[:], t["w_qkv0"].rearrange(two, p=P))
            load("mix", mix, t["mix"])
            load("idx_col", idx_col[:], t["idx"].rearrange("(p j) -> p j", j=SJ))
            load("idx_row", idx_row, t["idx_row"])
            load("mask", mask_u8[:], t["mask"])
            load("ctxT", ctxT[:], t["ctxT"].rearrange(two, p=P))
            load("wkvx", wkvx[:], t["wkvx"].rearrange(two, p=P), of="keys")
            load("bkx", bkx[:], t["bkx"], of="keys")
            load("bvx", bvx[:], t["bvx"], of="keys")
            load("atoms", atoms, t["atoms"])
            load("imp", weighted, t["imp"])
            load("x", x_tok[0][:], t["x"].rearrange("(i p) d -> p i d", p=P))
            load("w_out0", w_out0[:], t["w_out0"].rearrange(two, p=P))
            load("ctx", ctx_tok[:], t["ctx"].rearrange("(k p) d -> p k d", p=P))
            load("w_router0", w_router0[:], t["w_router0"].rearrange(two, p=P))
            load("w_ffn0", w_ffn0[:], t["w_ffn0"].rearrange(two, p=P))
            load("wq1", wq1[:], t["wq1"].rearrange(two, p=P), of="stage4")
            load("wk1", wk1[:], t["wk1"].rearrange(two, p=P), of="stage4")
            load("wv1", wv1[:], t["wv1"].rearrange(two, p=P), of="stage4")
            load("wo1", wo1[:], t["wo1"].rearrange(two, p=P), of="stage4")
            load("wqx", wqx[:], t["wqx"].rearrange(two, p=P), of="stage5")
            load("wpx", wpx[:], t["wpx"].rearrange(two, p=P), of="stage5")
            load("bqx", bqx[:], t["bqx"], of="stage5")
            load("bpx", bpx[:], t["bpx"], of="stage5")
            load("w_router1", w_router1[:], t["w_router1"].rearrange(two, p=P), of="stage6")
            load("w_su", w_su[:], t["w_su"].rearrange(two, p=P), of="stage6")
            load("w_sd", w_sd[:], t["w_sd"], of="stage6")
            if STAGES >= 6:
                sp.wait_ge(sem("qstack_ready"), 1)
                load("w_up", w_up.rearrange("p c k h -> p (c k h)"), t["w_up"])
                sp.wait_ge(sem("px_ready"), TT * HX)
                sp.wait_ge(sem("ox_ps"), TT * HX)
                load("w_down", w_down, t["w_down"].rearrange("(g p) d -> p g d", p=P))
            for i in range(TT):
                sp.wait_ge(sem(f"x_ready{STAGES}"), i + 1)
                sp.dma_start(out[i * P:(i + 1) * P, :], x_tok[STAGES % 2][:, i, :]).then_inc(sem("out_done"), 16)
            sp.wait_ge(sem("out_done"), 16 * TT)

        @block.gpsimd
        def _(pool):
            link = linker(pool, "pool_chain")

            pool.memset(minus_half[:], -0.5)
            pool.memset(keep_state[:], 1.0)
            pool.memset(zero[:], 0.0)
            pool.memset(ident[:], 0.0)
            pool.memset(ident_b[:], 0.0)
            pool.memset(tri_b[:], 1.0)
            pool.memset(ones_b[:], 1.0)
            pool.memset(win_own[:], 0.0)
            pool.memset(win_prev[:], 0.0)
            pool.memset(head_of[:], 1.0)
            pool.memset(head_rows[:], 1.0)
            pool.memset(pair_rows[:], 1.0)
            link(pool.memset(spread[:], 1.0))
            link(pool.memset(keep_state[:, S:S + 1], 0.0))

            def select(buf, pattern, base, mult, op, fill):
                return pool.affine_select(out=buf, in_=buf, compare_op=op, fill=fill, base=base,
                                          pattern=pattern, channel_multiplier=mult)

            link(select(ident[:], [[-1, P]], 0, 1, ALU.not_equal, 1.0))
            link(select(ident_b[:], [[-1, P]], 0, 1, ALU.not_equal, 1.0))
            pool.iota(iota_row[:], [[1, D]], base=0, channel_multiplier=0, allow_small_or_imprecise_dtypes=True)
            link(pool.iota(part_id[:], [[P, DC]], base=0, channel_multiplier=1, allow_small_or_imprecise_dtypes=True))
            link(select(tri_b[:], [[1, P]], 0, -1, ALU.is_ge, 0.0))
            link(select(win_own[:], [[0, HU], [-1, P]], 0, 1, ALU.is_ge, MASKED))
            link(select(win_prev[:], [[0, HU], [1, P]], 0, -1, ALU.is_ge, MASKED))
            span = [[-HU * DH1, UC], [-DH1, HU]]
            link(select(head_of[:], span, 0, 1, ALU.is_ge, 0.0))
            link(select(head_of[:], [[HU * DH1, UC], [DH1, HU]], DH1 - 1, -1, ALU.is_ge, 0.0))
            link(select(head_rows[:], [[1, D]], 0, -DH1, ALU.is_ge, 0.0))
            link(select(head_rows[:], [[-1, D]], DH1 - 1, DH1, ALU.is_ge, 0.0))
            link(select(pair_rows[:], [[1, D]], 0, -DHX, ALU.is_ge, 0.0))
            link(select(pair_rows[:], [[-1, D]], DHX - 1, DHX, ALU.is_ge, 0.0))
            link(select(spread[:], [[1, NG * P]], 0, -HE, ALU.is_ge, 0.0))
            link(select(spread[:], [[-1, NG * P]], HE - 1, HE, ALU.is_ge, 0.0))
            pool.sem_inc(sem("const_ready"), 1)

            def linear_numerator(c):
                pool.wait_ge(sem("sums_ready"), c + 1)
                if c:
                    pool.wait_ge(sem("lin_ready"), c)
                pool.tensor_tensor(out=num, in0=phi_q, in1=kv_sum, op=ALU.mult).then_inc(sem("num_ready"), 1)

            def inverse_deviation(n, i):
                pool.wait_ge(sem(f"var_ready{n}"), i + 1)
                link(pool.tensor_scalar(var_eps[:, i:i + 1], meanvar[:, i, 1:2], EPS_LN, None, ALU.add))
                pool.tensor_tensor(out=rstd[:, i:i + 1], in0=var_eps[:, i:i + 1], in1=minus_half[:, i:i + 1],
                                   op=ALU.pow).then_inc(sem(f"rstd_ready{n}"), 1)

            for c in range(DC):
                linear_numerator(c)
            def stack_keys(k):
                s = k % 2
                pool.wait_ge(sem("kr_ready"), k + 1)
                z = ks[:, s, :].rearrange("p (h d) -> p h d", h=HX)
                r = kr[:, s, :].rearrange("p (h d) -> p h d", h=HX)
                rest = kres[:, s, :].rearrange("p (h d) -> p h d", h=HX)
                part = kstack[:, s, :].rearrange("p (h w) -> p h w", h=HX)
                scale = ksc[:, k, :].unsqueeze(2).broadcast_to([P, HX, DHX])
                pool.tensor_tensor(out=z, in0=r, in1=scale, op=ALU.mult).then_inc(sem("ks_ready"), 1)
                pool.wait_ge(sem("ks_ready"), k + 1)
                if k >= 2:
                    pool.wait_ge(sem("kTx_ps"), k - 1)
                link(pool.tensor_copy(part[:, :, 0:DHX], z))
                link(pool.tensor_tensor(out=rest, in0=z, in1=part[:, :, 0:DHX], op=ALU.subtract))
                link(pool.tensor_copy(part[:, :, DHX:2 * DHX], rest))
                pool.tensor_tensor(out=part[:, :, 2 * DHX:3 * DHX], in0=rest, in1=part[:, :, DHX:2 * DHX],
                                   op=ALU.subtract).then_inc(sem("kstack_ready"), 1)

            for n in range(1, STAGES + 1):
                if n == 3:
                    pool.wait_ge(sem("x_ready2"), TT)
                    link(pool.memset(kstack, 0.0))
                    for k in range(KT):
                        stack_keys(k)
                if n == 5:
                    for u in range(TT * HX):
                        pool.wait_ge(sem("maxx_ready"), u + 1)
                        pool.tensor_scalar(nbx[:, u:u + 1], mxx[:, u:u + 1], -1.0, math.log(255.0),
                                           ALU.mult, ALU.add).then_inc(sem("biasx_ready"), 1)
                        if u > HX and u % HX == NORM_AT - 2:
                            inverse_deviation(5, u // HX - 1)
                for i in range(TT - 1 if n == 5 else 0, TT):
                    inverse_deviation(n, i)
                if n == 3 and STAGES > 3:
                    pool.wait_ge(sem("x_ready3"), TT)
                    pool.memset(v1, 0.0).then_inc(sem("v1_cleared"), 1)
                    pool.memset(ivh, 0.0).then_inc(sem("ivh_cleared"), 1)
                    pool.memset(qstack, 0.0).then_inc(sem("qstack_cleared"), 1)

        @block.scalar
        def _(act):
            link = linker(act, "act_chain")

            act.wait_ge(sem("mixmax_ready"), 1)
            act.activation(mix, mix, ACT.Exp, bias=mix_z[:, 0:1], accum_out=mix_z[:, 1:2]).then_inc(sem("mixexp_ready"), 1)

            for c in range(DC):
                act.wait_ge(sem("qkv_ps"), c + 1)
                if c:
                    act.wait_ge(sem("phi_ready"), c)
                for m, b in ((0, 3 * c), (1, 3 * c + 2)):
                    act.activation(exp_kq[:, m, :], bank(b), ACT.Exp)
                    act.activation(relu_kq[:, m, :], bank(b), ACT.Relu).then_inc(sem("exp_ready"), 1)
            act.wait_ge(sem("mixT_ps"), 1)
            act.activation(mixT, bank(7)[0:NA, 0:E0], ACT.Copy).then_inc(sem("mixT_ready"), 1)
            act.wait_ge(sem("in_imp"), 16)
            act.activation(weighted, weighted, ACT.Sigmoid).then_inc(sem("imp_ready"), 1)
            for k in range(KT):
                act.wait_ge(sem("kx_ps"), k + 1)
                act.activation(kx[:, k, :], bank(6 + k % 2)[:, 0:D], ACT.Copy).then_inc(sem("kx_out"), 1)
            act.wait_ge(sem("in_keys"), 3 * 16)
            for v in range(DC * B):
                c, half = divmod(v, B)
                act.wait_ge(sem("vTx_ps"), v + 1)
                act.activation(vTx[:, c, half * M:(half + 1) * M], bank(6 + v % 2), ACT.Identity,
                               bias=bvx[:, c:c + 1]).then_inc(sem("vTx_ready"), 1)

            def to_xT(n):
                for i in range(TT):
                    act.wait_ge(sem(f"xT_ps{n}"), i + 1)
                    slot = bank(4 + i % 2)[:, 0:D].rearrange("p (c t) -> p c t", c=DC)
                    act.activation(xT[n % 2][:, :, i * P:(i + 1) * P], slot, ACT.Copy).then_inc(sem(f"xT_ready{n}"), 1)

            def stage2():
                for i in range(TT):
                    act.wait_ge(sem("nb2_ready"), i + 1)
                    act.activation(p2[:, i, :], s2[:, i, :], ACT.Exp, bias=nb2[:, i:i + 1], scale=1.0 / 16,
                                   accum_out=z2[:, i:i + 1]).then_inc(sem("p2_ready"), 1)
                    if i:
                        evac2(i - 1)
                evac2(TT - 1)

            def evac2(i):
                act.wait_ge(sem("pT2_ps"), i + 1)
                act.activation(pT2[:, i].rearrange("p k q -> p (k q)"), bank(4 + i % 2), ACT.Copy).then_inc(sem("pT2_ready"), 1)

            def stage3():
                act.wait_ge(sem("gap0_ready"), 1)
                act.activation(exp0, gap0, ACT.Exp).then_inc(sem("exp0_ready"), 1)
                act.wait_ge(sem("gate0T_ps"), 1)
                act.activation(gate0T, bank(0)[0:E0, :], ACT.Copy).then_inc(sem("gate0T_ready"), 1)
                for j in range(SJ + 2):
                    if j < SJ:
                        act.wait_ge(sem("vals_ps"), j + 1)
                        if j >= 2:
                            act.wait_ge(sem("prod_ready"), j - 1)
                        act.activation(vals[:, j % 2, :], bank(3 + j % 2 * 2), ACT.Copy).then_inc(sem("vals_ready"), 1)
                    if j - 2 >= TURN_AT and j % 2 == TURN_AT % 2:
                        k = (j - 2 - TURN_AT) // 2
                        act.wait_ge(sem("kTx_ps"), k + 1)
                        act.activation(kTx[:, :, k * P:(k + 1) * P], bank(4).bitcast(BF16).rearrange("p (c t) -> p c t", c=HX // 2),
                                       ACT.Copy).then_inc(sem("kTx_ready"), 1)

            def stage4():
                for c in range(DC):
                    act.wait_ge(sem("qk1_ps"), 2 * c + 1)
                    act.activation(qT1[:, c, :], bank(2 * c), ACT.Copy, scale=DH1 ** -0.5).then_inc(sem("qT1_ready"), 1)
                    act.wait_ge(sem("qk1_ps"), 2 * c + 2)
                    act.wait_ge(sem("head_sel_ready"), 1)
                    for j in range(HU):
                        a = act.activation(kT1[:, c, j, :], bank(2 * c + 1), ACT.Copy, scale=head_sel[:, j:j + 1])
                    a.then_inc(sem("kT1_ready"), 1)
                for u in range(TT * H1 // HU):
                    i, g = divmod(u, H1 // HU)
                    nk = 1 + i % 2
                    act.wait_ge(sem("max1_ready"), u + 1)
                    if u >= 2:
                        act.wait_ge(sem("pT1_ps"), u - 1)
                    for j in range(HU):
                        a = act.activation(unit_p1(u)[:, j, 0:nk, :], unit_s1(u)[:, 0:nk, j, :], ACT.Exp,
                                           bias=nmx1[:, u % 2, j:j + 1],
                                           accum_out=z1[:, i, HU * g + j:HU * g + j + 1])
                    a.then_inc(sem("p1_ready"), 1)

            def stage5():
                for c in range(HX // 2):
                    act.wait_ge(sem("qTx_ps"), c + 1)
                    act.activation(qTx[:, c, :], bank(6 + c % 2)[:, 0:N // 2].bitcast(BF16), ACT.Copy).then_inc(sem("qTx_ready"), 1)
                for u in range(TT * HX):
                    i, h = divmod(u, HX)
                    act.wait_ge(sem("biasx_ready"), u + 1)
                    if u >= PX:
                        act.wait_ge(sem("pTx_ps"), u - PX + 1)
                    act.activation(px[:, u % PX, :], sx[:, u % 3, :], ACT.Exp, bias=nbx[:, u:u + 1],
                                   accum_out=zx[:, i, h:h + 1]).then_inc(sem("px_ready"), 1)
                    if u and by_scalar(u - 1):
                        evac_px(u - 1)
                    if h == 1 and i:
                        evac_sums(i - 1)
                    if h == 3 and i:
                        evac_z(i - 1)
                if by_scalar(TT * HX - 1):
                    evac_px(TT * HX - 1)
                evac_sums(TT - 1)
                evac_z(TT - 1)

            def evac_px(u):
                act.wait_ge(sem("pTx_ps"), u + 1)
                if u >= 2:
                    act.wait_ge(sem("ox_ps"), u - 1)
                act.activation(pTx[:, u % 2, :], bank(4 + u % 2).bitcast(I16), ACT.Copy).then_inc(sem("pTx_act"), 1)

            def evac_sums(i):
                act.wait_ge(sem("ox_ps"), HX * (i + 1))
                if i >= 2:
                    act.wait_ge(sem("proj5"), i - 1)
                for c in range(DC):
                    a = act.activation(attTx[:, i % 2, c, :], bank(6 + i % 2)[:, c * P:(c + 1) * P], ACT.Copy,
                                       scale=vsc[:, c:c + 1])
                a.then_inc(sem("sumsx_out"), 1)

            def evac_z(i):
                act.wait_ge(sem("rzTx_ps"), i + 1)
                act.activation(rzTx[:], bank(6 + i % 2)[0:HX, 0:P], ACT.Copy).then_inc(sem("rzTx_ready"), 1)

            def stage6():
                act.wait_ge(sem("score1_ps"), 1)
                act.activation(score1.rearrange("p i e -> p (i e)"), bank(0)[:, 0:TT * E1], ACT.Sigmoid).then_inc(sem("score1_ready"), 1)
                act.wait_ge(sem("gate1T_ps"), 1)
                act.activation(gate1T, bank(5)[0:E1, :], ACT.Copy).then_inc(sem("gate1T_ready"), 1)
                for g in range(NG + 1):
                    act.wait_ge(sem("up_ps"), g + 1)
                    if g >= 2:
                        act.wait_ge(sem("hidden_ready"), g - 1)
                    rows = P if g < NG else HS
                    act.activation(silu[0:rows, g % 2, :], bank(g % 2)[0:rows, :], ACT.Silu).then_inc(sem("silu_ready"), 1)

            unit = [None, None, stage2, stage3, stage4, stage5, stage6]
            for n in range(1, STAGES + 1):
                if n > 1:
                    unit[n]()
                if n < STAGES:
                    to_xT(n)

        @block.tensor
        def _(pe):
            def dense(dst, lhsT, rhs, start=True, stop=True, **kw):
                for c in range(DC):
                    mm = pe.matmul(dst, lhsT(c), rhs(c), start=start and c == 0, stop=stop and c == DC - 1, **kw)
                return mm

            pe.wait_ge(sem("in_xT"), 16)
            pe.wait_ge(sem("in_w_qkv0"), 16)
            for c in range(DC):
                for k, m in enumerate((1, 2, 0)):
                    mm = dense(bank(3 * c + k), lambda d: w_qkv0[:, d, D * m + P * c:D * m + P * (c + 1)],
                               lambda d: xT[0][:, d, :])
                mm.then_inc(sem("qkv_ps"), 1)
            pe.wait_ge(sem("const_ready"), 1)
            pe.wait_ge(sem("mix_ready"), 1)
            pe.transpose(bank(7)[0:NA, 0:E0], mix, ident[0:E0, 0:E0]).then_inc(sem("mixT_ps"), 1)
            pe.wait_ge(sem("in_ctxT"), 16)
            pe.wait_ge(sem("in_keys"), 3 * 16)
            for k in range(KT):
                if k == 1:
                    pe.wait_ge(sem("mixT_ready"), 1)
                if k >= 2:
                    pe.wait_ge(sem("kx_out"), k - 1)
                dense(bank(6 + k % 2)[:, 0:D], lambda d: ctxT[:, d, k * P:(k + 1) * P], lambda d: wkvx[:, d, 0:D]).then_inc(sem("kx_ps"), 1)
            for v in range(DC * B):
                c, half = divmod(v, B)
                if v < 2:
                    pe.wait_ge(sem("kx_out"), KT - 1 + v)
                else:
                    pe.wait_ge(sem("vTx_ready"), v - 1)
                dense(bank(6 + v % 2), lambda d: wkvx[:, d, D + c * P:D + (c + 1) * P],
                      lambda d: ctxT[:, d, half * M:(half + 1) * M]).then_inc(sem("vTx_ps"), 1)
            pe.wait_ge(sem("in_atoms"), 16)
            pe.wait_ge(sem("exp_ready"), DC + 1)
            pe.wait_ge(sem("phi_ready"), 1)
            for k in range(NS // 512):
                pe.matmul(bank(k)[0:E0, :], mixT, atoms[:, 512 * k:512 * (k + 1)],
                          start=True, stop=True).then_inc(sem("delta_ps"), 1)
            pe.wait_ge(sem("vTx_ready"), DC * B)
            pe.wait_ge(sem("lin_ready"), DC)
            pe.wait_ge(sem("in_w_out0"), 16)
            for i in range(TT):
                dense(proj(i), lambda c: lin[:, c, i * P:(i + 1) * P], lambda c: w_out0[:, c, :]).then_inc(sem("proj1"), 1)

            def transpose_x(n):
                for i in range(TT):
                    pe.wait_ge(sem(f"x_ready{n}"), i + 1)
                    if n == 3 and i == 0:
                        pe.wait_ge(sem("kTx_ready"), KT)
                    if i >= 2:
                        pe.wait_ge(sem(f"xT_ready{n}"), i - 1)
                    for c in range(DC):
                        mm = pe.transpose(bank(4 + i % 2)[:, c * P:(c + 1) * P], x_tok[n % 2][:, i, c * P:(c + 1) * P], ident[:])
                    mm.then_inc(sem(f"xT_ps{n}"), 1)

            def tile_of(n, i):
                return lambda c: xT[n % 2][:, c, i * P:(i + 1) * P]

            def stage2():
                pe.wait_ge(sem("in_ctxT"), 16)
                for i in range(TT):
                    b = i // (TT // B)
                    pe.wait_ge(sem("weighted_ready"), i + 1)
                    pe.wait_ge(sem("xT_ready1"), i + 1)
                    dense(bank(i), tile_of(1, i), lambda c: ctxT[:, c, b * M:(b + 1) * M]).then_inc(sem("s2_ps"), 1)
                pe.wait_ge(sem("in_ctx"), 16)
                pe.wait_ge(sem("xT_ready1"), TT)
                for i in range(TT + 1):
                    if i < TT:
                        pe.wait_ge(sem("p2_ready"), i + 1)
                        if i >= 2:
                            pe.wait_ge(sem("pT2_ready"), i - 1)
                        for k in range(MT):
                            mm = pe.transpose(bank(4 + i % 2)[:, k * P:(k + 1) * P], p2[:, i, k * P:(k + 1) * P], ident[:])
                        mm.then_inc(sem("pT2_ps"), 1)
                    if i:
                        b = (i - 1) // (TT // B)
                        pe.wait_ge(sem("pT2_ready"), i)
                        for k in range(MT):
                            mm = pe.matmul(proj(i - 1), pT2[:, i - 1, k, :], ctx_tok[:, b * MT + k, :],
                                           start=k == 0, stop=k == MT - 1)
                        mm.then_inc(sem("proj2"), 1)

            def stage3():
                pe.wait_ge(sem("in_w_router0"), 16)
                pe.wait_ge(sem("in_w_ffn0"), 16)
                for i in range(TT):
                    pe.wait_ge(sem("xT_ready2"), i + 1)
                    mm = dense(bank(0)[:, E0 * i:E0 * (i + 1)], tile_of(2, i), lambda c: w_router0[:, c, :])
                mm.then_inc(sem("logit0_ps"), 1)
                for i in range(TT):
                    dense(proj(i), tile_of(2, i), lambda c: w_ffn0[:, c, :], start=i % 2 == 0, stop=False,
                          skip_group_check=True)

                def gather(j):
                    if j >= 2:
                        pe.wait_ge(sem("prod_ready"), j - 1)
                    dense(bank(2 if j % 2 else 1), lambda c: col_hot[:, c, j:NS:SJ], lambda c: xT[0][:, c, :])

                def values(j):
                    if j >= 2:
                        pe.wait_ge(sem("vals_ready"), j - 1)
                    pe.matmul(bank(3 + j % 2 * 2), weighted[:, j:NS:SJ], gate0T, start=True, stop=True).then_inc(sem("vals_ps"), 1)

                def turn_keys(k):
                    pe.wait_ge(sem("kstack_ready"), k + 1)
                    if k:
                        pe.wait_ge(sem("kTx_ready"), k)
                    for c in range(HX // 2):
                        mm = pe.transpose(bank(4).bitcast(BF16)[:, c * P:(c + 1) * P], kstack[:, k % 2, c * P:(c + 1) * P], ident_b[:])
                    mm.then_inc(sem("kTx_ps"), 1)

                gather(0)
                gather(1)
                pe.wait_ge(sem("gate0_ready"), 1)
                for i in range(TT):
                    mm = pe.transpose(bank(0)[0:E0, i * P:(i + 1) * P], gate0[:, i, :], ident[:])
                mm.then_inc(sem("gate0T_ps"), 1)
                pe.wait_ge(sem("gate0T_ready"), 1)
                values(0)
                values(1)
                for j in range(SJ):
                    pe.wait_ge(sem("prod_ready"), j + 1)
                    for i in range(TT):
                        mm = pe.matmul(proj(i), prod[:, j % 2, i * P:(i + 1) * P], row_hot[:, j, :],
                                       start=False, stop=j == SJ - 1, skip_group_check=True)
                        if j == SJ - 1:
                            mm.then_inc(sem("proj3"), 1)
                    if j < SJ - 1:
                        mm.then_inc(sem("prod_used"), 1)
                    if j + 2 < SJ:
                        gather(j + 2)
                        values(j + 2)
                    if j >= TURN_AT and j % 2 == TURN_AT % 2:
                        turn_keys((j - TURN_AT) // 2)

            def stage4():
                pe.wait_ge(sem("in_stage4"), 4 * 16)
                pe.wait_ge(sem("xT_ready3"), TT)
                for c in range(DC):
                    for k, w in ((0, wq1), (1, wk1)):
                        dense(bank(2 * c + k), lambda d: w[:, d, c * P:(c + 1) * P], lambda d: xT[1][:, d, :]).then_inc(sem("qk1_ps"), 1)
                for i in range(TT):
                    dense(bank(4 + i // 2)[:, D * (i % 2):D * (i % 2) + D], tile_of(3, i), lambda d: wv1[:, d, :]).then_inc(sem("v1_ps"), 1)
                for c in range(DC):
                    for k in range(KT):
                        mm = pe.transpose(bank(6 + c).bitcast(BF16)[:, k * P:(k + 1) * P], ivT[:, c, k * P:(k + 1) * P], ident_b[:])
                    mm.then_inc(sem("iv_ps"), 1)
                units = TT * H1 // HU

                def scores(u):
                    i, g8 = divmod(u, H1 // HU)
                    c, g = divmod(g8, UC)
                    rows = slice(g * HU * DH1, (g + 1) * HU * DH1)
                    if u >= 2:
                        pe.wait_ge(sem("p1_ready"), u - 1)
                    nk = 1 + i % 2
                    for b in range(nk):
                        kt = i - nk + 1 + b
                        dst = unit_s1(u)[:, b]
                        pe.matmul(dst, qT1[rows, c, i * P:(i + 1) * P], kT1[rows, c, :, kt * P:(kt + 1) * P], start=True, stop=False)
                        mm = pe.matmul(dst, ident_b[:], (win_own if kt == i else win_prev)[:], start=False, stop=True)
                    mm.then_inc(sem("s1_ps"), 1)

                def turn(u):
                    i, g8 = divmod(u, H1 // HU)
                    nk = 1 + i % 2
                    pe.wait_ge(sem("p1_ready"), u + 1)
                    if u:
                        pe.wait_ge(sem("pT1_ready"), u)
                    for j in range(HU):
                        for b in range(nk):
                            at = (2 * j + b) * P
                            mm = pe.transpose(bank(4, 2)[:, at:at + P], unit_p1(u)[:, j, b, :], ident[:])
                    mm.then_inc(sem("pT1_ps"), 1)

                def apply(u):
                    i, g8 = divmod(u, H1 // HU)
                    nk = 1 + i % 2
                    pe.wait_ge(sem("pT1_ready"), u + 1)
                    if g8 == 0 and u:
                        pe.wait_ge(sem("sums1_out"), i)
                    if u == 0:
                        pe.wait_ge(sem("ivtok_ready"), DC)
                    g = g8 % UC
                    dst = bank(6)[g * HU * DH1:(g + 1) * HU * DH1, g8 // UC * P:(g8 // UC + 1) * P]
                    for j in range(HU):
                        for b in range(nk):
                            kt = i - nk + 1 + b
                            mm = pe.matmul(dst, v1[:, (kt * (H1 // HU) + g8) * HU + j, :], unit_pT1(u)[:, j, b, :],
                                           start=j == 0 and b == 0, stop=j == HU - 1 and b == nk - 1)
                    mm.then_inc(sem("o1_ps"), 1)

                def turn_z(i):
                    pe.wait_ge(sem("rz1_ready"), i + 1)
                    if i:
                        pe.wait_ge(sem("res4_ready"), i)
                    pe.transpose(bank(7)[0:H1, 0:P], rz1[:, i, :], ident[:]).then_inc(sem("rzT1_ps"), 1)

                def spread_z(i):
                    pe.wait_ge(sem("rzT1_ready"), i + 1)
                    for c in range(DC):
                        mm = pe.matmul(bank(7)[:, (1 + c) * P:(2 + c) * P], head_rows[:, c * P:(c + 1) * P], rzT1,
                                       start=True, stop=True)
                    mm.then_inc(sem("zf1_ps"), 1)

                def project(i):
                    pe.wait_ge(sem("att1_ready"), i + 1)
                    dense(bank(7)[:, 0:D], lambda c: attT1[:, i % 2, c, :], lambda c: wo1[:, c, :]).then_inc(sem("proj4"), 1)

                pe.wait_ge(sem("qT1_ready"), DC)
                pe.wait_ge(sem("kT1_ready"), DC)
                pe.wait_ge(sem("v1_ready"), TT // 2)
                per = H1 // HU
                scores(0)
                for u in range(units + 1):
                    if u + 1 < units:
                        scores(u + 1)
                    if u < units:
                        turn(u)
                    if u % per == 1 and u > per:
                        turn_z(u // per - 1)
                    if u % per == 2 and u > per:
                        spread_z(u // per - 1)
                    if u % per == 4 and u > per:
                        project(u // per - 1)
                    if u:
                        apply(u - 1)
                turn_z(TT - 1)
                spread_z(TT - 1)
                project(TT - 1)

            def stage5():
                pe.wait_ge(sem("in_stage5"), 4 * 16)
                pe.wait_ge(sem("xT_ready4"), TT)
                for i in range(TT):
                    dense(bank(i // 2)[:, D * (i % 2):D * (i % 2) + D], tile_of(4, i), lambda d: wqx[:, d, :]).then_inc(sem("qx_ps"), 1)
                pe.wait_ge(sem("qstack_ready"), 1)
                for c in range(HX // 2):
                    if c >= 2:
                        pe.wait_ge(sem("qTx_ready"), c - 1)
                    for i in range(TT):
                        mm = pe.transpose(bank(6 + c % 2).bitcast(BF16)[:, i * P:(i + 1) * P],
                                          qstack[:, i, c * P:(c + 1) * P], ident_b[:])
                    mm.then_inc(sem("qTx_ps"), 1)
                pe.wait_ge(sem("qTx_ready"), HX // 2)
                pe.wait_ge(sem("kTx_ready"), KT)
                pe.wait_ge(sem("qx_ready"), TT // 2)
                units = TT * HX

                def scores(u):
                    i, h = divmod(u, HX)
                    if u >= 2:
                        pe.wait_ge(sem("maxx_ready"), u - 1)
                    rows = slice(KW * (h % 2), KW * (h % 2 + 1))
                    for half in range(2):
                        mm = pe.matmul(bank(2 * (u % 2) + half), qTx[rows, h // 2, i * P:(i + 1) * P],
                                       kTx[rows, h // 2, half * 512:(half + 1) * 512], start=True, stop=True)
                    mm.then_inc(sem("sx_ps"), 1)

                def turn(u):
                    pe.wait_ge(sem("px_ready"), u + 1)
                    if u >= 2:
                        pTx_ready(pe, u - 2)
                    for k in range(KT):
                        mm = pe.transpose(bank(4 + u % 2).bitcast(BF16)[:, k * P:(k + 1) * P],
                                          px[:, u % PX, k * P:(k + 1) * P].bitcast(BF16), ident_b[:])
                    mm.then_inc(sem("pTx_ps"), 1)

                def apply(u):
                    i, h = divmod(u, HX)
                    pTx_ready(pe, u)
                    c, pair = divmod(h // 2, P // PAIR)
                    dst = bank(6 + i % 2)[pair * PAIR:(pair + 1) * PAIR, c * P:(c + 1) * P]
                    for k in range(KT):
                        mm = pe.matmul(dst, ivh[:, k * HX + h, :], pTx[:, u % 2, k * P:(k + 1) * P],
                                       start=h % 2 == 0 and k == 0, stop=h % 2 == 1 and k == KT - 1)
                    mm.then_inc(sem("ox_ps"), 1)

                def turn_z(i):
                    pe.wait_ge(sem("rzx_ready"), i + 1)
                    pe.wait_ge(sem("sumsx_out"), i + 1)
                    pe.transpose(bank(6 + i % 2)[0:HX, 0:P], rzx[:, i, :], ident[:]).then_inc(sem("rzTx_ps"), 1)

                def spread_z(i):
                    pe.wait_ge(sem("rzTx_ready"), i + 1)
                    for c in range(DC):
                        mm = pe.matmul(bank(6 + i % 2)[:, D + c * P:D + (c + 1) * P], pair_rows[:, c * P:(c + 1) * P], rzTx[:],
                                       start=True, stop=True)
                    mm.then_inc(sem("zfx_ps"), 1)

                def project(i):
                    pe.wait_ge(sem("attx_ready"), i + 1)
                    dense(bank(6 + i % 2)[:, 0:D], lambda c: attTx[:, i % 2, c, :], lambda c: wpx[:, c, :]).then_inc(sem("proj5"), 1)

                pe.wait_ge(sem("in_stage5"), 4 * 16)
                for u in range(3):
                    scores(u)
                for u in range(units + 1):
                    if u + 3 < units:
                        scores(u + 3)
                    if u < units:
                        turn(u)
                    if u > HX and u % HX == 3:
                        turn_z(u // HX - 1)
                    if u > HX and u % HX == 5:
                        spread_z(u // HX - 1)
                    if u > HX and u % HX == 7:
                        project(u // HX - 1)
                    if u % HX == 1 and u > 2 * HX:
                        pe.wait_ge(sem("res5_ready"), u // HX - 1)
                    if u:
                        apply(u - 1)
                turn_z(TT - 1)
                spread_z(TT - 1)
                project(TT - 1)

            def stage6():
                pe.wait_ge(sem("in_stage6"), 3 * 16)
                for i in range(TT):
                    pe.wait_ge(sem("xT_ready5"), i + 1)
                    mm = dense(bank(0)[:, E1 * i:E1 * (i + 1)], tile_of(5, i), lambda c: w_router1[:, c, :])
                mm.then_inc(sem("score1_ps"), 1)
                pe.wait_ge(sem("picked_ready"), TT)
                for i in range(TT):
                    for k in range(i + 1):
                        mm = pe.matmul(bank(1)[:, E1 * i:E1 * (i + 1)], (tri_b if k == i else ones_b)[:], picked_b[:, k, :],
                                       start=k == 0, stop=k == i)
                mm.then_inc(sem("count_ps"), 1)
                pe.wait_ge(sem("gate1_ready"), 1)
                for i in range(TT):
                    mm = pe.transpose(bank(5)[0:E1, i * P:(i + 1) * P], gate1[:, i, :], ident[:])
                mm.then_inc(sem("gate1T_ps"), 1)
                pe.wait_ge(sem("in_w_up"), 16)
                pe.wait_ge(sem("gate1T_ready"), 1)

                def up(g):
                    if g >= 2:
                        pe.wait_ge(sem("hidden_ready"), g - 1)
                    xs = lambda c: xT[1][:, c, :]
                    if g < NG:
                        rows = slice(P * g, P * (g + 1))
                        dense(bank(g % 2), lambda c: w_up[:, c, 0, rows], xs)
                        dense(bank(2 + g % 2), lambda c: w_up[:, c, 1, rows], xs)
                        mm = pe.matmul(bank(4 + g % 2), spread[:, g * P:(g + 1) * P], gate1T, start=True, stop=True)
                    else:
                        dense(bank(g % 2)[0:HS, :], lambda c: w_su[:, c, HS:2 * HS], xs)
                        mm = dense(bank(2 + g % 2)[0:HS, :], lambda c: w_su[:, c, 0:HS], xs)
                    mm.then_inc(sem("up_ps"), 1)

                def down(g):
                    pe.wait_ge(sem("hidden_ready"), g + 1)
                    for i in range(TT):
                        tile = slice(i * P, (i + 1) * P)
                        if g < NG:
                            mm = pe.matmul(proj(i), hidden[:, g % 2, tile], w_down[:, g, :],
                                           start=g == 0 and i % 2 == 0, stop=False, skip_group_check=True)
                        else:
                            mm = pe.matmul(proj(i), shared[:, tile], w_sd[:], start=False, stop=True, skip_group_check=True)
                            mm.then_inc(sem("proj6"), 1)
                    if g < NG:
                        mm.then_inc(sem("hidden_used"), 1)

                up(0)
                for g in range(NG + 1):
                    if g < NG:
                        up(g + 1)
                    if g == 0:
                        pe.wait_ge(sem("in_w_down"), 16)
                    down(g)

            unit = [None, None, stage2, stage3, stage4, stage5, stage6]
            for n in range(1, STAGES + 1):
                if n > 1:
                    unit[n]()
                if n < STAGES:
                    transpose_x(n)

        @block.vector
        def _(dve):
            link = linker(dve, "dve_chain")
            TS, TTN, STT = dve.tensor_scalar, dve.tensor_tensor, dve.scalar_tensor_tensor

            dve.wait_ge(sem("in_mix"), 16)
            dve.tensor_reduce(mix_z[:, 0:1], mix, AX.X, ALU.max, negate=True).then_inc(sem("mixmax_ready"), 1)
            dve.wait_ge(sem("in_idx_col"), 16)
            link(TS(idx_col[:], idx_col[:], D.bit_length() - 1, None, ALU.logical_shift_right))
            link(dve.tensor_copy(row_id, idx_col[:]))
            dve.wait_ge(sem("const_ready"), 1)
            for j in range(SJ):
                TS(row_hot[:, j, :], iota_row[:], row_id[:, j:j + 1], None, ALU.is_equal)
            dve.wait_ge(sem("mixexp_ready"), 1)
            link(dve.reciprocal(mix_z[:, 2:3], mix_z[:, 1:2]))
            TS(mix, mix, mix_z[:, 2:3], None, ALU.mult).then_inc(sem("mix_ready"), 1)

            def late_constants():
                dve.wait_ge(sem("in_idx_row"), 16)
                link(TS(idx_row, idx_row, D - 1, None, ALU.bitwise_and))
                for c in range(DC):
                    TS(col_hot[:, c, :], idx_row, part_id[:, c:c + 1], None, ALU.is_equal)
                dve.wait_ge(sem("imp_ready"), 1)
                for k in range(NS // 512):
                    dve.wait_ge(sem("delta_ps"), k + 1)
                    w = weighted[:, 512 * k:512 * (k + 1)]
                    TTN(out=w, in0=bank(k)[0:E0, :], in1=w, op=ALU.mult).then_inc(sem("weighted_ready"), 1)
                dve.wait_ge(sem("in_mask"), 16)
                link(TS(mask_add[:], mask_u8[:], 1.0, None, ALU.min))
                link(dve.tensor_reduce(valid[:], mask_add[:], AX.X, ALU.max))
                link(TS(mask_add[:], mask_add[:], -1.0, -16 * MASKED, ALU.add, ALU.mult))
                link(dve.tensor_reduce(head_sel[:], head_of[:].rearrange("p g j -> p j g"), AX.X, ALU.add))
                dve.sem_inc(sem("head_sel_ready"), 1)

            for c in range(DC):
                dve.wait_ge(sem("exp_ready"), 2 * c + 1)
                link(STT(out=phi_k, in0=exp_kq[:, 0, :], scalar=1.0, in1=relu_kq[:, 0, :], op0=ALU.min, op1=ALU.add))
                link(TTN(out=kv, in0=phi_k, in1=bank(3 * c + 1), op=ALU.mult))
                if c:
                    dve.wait_ge(sem("num_ready"), c)
                dve.tensor_tensor_scan(kv_sum, keep_state[:], kv, 0.0, ALU.mult, ALU.add)
                link(dve.tensor_tensor_scan(k_sum, keep_state[:], phi_k, 0.0, ALU.mult, ALU.add))
                dve.wait_ge(sem("exp_ready"), 2 * c + 2)
                STT(out=phi_q, in0=exp_kq[:, 1, :], scalar=1.0, in1=relu_kq[:, 1, :], op0=ALU.min,
                    op1=ALU.add).then_inc(sem("phi_ready"), 1)
                dve.wait_ge(sem("phi_ready"), c + 1)
                dve.sem_inc(sem("sums_ready"), 1)
                link(TTN(out=den, in0=phi_q, in1=k_sum, op=ALU.mult))
                link(TS(den, den, EPS_LIN, None, ALU.add))
                link(dve.reciprocal(den, den))
                dve.wait_ge(sem("num_ready"), c + 1)
                TTN(out=lin[:, c, :], in0=num, in1=den, op=ALU.mult).then_inc(sem("lin_ready"), 1)
            late_constants()

            def norm_stats(n, i):
                link(dve.bn_stats(stats[:, i, :], res[:, i, :]))
                dve.bn_aggr(meanvar[:, i, :], stats[:, i, :]).then_inc(sem(f"var_ready{n}"), 1)

            def norm_scale(n, i):
                dve.wait_ge(sem(f"rstd_ready{n}"), i + 1)
                TS(x_tok[n % 2][:, i, :], res[:, i, :], meanvar[:, i, 0:1], rstd[:, i:i + 1],
                   ALU.subtract, ALU.mult).then_inc(sem(f"x_ready{n}"), 1)

            def norm(n, residual):
                for i in range(TT):
                    residual(i)
                    norm_stats(n, i)
                    if i:
                        norm_scale(n, i - 1)
                norm_scale(n, TT - 1)

            def projected(n, i):
                dve.wait_ge(sem(f"proj{n}"), 2 * (i // 2) + 2)

            def residual1(i):
                projected(1, i)
                dve.wait_ge(sem("in_x"), 16)
                link(STT(out=res[:, i, :], in0=proj(i), scalar=16 ** -0.5, in1=x_tok[0][:, i, :], op0=ALU.mult, op1=ALU.add))

            def stage2():
                for i in range(TT):
                    dve.wait_ge(sem("s2_ps"), i + 1)
                    link(dve.tensor_tensor_reduce(s2[:, i, :], bank(i), mask_add[:, i // (TT // B), :], 1.0, LOWEST,
                                                  ALU.add, ALU.max, mx2[:, i:i + 1]))
                    TS(nb2[:, i:i + 1], mx2[:, i:i + 1], -1.0 / 16, None, ALU.mult).then_inc(sem("nb2_ready"), 1)
                for i in range(TT):
                    dve.wait_ge(sem("p2_ready"), i + 1)
                    link(dve.reciprocal(rz2[:, i:i + 1], z2[:, i:i + 1]))
                    link(TS(rz2[:, i:i + 1], rz2[:, i:i + 1], valid[:, i // (TT // B):i // (TT // B) + 1], None, ALU.mult))

            def residual2(i):
                projected(2, i)
                link(STT(out=res[:, i, :], in0=proj(i), scalar=rz2[:, i:i + 1], in1=x_tok[1][:, i, :], op0=ALU.mult, op1=ALU.add))

            def residual(n):
                def add(i):
                    projected(n, i)
                    link(TTN(out=res[:, i, :], in0=proj(i), in1=x_tok[(n - 1) % 2][:, i, :], op=ALU.add))
                return add

            def stage3():
                dve.wait_ge(sem("logit0_ps"), 1)
                link(TS(logit0.rearrange("p i e -> p (i e)"), bank(0)[:, 0:TT * E0], -50.0, 50.0, ALU.max, ALU.min))
                for i in range(TT):
                    link(dve.max(top0[:, i, :], logit0[:, i, :]))
                for i in range(TT):
                    link(dve.max_index(idx0[:, i, :], top0[:, i, :], logit0[:, i, :]))
                TTN(out=gap0, in0=top0[:, :, 1], in1=top0[:, :, 0], op=ALU.subtract).then_inc(sem("gap0_ready"), 1)
                link(dve.tensor_copy(idx0f, idx0))
                ids = iota_row[:, 0:E0].unsqueeze(1).broadcast_to([P, TT, E0])
                for k, hot_k in ((0, hot0), (1, hot1)):
                    link(TTN(out=hot_k, in0=idx0f[:, :, k:k + 1].broadcast_to([P, TT, E0]), in1=ids, op=ALU.is_equal))
                dve.wait_ge(sem("exp0_ready"), 1)
                link(TS(w10, exp0, 1.0, None, ALU.add))
                link(dve.reciprocal(w10, w10))
                link(TTN(out=w20, in0=w10, in1=exp0, op=ALU.mult))
                for hot_k, w in ((hot0, w10), (hot1, w20)):
                    link(TTN(out=hot_k, in0=hot_k, in1=w.unsqueeze(2).broadcast_to([P, TT, E0]), op=ALU.mult))
                TTN(out=gate0, in0=hot0, in1=hot1, op=ALU.add).then_inc(sem("gate0_ready"), 1)

                def quantise(am, sc, rs):
                    link(TS(sc, am, 1.0 / 127, 1e-8, ALU.mult, ALU.max))
                    link(dve.reciprocal(rs, sc))

                def quantise_keys(k):
                    z = kx[:, k, :]
                    heads = z.rearrange("p (h d) -> p h d", h=HX)
                    dve.wait_ge(sem("kx_out"), k + 1)
                    link(TTN(out=z, in0=z, in1=bkx[:], op=ALU.add))
                    link(dve.tensor_reduce(kam[:, k, :], heads, AX.X, ALU.max, apply_absolute_value=True))
                    quantise(kam[:, k, :], ksc[:, k, :], krs[:, k, :])
                    if k >= 2:
                        dve.wait_ge(sem("ks_ready"), k - 1)
                    r = kr[:, k % 2, :]
                    link(TTN(out=r.rearrange("p (h d) -> p h d", h=HX), in0=heads,
                             in1=krs[:, k, :].unsqueeze(2).broadcast_to([P, HX, DHX]), op=ALU.mult))
                    link(TS(r, r, ROUND, ROUND, ALU.add, ALU.subtract))
                    TS(r, r, 127.0, -127.0, ALU.min, ALU.max).then_inc(sem("kr_ready"), 1)

                def quantise_values(c):
                    dve.wait_ge(sem("vTx_ready"), B * (c + 1))
                    link(dve.tensor_reduce(vam[:, c:c + 1], vTx[:, c, :], AX.X, ALU.max, apply_absolute_value=True))
                    quantise(vam[:, c:c + 1], vsc[:, c:c + 1], vrs[:, c:c + 1])
                    link(TS(vr, vTx[:, c, :], vrs[:, c:c + 1], ROUND, ALU.mult, ALU.add))
                    link(TS(vr, vr, ROUND, 127.0, ALU.subtract, ALU.min))
                    link(TS(ivT[:, c, :], vr, -127.0, None, ALU.max))

                quantise_keys(0)
                for j in range(SJ):
                    dve.wait_ge(sem("vals_ready"), j + 1)
                    if j >= 2:
                        dve.wait_ge(sem("prod_used"), j - 1)
                    TTN(out=prod[:, j % 2, :], in0=bank(2 if j % 2 else 1), in1=vals[:, j % 2, :],
                        op=ALU.mult).then_inc(sem("prod_ready"), 1)
                    if j % 2 == 0 and j // 2 + 1 < KT:
                        quantise_keys(j // 2 + 1)
                    if j in VALUES_AT:
                        quantise_values(VALUES_AT.index(j))

            def stage4():
                dve.wait_ge(sem("v1_cleared"), 1)
                units_v = v1.rearrange("p (t j) w -> p t j w", j=HU)
                for k in range(TT // 2):
                    dve.wait_ge(sem("v1_ps"), 2 * k + 2)
                    heads = bank(4 + k).rearrange("p (t j d) -> p t j d", j=HU, d=DH1)
                    for j in range(HU):
                        v = dve.tensor_copy(units_v[:, 2 * k * (H1 // HU):2 * (k + 1) * (H1 // HU), j, j * DH1:(j + 1) * DH1],
                                            heads[:, :, j, :])
                    v.then_inc(sem("v1_ready"), 1)

                def maxima(u):
                    nk = 1 + u // (H1 // HU) % 2
                    dve.wait_ge(sem("s1_ps"), u + 1)
                    if u >= 2:
                        dve.wait_ge(sem("p1_ready"), u - 1)
                    dve.tensor_reduce(nmx1[:, u % 2, :], unit_s1(u)[:, 0:nk].rearrange("p b j k -> p j b k"), AX.XY, ALU.max,
                                      negate=True).then_inc(sem("max1_ready"), 1)

                def evacuate(u):
                    nk = 1 + u // (H1 // HU) % 2
                    dve.wait_ge(sem("pT1_ps"), u + 1)
                    if u >= 2:
                        dve.wait_ge(sem("o1_ps"), u - 1)
                    src = bank(4, 2).rearrange("p (j b q) -> p j b q", b=2, j=HU)[:, :, 0:nk, :]
                    dve.tensor_copy(unit_pT1(u)[:, :, 0:nk, :], src).then_inc(sem("pT1_ready"), 1)

                def invert_z(i):
                    dve.wait_ge(sem("p1_ready"), H1 // HU * (i + 1))
                    dve.reciprocal(rz1[:, i, :], z1[:, i, :]).then_inc(sem("rz1_ready"), 1)

                def take_sums(i):
                    dve.wait_ge(sem("o1_ps"), H1 // HU * (i + 1))
                    dve.tensor_copy(attT1[:, i % 2].rearrange("p c q -> p (c q)"), bank(6)[:, 0:D]).then_inc(sem("sums1_out"), 1)

                def take_z(i):
                    dve.wait_ge(sem("rzT1_ps"), i + 1)
                    dve.tensor_copy(rzT1, bank(7)[0:H1, 0:P]).then_inc(sem("rzT1_ready"), 1)

                def normalise(i):
                    dve.wait_ge(sem("zf1_ps"), i + 1)
                    dve.wait_ge(sem("sums1_out"), i + 1)
                    a = attT1[:, i % 2].rearrange("p c q -> p (c q)")
                    TTN(out=a, in0=bank(7)[:, P:P + D], in1=a, op=ALU.mult).then_inc(sem("att1_ready"), 1)

                def add(i):
                    dve.wait_ge(sem("proj4"), i + 1)
                    TTN(out=res[:, i, :], in0=bank(7)[:, 0:D], in1=x_tok[1][:, i, :], op=ALU.add).then_inc(sem("res4_ready"), 1)
                    dve.wait_ge(sem("res4_ready"), i + 1)

                per = H1 // HU
                units = TT * per
                maxima(0)
                dve.wait_ge(sem("ivh_cleared"), 1)
                for c in range(DC):
                    dve.wait_ge(sem("iv_ps"), c + 1)
                    src = bank(6 + c).bitcast(BF16).rearrange("p (k g j d) -> p k g j d", k=KT, j=2, d=DHX)
                    dst = ivh.rearrange("p (k c g j) (l d) -> p k c g j l d", k=KT, c=DC, j=2, l=2)
                    for j in range(2):
                        v = dve.tensor_copy(dst[:, :, c, :, j, j, :], src[:, :, :, j, :])
                    v.then_inc(sem("ivtok_ready"), 1)
                for u in range(units):
                    i = u // per - 1
                    if i >= 0 and u % per == 1:
                        take_sums(i)
                    if i >= 0 and u % per == 2:
                        take_z(i)
                    if i >= 0 and u % per == 3:
                        normalise(i)
                    if u + 1 < units:
                        maxima(u + 1)
                    evacuate(u)
                    if i >= 0 and u % per == 0:
                        invert_z(i)
                    if i >= 0 and u % per == 5:
                        add(i)
                        norm_stats(4, i)
                    if i >= 0 and u % per == 6:
                        norm_scale(4, i)
                invert_z(TT - 1)
                take_sums(TT - 1)
                take_z(TT - 1)
                normalise(TT - 1)
                add(TT - 1)
                norm_stats(4, TT - 1)
                norm_scale(4, TT - 1)

            def stage5():
                def quantise(am, sc, rs):
                    link(TS(sc, am, 1.0 / 127, 1e-8, ALU.mult, ALU.max))
                    link(dve.reciprocal(rs, sc))

                def nearest(z):
                    link(TS(z, z, ROUND, ROUND, ALU.add, ALU.subtract))
                    link(TS(z, z, 127.0, -127.0, ALU.min, ALU.max))

                dve.wait_ge(sem("in_stage5"), 4 * 16)
                for i in range(0, TT, 2):
                    dve.wait_ge(sem("qx_ps"), i + 2)
                    TTN(out=qx[:, i:i + 2, :], in0=bank(i // 2).rearrange("p (i d) -> p i d", i=2),
                        in1=bqx[:].unsqueeze(1).broadcast_to([P, 2, D]), op=ALU.add).then_inc(sem("qx_ready"), 1)
                dve.wait_ge(sem("qx_ready"), TT // 2)
                flat = qx.rearrange("p i d -> p (i d)")
                link(TS(flat, flat, DHX ** -0.5, None, ALU.mult))
                heads = flat.rearrange("p (h d) -> p h d", d=DHX)
                qam_, qsc_, qrs_ = (z.rearrange("p i h -> p (i h)") for z in (qam, qsc, qrs))
                link(dve.tensor_reduce(qam_, heads, AX.X, ALU.max, apply_absolute_value=True))
                quantise(qam_, qsc_, qrs_)
                link(TTN(out=heads, in0=heads, in1=qrs_.unsqueeze(2).broadcast_to([P, TT * HX, DHX]), op=ALU.mult))
                nearest(flat)
                dve.wait_ge(sem("qstack_cleared"), 1)
                stack = qstack.rearrange("p i (h w) -> p (i h) w", w=KW)
                for k in range(3):
                    q = dve.tensor_copy(stack[:, :, k * DHX:(k + 1) * DHX], heads)
                q.then_inc(sem("qstack_ready"), 1)
                dve.wait_ge(sem("in_stage5"), 4 * 16)
                link(TTN(out=x_tok[0][:], in0=x_tok[0][:], in1=bpx[:].unsqueeze(1).broadcast_to([P, TT, D]), op=ALU.add))

                def maximum(u):
                    dve.wait_ge(sem("sx_ps"), u + 1)
                    if u >= 3:
                        dve.wait_ge(sem("px_ready"), u - 2)
                    dve.tensor_tensor_reduce(sx[:, u % 3, :], bank(2 * (u % 2), 2), zero[:].broadcast_to([P, B * M]),
                                             qsc[:, u // HX, u % HX:u % HX + 1], LOWEST, ALU.add, ALU.max,
                                             mxx[:, u:u + 1]).then_inc(sem("maxx_ready"), 1)

                def evacuate(u):
                    dve.wait_ge(sem("pTx_ps"), u + 1)
                    if u >= 2:
                        dve.wait_ge(sem("ox_ps"), u - 1)
                    dve.tensor_copy(pTx[:, u % 2, :], bank(4 + u % 2).bitcast(I16)).then_inc(sem("pTx_dve"), 1)

                def invert_z(i):
                    dve.wait_ge(sem("px_ready"), HX * (i + 1))
                    dve.reciprocal(rzx[:, i, :], zx[:, i, :]).then_inc(sem("rzx_ready"), 1)

                def normalise(i):
                    dve.wait_ge(sem("zfx_ps"), i + 1)
                    a = attTx[:, i % 2].rearrange("p c q -> p (c q)")
                    TTN(out=a, in0=bank(6 + i % 2)[:, D:2 * D], in1=a, op=ALU.mult).then_inc(sem("attx_ready"), 1)

                def add(i):
                    dve.wait_ge(sem("proj5"), i + 1)
                    TTN(out=res[:, i, :], in0=bank(6 + i % 2)[:, 0:D], in1=x_tok[0][:, i, :], op=ALU.add).then_inc(sem("res5_ready"), 1)
                    dve.wait_ge(sem("res5_ready"), i + 1)

                units = TT * HX
                maximum(0)
                maximum(1)
                for u in range(units):
                    if u + 2 < units:
                        maximum(u + 2)
                    if not by_scalar(u):
                        evacuate(u)
                    if u >= HX:
                        i = u // HX - 1
                        if u % HX == 1:
                            invert_z(i)
                        if u % HX == 5:
                            normalise(i)
                        if u % HX == 7:
                            add(i)
                            norm_stats(5, i)
                        if u % HX == NORM_AT:
                            norm_scale(5, i)
                invert_z(TT - 1)
                normalise(TT - 1)
                add(TT - 1)
                norm_stats(5, TT - 1)
                norm_scale(5, TT - 1)

            def stage6():
                dve.wait_ge(sem("score1_ready"), 1)
                ids = iota_row[:, 0:E1].unsqueeze(1).broadcast_to([P, TOPK, E1])
                for i in range(TT):
                    link(dve.max(top1[:, i, :], score1[:, i, :]))
                for i in range(TT):
                    link(dve.max_index(idx1[:, i, :], top1[:, i, :], score1[:, i, :]))
                link(dve.tensor_copy(idx1f, idx1))
                link(dve.tensor_reduce(sum1, top1[:, :, 0:TOPK], AX.X, ALU.add))
                link(dve.reciprocal(rsum1, sum1))
                for i in range(TT):
                    link(TTN(out=hot, in0=idx1f[:, i, 0:TOPK].unsqueeze(2).broadcast_to([P, TOPK, E1]), in1=ids, op=ALU.is_equal))
                    link(dve.tensor_reduce(picked[:, i, :], hot.rearrange("p k e -> p e k"), AX.X, ALU.add))
                    dve.tensor_copy(picked_b[:, i, :], picked[:, i, :]).then_inc(sem("picked_ready"), 1)
                link(TTN(out=gate1, in0=picked, in1=score1, op=ALU.mult))
                link(TTN(out=gate1, in0=gate1, in1=rsum1.unsqueeze(2).broadcast_to([P, TT, E1]), op=ALU.mult))
                dve.wait_ge(sem("count_ps"), 1)
                flat = gate1.rearrange("p i e -> p (i e)")
                STT(out=flat, in0=bank(1)[:, 0:TT * E1], scalar=float(CAP), in1=flat, op0=ALU.is_le, op1=ALU.mult).then_inc(sem("gate1_ready"), 1)
                for g in range(NG + 1):
                    s = g % 2
                    dve.wait_ge(sem("silu_ready"), g + 1)
                    if g < NG:
                        link(TTN(out=gated[:, s, :], in0=bank(2 + s), in1=silu[:, s, :], op=ALU.mult))
                        if g >= 2:
                            dve.wait_ge(sem("hidden_used"), g - 1)
                        TTN(out=hidden[:, s, :], in0=bank(4 + s), in1=gated[:, s, :], op=ALU.mult).then_inc(sem("hidden_ready"), 1)
                    else:
                        TTN(out=shared, in0=bank(2 + s)[0:HS, :], in1=silu[0:HS, s, :], op=ALU.mult).then_inc(sem("hidden_ready"), 1)

            work = [None, None, stage2, stage3, stage4, stage5, stage6]
            adds = [None, residual1, residual2, residual(3), None, None, residual(6)]
            for n in range(1, STAGES + 1):
                if n > 1:
                    work[n]()
                if adds[n]:
                    norm(n, adds[n])


def _layout(a):
    def rows(v, shape):
        return np.broadcast_to(v, (P,) + shape)

    x = a["x"].reshape(N, D)
    ctx = a["ctx_2048"].reshape(B * M, D)
    idx = a["L0_ffn_mask_idx"]
    return {
        "x": x, "xT": x.T, "w_qkv0": a["L0_attn_W_qkv"].T, "w_out0": a["L0_attn_W_out"].T,
        "ctx": ctx, "ctxT": ctx.T, "mask": rows(a["mask_BxS2_bk0"], (B, M)),
        "w_router0": a["L0_ffn_gate_w"].T, "w_ffn0": a["L0_ffn_W"].T, "atoms": a["L0_ffn_atoms"],
        "mix": a["L0_ffn_expert_atom_weights"], "imp": a["L0_ffn_importance"],
        "idx": idx, "idx_row": rows(idx, (NS,)),
        "wq1": a["L1_attn_Wq"].T, "wk1": a["L1_attn_Wk"].T, "wv1": a["L1_attn_Wv"].T, "wo1": a["L1_attn_Wo"].T,
        "wqx": a["L1_xattn_Wq"], "wkvx": a["L1_xattn_Wkv"], "wpx": a["L1_xattn_Wp"],
        "bqx": rows(a["L1_xattn_bq"], (D,)), "bkx": rows(a["L1_xattn_bkv"][0:D], (D,)),
        "bvx": a["L1_xattn_bkv"][D:2 * D].reshape(DC, P).T, "bpx": rows(a["L1_xattn_bp"], (D,)),
        "w_router1": a["L1_ffn_w_gate"], "w_su": a["L1_ffn_w_shared_up"], "w_sd": a["L1_ffn_w_shared_down"],
        "w_up": a["L1_ffn_w_up"].reshape(E1, DC, P, 2, HE).transpose(2, 1, 3, 0, 4).reshape(P, -1), "w_down": a["L1_ffn_w_down"].reshape(E1 * HE, D),
    }


def kernel(**inputs):
    import numpy as _np
    import concourse.bacc as _bacc
    from concourse import mybir as _mybir
    from concourse.bass_utils import run_bass_kernel_spmd as _run

    nc = _bacc.Bacc("TRN2", target_bir_lowering=False, num_devices=1)
    arrays, tensors = {}, {}
    for name, a in _layout({k: _np.asarray(v) for k, v in inputs.items()}).items():
        a = _np.ascontiguousarray(a)
        arrays[f"in_{name}_dram"] = a
        tensors[name] = nc.dram_tensor(f"in_{name}_dram", a.shape, _mybir.dt.from_np(a.dtype), kind="ExternalInput").ap()
    out = nc.dram_tensor("out_0_dram", (N, D), _mybir.dt.float32, kind="ExternalOutput").ap()
    build(nc, tensors, out)
    r = _run(nc, [arrays], core_ids=[0])
    return r.results[0]["out_0_dram"].reshape(B, S, D)
```

```python
import math
from contextlib import ExitStack

import numpy as np
import concourse.bass as bass
from concourse import mybir
from concourse.alu_op_type import AluOpType as ALU

ACT = mybir.ActivationFunctionType
AX = mybir.AxisListType
F32 = mybir.dt.float32
BF16 = mybir.dt.bfloat16
I32 = mybir.dt.int32
I16 = mybir.dt.int16
U32 = mybir.dt.uint32
U8 = mybir.dt.uint8

P = 128
B, S, D = 2, 256, 256
N = B * S
TT = N // P
DC = D // P
M = 512
MT = M // P
KT = B * MT
EPS_LN = 1e-5
EPS_LIN = 1e-9
E0, NA, NS = 8, 64, 2048
SJ = NS // P
H1, DH1 = 32, 8
HU = 4
UC = P // (HU * DH1)
HX, DHX = 16, 16
PAIR = 2 * DHX
KW = 64
E1, HE, HS, TOPK, CAP = 64, 32, 64, 6, 128
EG = P // HE
NG = E1 // EG
MASKED = -1.0e30
LOWEST = -3.0e38
ROUND = 12582912.0
STAGES = 6
PX = 3
SHARE = ((1, 3, 5), 7)
TURN_AT = 1
VALUES_AT = (5, 11)
NORM_AT = 11


def build(nc, t, out):
    with ExitStack() as ctx:
        def sb(name, shape, dt=F32):
            return ctx.enter_context(nc.sbuf_tensor(name, shape, dt))

        sems = {}

        def sem(name):
            if name not in sems:
                sems[name] = ctx.enter_context(nc.semaphore(name))
            return sems[name]

        ps = ctx.enter_context(nc.psum_tensor("ps", [P, 8 * 512], F32))

        def bank(k, n=1):
            return ps[:, 512 * k:512 * (k + n)]

        x_tok = [sb("x_even", [P, TT, D]), sb("x_odd", [P, TT, D])]
        xT = [sb("xT_even", [P, DC, N]), sb("xT_odd", [P, DC, N])]
        res = sb("res", [P, TT, D])
        stats = sb("stats", [P, TT, 6])
        meanvar = sb("meanvar", [P, TT, 2])
        var_eps = sb("var_eps", [P, TT])
        rstd = sb("rstd", [P, TT])
        minus_half = sb("minus_half", [P, TT])
        w_qkv0 = sb("w_qkv0", [P, DC, 3 * D])
        w_out0 = sb("w_out0", [P, DC, D])
        ctxT = sb("ctxT", [P, DC, B * M])
        ctx_tok = sb("ctx_tok", [P, KT, D])
        mask_u8 = sb("mask_u8", [P, B, M], U8)
        mask_add = sb("mask_add", [P, B, M])
        valid = sb("valid", [P, B])
        w_ffn0 = sb("w_ffn0", [P, DC, D])
        w_router0 = sb("w_router0", [P, DC, E0])
        wq1 = sb("wq1", [P, DC, D])
        wk1 = sb("wk1", [P, DC, D])
        wv1 = sb("wv1", [P, DC, D])
        wo1 = sb("wo1", [P, DC, D])
        wqx = sb("wqx", [P, DC, D])
        wkvx = sb("wkvx", [P, DC, 2 * D])
        wpx = sb("wpx", [P, DC, D])
        bqx = sb("bqx", [P, D])
        bkx = sb("bkx", [P, D])
        bpx = sb("bpx", [P, D])
        bvx = sb("bvx", [P, DC])
        w_router1 = sb("w_router1", [P, DC, E1])
        w_su = sb("w_su", [P, DC, 2 * HS])
        w_sd = sb("w_sd", [HS, D])
        ident = sb("ident", [P, P])
        ident_b = sb("ident_b", [P, P], BF16)
        tri_b = sb("tri_b", [P, P], BF16)
        ones_b = sb("ones_b", [P, P], BF16)
        keep_state = sb("keep_state", [P, N])
        iota_row = sb("iota_row", [P, D])
        part_id = sb("part_id", [P, DC])
        window = sb("window", [P, 2, P])
        zero = sb("zero", [P, 1])
        head_of = sb("head_of", [P, UC, HU])
        head_sel = sb("head_sel", [P, HU])
        unit_sel = sb("unit_sel", [P, UC])
        head_rows = sb("head_rows", [H1, D])
        small = sb("small", [P, 2048])

        area = {"a": sb("area_a", [P, 12288]), "b": sb("area_b", [P, 14336])}
        taken = {"small": 0}
        area["small"] = small

        def carve(where, at, shape, dt=F32, rows=P):
            words = math.prod(shape) * mybir.dt.size(dt) // 4
            assert at + words <= area[where].shape[1], (where, at, shape)
            v = area[where][0:rows, at:at + words]
            if dt != F32:
                v = v.bitcast(dt)
            if len(shape) == 2:
                v = v.rearrange("p (a b) -> p a b", a=shape[0])
            if len(shape) == 3:
                v = v.rearrange("p (a b c) -> p a b c", a=shape[0], b=shape[1])
            return v

        def tiny(shape, dt=F32):
            v = carve("small", taken["small"], shape, dt)
            taken["small"] += (math.prod(shape) * mybir.dt.size(dt) + 3) // 4
            return v

        exp_kq = carve("a", 0, [2, N])
        relu_kq = carve("a", 2 * N, [2, N])
        phi_k = carve("a", 4 * N, [N])
        kv = carve("a", 5 * N, [N])
        kv_sum = carve("a", 6 * N, [N])
        k_sum = carve("a", 7 * N, [N])
        phi_q = carve("a", 8 * N, [N])
        den = carve("a", 9 * N, [N])
        num = carve("a", 10 * N, [N])
        lin = carve("a", 11 * N, [DC, N])
        s2 = carve("a", 8 * N, [TT, M])
        p2 = carve("a", 0, [TT, M])
        pT2 = carve("a", 4 * M, [TT, MT, P])
        mx2, nb2, z2, rz2 = tiny([TT]), tiny([TT]), tiny([TT]), tiny([TT])
        atoms = carve("b", 0, [NS], rows=NA)
        idx_row = carve("b", NS, [NS], I32)
        col_hot = carve("b", 2 * NS, [DC, NS], BF16)
        x_parts = [carve("b", 3 * NS + k * DC * N // 2, [DC, N], BF16) for k in range(3)]
        x_rest = carve("a", 10 * N, [DC, N])
        row_hot = carve("b", 4 * NS, [SJ, D])
        weighted = carve("b", 4 * NS + SJ * D, [NS], rows=E0)
        idx_col = sb("idx_col", [P, SJ], I32)
        row_id = tiny([SJ])
        mix = tiny([NA])[0:E0]
        mix_z = tiny([3])[0:E0]
        mixT = tiny([E0])[0:NA]
        vals = carve("a", 0, [2, N])
        prod = carve("a", 2 * N, [2, N])
        logit0, top0 = tiny([TT, E0]), tiny([TT, 8])
        idx0, idx0f = tiny([TT, 8], U32), tiny([TT, 8])
        gap0, exp0, w20, w10 = tiny([TT]), tiny([TT]), tiny([TT]), tiny([TT])
        hot0, hot1, gate0 = tiny([TT, E0]), tiny([TT, E0]), tiny([TT, E0])
        gate0T = carve("a", 4 * N, [N], rows=E0)
        qT1 = carve("b", 20 * N, [DC * UC, N])
        kT1 = carve("a", 2 * N, [DC, HU, N])
        v1 = carve("a", 10 * N, [TT * H1 // HU * HU, HU * DH1])
        p1 = carve("a", 18 * N, [2, HU * 2 * P])
        s1 = [carve("b", 18 * N, [HU, 2 * P]), carve("a", 22 * N, [HU, 2 * P])]
        pT1 = carve("b", 8 * N, [2, HU * 2 * P])
        attT1 = carve("b", 12 * N, [2, DC, P])
        rzT1 = carve("b", 13 * N, [P], rows=H1)
        nmx1, z1, rz1 = tiny([2, HU]), tiny([TT, H1]), tiny([TT, H1])
        vTx = carve("a", 13 * N, [DC, B * M])
        kx = carve("a", 17 * N, [KT, D])
        kr = carve("a", 5 * N, [2, D])
        ks = carve("a", 6 * N, [2, D])
        kres = carve("a", 7 * N, [2, D])
        kstack = carve("a", 8 * N, [2, HX * KW], BF16)
        vr = carve("a", 10 * N, [B * M])
        ivT = carve("a", 22 * N, [DC, B * M], BF16)
        kTx = carve("b", 0, [HX // 2, B * M], BF16)
        px = carve("b", 8 * N, [PX, B * M], I16)
        ivh = carve("b", 14 * N, [KT * HX, PAIR], BF16)
        qstack = carve("a", 0, [TT, HX * KW], BF16)
        qTx = carve("b", 18 * N, [HX // 2, 2, N], BF16)
        qx = carve("a", 10 * N, [TT, D])
        pair_rows = sb("pair_rows", [HX, D])
        rzTx = sb("rzTx", [HX, P])
        attTx = sb("attTx", [P, 2, DC, P])
        kam, ksc, krs = tiny([KT, HX]), tiny([KT, HX]), tiny([KT, HX])
        vam, vsc, vrs = tiny([DC]), tiny([DC]), tiny([DC])
        qam, qsc, qrs = tiny([TT, HX]), tiny([TT, HX]), tiny([TT, HX])
        mxx, nbx = tiny([TT * HX]), tiny([TT * HX])
        zx, rzx = tiny([TT, HX]), tiny([TT, HX])
        sx = carve("a", DC * E1 * 2 * HE, [3, B * M])
        pTx = carve("a", DC * E1 * 2 * HE + 3 * B * M, [2, KT * P], BF16)
        w_up = carve("a", 0, [DC, 2, E1 * HE])
        w_down = carve("a", DC * E1 * 2 * HE, [NG, D])
        spread = sb("spread", [2 * E1, NG * P], BF16)
        gate1T = carve("b", 0, [N], rows=E1)
        silu = carve("b", N, [2, N])
        gated = carve("b", 3 * N, [2, N])
        hidden = carve("b", 5 * N, [2, N])
        shared = carve("b", 7 * N, [N], rows=HS)
        score1 = carve("b", 8 * N, [TT, E1])
        hot = carve("b", 8 * N + TT * E1, [TOPK, E1])
        picked = carve("b", 8 * N + TT * E1 + TOPK * E1, [TT, E1])
        picked_b = carve("b", 8 * N + 2 * TT * E1 + TOPK * E1, [TT, E1], BF16)
        gate1 = carve("b", 8 * N + 3 * TT * E1 + TOPK * E1, [TT, E1])
        base = 8 * N + 4 * TT * E1 + TOPK * E1
        gate1S, gate1L = carve("b", base, [N], BF16), carve("b", base + N // 2, [N], BF16, rows=E1)
        silu_shared = carve("b", base + N, [N], rows=HS)
        top1, idx1, idx1f = tiny([TT, 8]), tiny([TT, 8], U32), tiny([TT, 8])
        sum1, rsum1 = tiny([TT]), tiny([TT])

        def proj(i):
            return bank(6 + i // 2)[:, D * (i % 2):D * (i % 2) + D]

        def nth(n, i):
            return TT * (n - 1) + i + 1

        def by_scalar(u):
            return u % SHARE[1] in SHARE[0]

        def pTx_ready(eng, u):
            by_act = by_scalar(u)
            eng.wait_ge(sem("pTx_act" if by_act else "pTx_dve"), sum(by_scalar(k) == by_act for k in range(u + 1)))

        def unit_s1(u):
            return bank(2 * (u % 2), 2).rearrange("p (b j k) -> p b j k", b=2, j=HU)

        def unit_p1(u):
            return p1[:, u % 2].rearrange("p (j b k) -> p j b k", b=2, j=HU)

        def unit_pT1(u):
            return pT1[:, u % 2].rearrange("p (j b q) -> p j b q", b=2, j=HU)

        block = ctx.enter_context(nc.Block())

        def linker(eng, name):
            count = [0]

            def link(ins):
                count[0] += 1
                ins.then_inc(sem(name), 1)
                eng.wait_ge(sem(name), count[0])
            return link

        @block.sync
        def _(sp):
            def load(name, dst, src, of=None):
                sp.dma_start(dst, src).then_inc(sem("in_" + (of or name)), 16)

            two = "(c p) n -> p c n"
            load("xT", xT[0][:], t["xT"].rearrange(two, p=P))
            load("w_qkv0", w_qkv0[:], t["w_qkv0"].rearrange(two, p=P))
            load("mix", mix, t["mix"])
            load("imp", weighted, t["imp"])
            load("idx_col", idx_col[:], t["idx"].rearrange("(p j) -> p j", j=SJ))
            load("idx_row", idx_row, t["idx_row"])
            load("mask", mask_u8[:], t["mask"])
            load("ctxT", ctxT[:], t["ctxT"].rearrange(two, p=P))
            load("wkvx", wkvx[:], t["wkvx"].rearrange(two, p=P), of="keys")
            load("bkx", bkx[:], t["bkx"], of="keys")
            load("bvx", bvx[:], t["bvx"], of="keys")
            load("atoms", atoms, t["atoms"])
            load("x", x_tok[0][:], t["x"].rearrange("(i p) d -> p i d", p=P))
            load("w_out0", w_out0[:], t["w_out0"].rearrange(two, p=P))
            load("ctx", ctx_tok[:], t["ctx"].rearrange("(k p) d -> p k d", p=P))
            load("w_router0", w_router0[:], t["w_router0"].rearrange(two, p=P))
            load("w_ffn0", w_ffn0[:], t["w_ffn0"].rearrange(two, p=P))
            load("wq1", wq1[:], t["wq1"].rearrange(two, p=P), of="stage4")
            load("wk1", wk1[:], t["wk1"].rearrange(two, p=P), of="stage4")
            load("wv1", wv1[:], t["wv1"].rearrange(two, p=P), of="stage4")
            load("wo1", wo1[:], t["wo1"].rearrange(two, p=P), of="stage4")
            load("wqx", wqx[:], t["wqx"].rearrange(two, p=P), of="stage5")
            load("wpx", wpx[:], t["wpx"].rearrange(two, p=P), of="stage5")
            load("bqx", bqx[:], t["bqx"], of="stage5")
            load("bpx", bpx[:], t["bpx"], of="stage5")
            load("w_router1", w_router1[:], t["w_router1"].rearrange(two, p=P), of="stage6")
            load("w_su", w_su[:], t["w_su"].rearrange(two, p=P), of="stage6")
            load("w_sd", w_sd[:], t["w_sd"], of="stage6")
            if STAGES >= 6:
                sp.wait_ge(sem("qTx_ps"), HX // 2)
                load("w_up", w_up.rearrange("p c k h -> p (c k h)"), t["w_up"])
                sp.wait_ge(sem("px_ready"), TT * HX)
                sp.wait_ge(sem("ox_ps"), TT * HX)
                load("w_down", w_down, t["w_down"].rearrange("(g p) d -> p g d", p=P))
            for i in range(TT):
                sp.wait_ge(sem(f"x_ready{STAGES}"), i + 1)
                sp.dma_start(out[i * P:(i + 1) * P, :], x_tok[STAGES % 2][:, i, :]).then_inc(sem("out_done"), 16)
            sp.wait_ge(sem("out_done"), 16 * TT)

        @block.gpsimd
        def _(pool):
            link = linker(pool, "pool_chain")

            def select(buf, pattern, base, mult, op, fill):
                return pool.affine_select(out=buf, in_=buf, compare_op=op, fill=fill, base=base,
                                          pattern=pattern, channel_multiplier=mult)

            pool.iota(part_id[:], [[P, DC]], base=0, channel_multiplier=1, allow_small_or_imprecise_dtypes=True)
            pool.memset(minus_half[:], -0.5)
            pool.memset(keep_state[:], 1.0)
            link(pool.memset(ident[:], 0.0))
            pool.memset(keep_state[:, S:S + 1], 0.0)
            link(select(ident[:], [[-1, P]], 0, 1, ALU.not_equal, 1.0))
            link(pool.iota(iota_row[:], [[1, D]], base=0, channel_multiplier=0, allow_small_or_imprecise_dtypes=True))
            pool.sem_inc(sem("first_const_ready"), 1)
            pool.memset(zero[:], 0.0)
            pool.memset(ident_b[:], 0.0)
            pool.memset(tri_b[:], 1.0)
            pool.memset(ones_b[:], 1.0)
            pool.memset(window[:], 0.0)
            pool.memset(head_of[:], 1.0)
            pool.memset(head_rows[:], 1.0)
            pool.memset(pair_rows[:], 1.0)
            link(pool.memset(spread[:], 1.0))
            link(select(ident_b[:], [[-1, P]], 0, 1, ALU.not_equal, 1.0))
            link(select(tri_b[:], [[1, P]], 0, -1, ALU.is_ge, 0.0))
            link(select(window[:, 1, :], [[-1, P]], 0, 1, ALU.is_ge, MASKED))
            link(select(window[:, 0, :], [[1, P]], 0, -1, ALU.is_ge, MASKED))
            span = [[-HU * DH1, UC], [-DH1, HU]]
            link(select(head_of[:], span, 0, 1, ALU.is_ge, 0.0))
            link(select(head_of[:], [[HU * DH1, UC], [DH1, HU]], DH1 - 1, -1, ALU.is_ge, 0.0))
            link(select(head_rows[:], [[1, D]], 0, -DH1, ALU.is_ge, 0.0))
            link(select(head_rows[:], [[-1, D]], DH1 - 1, DH1, ALU.is_ge, 0.0))
            link(select(pair_rows[:], [[1, D]], 0, -DHX, ALU.is_ge, 0.0))
            link(select(pair_rows[:], [[-1, D]], DHX - 1, DHX, ALU.is_ge, 0.0))
            for half in (spread[0:E1, :], spread[E1:2 * E1, :]):
                link(select(half, [[1, NG * P]], 0, -HE, ALU.is_ge, 0.0))
                link(select(half, [[-1, NG * P]], HE - 1, HE, ALU.is_ge, 0.0))
            pool.sem_inc(sem("const_ready"), 1)

            def linear_numerator(c):
                pool.wait_ge(sem("sums_ready"), c + 1)
                if c:
                    pool.wait_ge(sem("lin_ready"), c)
                pool.tensor_tensor(out=num, in0=phi_q, in1=kv_sum, op=ALU.mult).then_inc(sem("num_ready"), 1)

            def inverse_deviation(n, i):
                pool.wait_ge(sem("var_ready"), nth(n, i))
                link(pool.tensor_scalar(var_eps[:, i:i + 1], meanvar[:, i, 1:2], EPS_LN, None, ALU.add))
                pool.tensor_tensor(out=rstd[:, i:i + 1], in0=var_eps[:, i:i + 1], in1=minus_half[:, i:i + 1],
                                   op=ALU.pow).then_inc(sem("rstd_ready"), 1)

            pool.wait_ge(sem("row_id_ready"), 1)
            for c in range(DC):
                linear_numerator(c)
                for j in range(c * SJ // DC, (c + 1) * SJ // DC):
                    o = pool.tensor_scalar(row_hot[:, j, :], iota_row[:], row_id[:, j:j + 1], None, ALU.is_equal)
                o.then_inc(sem("row_hot_ready"), 1)

            def stack_keys(k):
                s = k % 2
                pool.wait_ge(sem("kr_ready"), k + 1)
                z = ks[:, s, :].rearrange("p (h d) -> p h d", h=HX)
                r = kr[:, s, :].rearrange("p (h d) -> p h d", h=HX)
                rest = kres[:, s, :].rearrange("p (h d) -> p h d", h=HX)
                part = kstack[:, s, :].rearrange("p (h w) -> p h w", h=HX)
                scale = ksc[:, k, :].unsqueeze(2).broadcast_to([P, HX, DHX])
                pool.tensor_tensor(out=z, in0=r, in1=scale, op=ALU.mult).then_inc(sem("ks_ready"), 1)
                pool.wait_ge(sem("ks_ready"), k + 1)
                if k >= 2:
                    pool.wait_ge(sem("kTx_ps"), k - 1)
                link(pool.tensor_copy(part[:, :, 0:DHX], z))
                link(pool.tensor_tensor(out=rest, in0=z, in1=part[:, :, 0:DHX], op=ALU.subtract))
                link(pool.tensor_copy(part[:, :, DHX:2 * DHX], rest))
                pool.tensor_tensor(out=part[:, :, 2 * DHX:3 * DHX], in0=rest, in1=part[:, :, DHX:2 * DHX],
                                   op=ALU.subtract).then_inc(sem("kstack_ready"), 1)

            for n in range(1, STAGES + 1):
                if n == 3:
                    pool.wait_ge(sem("x_ready2"), TT)
                    link(pool.memset(kstack, 0.0))
                    for k in range(KT):
                        stack_keys(k)
                if n == 5:
                    pool.wait_ge(sem("x_ready4"), TT)
                    pool.memset(qTx, 0.0).then_inc(sem("qTx_cleared"), 1)
                    pool.wait_ge(sem("in_stage5"), 4 * 16)
                    pool.wait_ge(sem("xT_ps"), nth(4, TT - 1))
                    pool.tensor_tensor(out=x_tok[0][:], in0=x_tok[0][:], in1=bpx[:].unsqueeze(1).broadcast_to([P, TT, D]),
                                       op=ALU.add).then_inc(sem("bias_added"), 1)
                    for u in range(TT * HX):
                        pool.wait_ge(sem("maxx_ready"), u + 1)
                        pool.tensor_scalar(nbx[:, u:u + 1], mxx[:, u:u + 1], -1.0, math.log(255.0),
                                           ALU.mult, ALU.add).then_inc(sem("biasx_ready"), 1)
                        if u > HX and u % HX == NORM_AT - 1:
                            inverse_deviation(5, u // HX - 1)
                for i in range(TT - 1 if n == 5 else 0, TT):
                    inverse_deviation(n, i)
                if n == 3 and STAGES > 3:
                    pool.wait_ge(sem("x_ready3"), TT)
                    pool.memset(v1, 0.0).then_inc(sem("v1_cleared"), 1)
                    pool.memset(ivh, 0.0).then_inc(sem("ivh_cleared"), 1)

        @block.scalar
        def _(act):
            link = linker(act, "act_chain")

            act.wait_ge(sem("in_imp"), 16)
            act.activation(weighted, weighted, ACT.Sigmoid).then_inc(sem("imp_ready"), 1)
            act.wait_ge(sem("mixmax_ready"), 1)
            act.activation(mix, mix, ACT.Exp, bias=mix_z[:, 0:1], accum_out=mix_z[:, 1:2]).then_inc(sem("mixexp_ready"), 1)

            for c in range(DC):
                act.wait_ge(sem("qkv_ps"), c + 1)
                if c:
                    act.wait_ge(sem("phi_ready"), c)
                for m, b in ((0, 3 * c), (1, 3 * c + 2)):
                    act.activation(exp_kq[:, m, :], bank(b), ACT.Exp)
                    act.activation(relu_kq[:, m, :], bank(b), ACT.Relu).then_inc(sem("exp_ready"), 1)
            act.wait_ge(sem("mixT_ps"), 1)
            act.activation(mixT, bank(7)[0:NA, 0:E0], ACT.Copy).then_inc(sem("mixT_ready"), 1)
            act.wait_ge(sem("in_keys"), 3 * 16)
            for v in range(DC * B):
                c, half = divmod(v, B)
                act.wait_ge(sem("vTx_ps"), v + 1)
                act.activation(vTx[:, c, half * M:(half + 1) * M], bank(6 + v % 2), ACT.Identity,
                               bias=bvx[:, c:c + 1]).then_inc(sem("vTx_ready"), 1)
            for k in range(KT):
                act.wait_ge(sem("kx_ps"), k + 1)
                act.activation(kx[:, k, :], bank(k % 2)[:, 0:D], ACT.Copy).then_inc(sem("kx_out"), 1)
            def to_xT(n):
                for i in range(TT):
                    act.wait_ge(sem("xT_ps"), nth(n, i))
                    slot = bank(4 + i % 2)[:, 0:D].rearrange("p (c t) -> p c t", c=DC)
                    act.activation(xT[n % 2][:, :, i * P:(i + 1) * P], slot, ACT.Copy).then_inc(sem(f"xT_ready{n}"), 1)

            def stage2():
                for i in range(TT):
                    act.wait_ge(sem("nb2_ready"), i + 1)
                    act.activation(p2[:, i, :], s2[:, i, :], ACT.Exp, bias=nb2[:, i:i + 1], scale=1.0 / 16,
                                   accum_out=z2[:, i:i + 1]).then_inc(sem("p2_ready"), 1)
                    if i:
                        evac2(i - 1)
                evac2(TT - 1)

            def evac2(i):
                act.wait_ge(sem("pT2_ps"), i + 1)
                act.activation(pT2[:, i].rearrange("p k q -> p (k q)"), bank(4 + i % 2), ACT.Copy).then_inc(sem("pT2_ready"), 1)

            def stage3():
                act.wait_ge(sem("xT_ready2"), TT)
                act.activation(x_parts[0], xT[0][:], ACT.Copy).then_inc(sem("x_high_ready"), 1)
                act.wait_ge(sem("gap0_ready"), 1)
                act.activation(exp0, gap0, ACT.Exp).then_inc(sem("exp0_ready"), 1)
                act.wait_ge(sem("gate0T_ps"), 1)
                act.activation(gate0T, bank(0)[0:E0, :], ACT.Copy).then_inc(sem("gate0T_ready"), 1)
                for j in range(SJ + 2):
                    if j < SJ:
                        act.wait_ge(sem("vals_ps"), j + 1)
                        if j >= 2:
                            act.wait_ge(sem("prod_ready"), j - 1)
                        act.activation(vals[:, j % 2, :], bank(3 + j % 2 * 2), ACT.Copy).then_inc(sem("vals_ready"), 1)
                    if j - 2 >= TURN_AT and j % 2 == TURN_AT % 2:
                        k = (j - 2 - TURN_AT) // 2
                        act.wait_ge(sem("kTx_ps"), k + 1)
                        act.activation(kTx[:, :, k * P:(k + 1) * P], bank(4).bitcast(BF16).rearrange("p (c t) -> p c t", c=HX // 2),
                                       ACT.Copy).then_inc(sem("kTx_ready"), 1)

            def stage4():
                for c in range(DC):
                    act.wait_ge(sem("qk1_ps"), 2 * c + 2)
                    act.wait_ge(sem("head_sel_ready"), 1)
                    for j in range(HU):
                        a = act.activation(kT1[:, c, j, :], bank(2 * c + 1), ACT.Copy, scale=head_sel[:, j:j + 1])
                    a.then_inc(sem("kT1_ready"), 1)
                for u in range(TT * H1 // HU):
                    i, g = divmod(u, H1 // HU)
                    nk = 1 + i % 2
                    act.wait_ge(sem("max1_ready"), u + 1)
                    if u >= 2:
                        act.wait_ge(sem("pT1_ps"), u - 1)
                    for j in range(HU):
                        a = act.activation(unit_p1(u)[:, j, 0:nk, :], s1[u % 2][:, j, 0:nk * P].rearrange("p (b k) -> p b k", b=nk),
                                           ACT.Exp, bias=nmx1[:, u % 2, j:j + 1], scale=-1.0,
                                           accum_out=z1[:, i, HU * g + j:HU * g + j + 1])
                    a.then_inc(sem("p1_ready"), 1)

            def stage5():
                act.wait_ge(sem("q_rounded"), 1)
                act.activation(qstack.rearrange("p i (h w) -> p (i h) w", w=KW)[:, :, 3 * DHX:KW],
                               qx.rearrange("p i (h d) -> p (i h) d", d=DHX), ACT.Copy).then_inc(sem("qstack_filled"), 1)
                act.wait_ge(sem("qTx_cleared"), 1)
                for c in range(HX // 2):
                    act.wait_ge(sem("qTx_ps"), c + 1)
                    act.activation(qTx[0:KW, c, 0, :], bank(6 + c % 2)[0:KW, 0:N // 2].bitcast(BF16), ACT.Copy).then_inc(sem("qTx_even"), 1)
                for u in range(TT * HX):
                    i, h = divmod(u, HX)
                    act.wait_ge(sem("biasx_ready"), u + 1)
                    if u >= PX:
                        act.wait_ge(sem("pTx_ps"), u - PX + 1)
                    act.activation(px[:, u % PX, :], sx[:, u % 3, :], ACT.Exp, bias=nbx[:, u:u + 1],
                                   accum_out=zx[:, i, h:h + 1]).then_inc(sem("px_ready"), 1)
                    if u and by_scalar(u - 1):
                        evac_px(u - 1)
                    if h == 1 and i:
                        evac_sums(i - 1)
                    if h == 4 and i:
                        evac_z(i - 1)
                if by_scalar(TT * HX - 1):
                    evac_px(TT * HX - 1)
                evac_sums(TT - 1)
                evac_z(TT - 1)

            def evac_px(u):
                act.wait_ge(sem("pTx_ps"), u + 1)
                if u >= 2:
                    act.wait_ge(sem("ox_ps"), u - 1)
                act.activation(pTx[:, u % 2, :], bank(4 + u % 2).bitcast(I16), ACT.Copy).then_inc(sem("pTx_act"), 1)

            def evac_sums(i):
                act.wait_ge(sem("ox_ps"), HX * (i + 1))
                if i >= 2:
                    act.wait_ge(sem("proj5"), i - 1)
                for c in range(DC):
                    a = act.activation(attTx[:, i % 2, c, :], bank(6 + i % 2)[:, c * P:(c + 1) * P], ACT.Copy,
                                       scale=vsc[:, c:c + 1])
                a.then_inc(sem("sumsx_out"), 1)

            def evac_z(i):
                act.wait_ge(sem("rzTx_ps"), i + 1)
                act.activation(rzTx[:], bank(6 + i % 2)[0:HX, 0:P], ACT.Copy).then_inc(sem("rzTx_ready"), 1)

            def stage6():
                act.wait_ge(sem("score1_ps"), 1)
                act.activation(score1.rearrange("p i e -> p (i e)"), bank(7)[:, 0:TT * E1], ACT.Sigmoid).then_inc(sem("score1_ready"), 1)

                def silu_of(g):
                    act.wait_ge(sem("up_ps"), g + 1)
                    if g >= 2:
                        act.wait_ge(sem("hidden_ready"), g - 1)
                    act.activation(silu[:, g % 2, :], bank(g % 2), ACT.Silu).then_inc(sem("silu_ready"), 1)

                silu_of(0)
                silu_of(1)
                act.wait_ge(sem("gate1T_ps"), 1)
                act.activation(gate1T, bank(5)[0:E1, :], ACT.Copy).then_inc(sem("gate1T_ready"), 1)
                act.wait_ge(sem("shared_ps"), 1)
                act.activation(silu_shared, bank(5)[HS:2 * HS, :], ACT.Silu).then_inc(sem("silu_shared_ready"), 1)
                for g in range(2, NG):
                    silu_of(g)

            unit = [None, None, stage2, stage3, stage4, stage5, stage6]
            for n in range(1, STAGES + 1):
                if n > 1:
                    unit[n]()
                if n < STAGES:
                    to_xT(n)

        @block.tensor
        def _(pe):
            def dense(dst, lhsT, rhs, start=True, stop=True, **kw):
                for c in range(DC):
                    mm = pe.matmul(dst, lhsT(c), rhs(c), start=start and c == 0, stop=stop and c == DC - 1, **kw)
                return mm

            pe.wait_ge(sem("in_xT"), 16)
            pe.wait_ge(sem("in_w_qkv0"), 16)
            for c in range(DC):
                for k, m in enumerate((1, 2, 0)):
                    mm = dense(bank(3 * c + k), lambda d: w_qkv0[:, d, D * m + P * c:D * m + P * (c + 1)],
                               lambda d: xT[0][:, d, :])
                mm.then_inc(sem("qkv_ps"), 1)
            pe.wait_ge(sem("first_const_ready"), 1)
            pe.wait_ge(sem("mix_ready"), 1)
            pe.transpose(bank(7)[0:NA, 0:E0], mix, ident[0:E0, 0:E0]).then_inc(sem("mixT_ps"), 1)
            pe.wait_ge(sem("in_ctxT"), 16)
            pe.wait_ge(sem("in_keys"), 3 * 16)
            for v in range(DC * B):
                c, half = divmod(v, B)
                if v == 1:
                    pe.wait_ge(sem("mixT_ready"), 1)
                if v >= 2:
                    pe.wait_ge(sem("vTx_ready"), v - 1)
                dense(bank(6 + v % 2), lambda d: wkvx[:, d, D + c * P:D + (c + 1) * P],
                      lambda d: ctxT[:, d, half * M:(half + 1) * M]).then_inc(sem("vTx_ps"), 1)
            pe.wait_ge(sem("exp_ready"), 1)
            pe.wait_ge(sem("phi_ready"), 1)

            def keys(k):
                if k >= 2:
                    pe.wait_ge(sem("kx_out"), k - 1)
                dense(bank(k % 2)[:, 0:D], lambda d: ctxT[:, d, k * P:(k + 1) * P], lambda d: wkvx[:, d, 0:D]).then_inc(sem("kx_ps"), 1)

            for k in range(KT):
                keys(k)
            pe.wait_ge(sem("vTx_ready"), DC * B)
            pe.wait_ge(sem("lin_ready"), DC)
            pe.wait_ge(sem("in_w_out0"), 16)
            for i in range(TT):
                dense(proj(i), lambda c: lin[:, c, i * P:(i + 1) * P], lambda c: w_out0[:, c, :]).then_inc(sem("proj1"), 1)

            def mix_atoms(k):
                pe.wait_ge(sem("in_atoms"), 16)
                pe.wait_ge(sem("nb2_ready"), k + 1)
                pe.matmul(bank(k)[0:E0, :], mixT, atoms[:, 512 * k:512 * (k + 1)],
                          start=True, stop=True).then_inc(sem("delta_ps"), 1)

            def transpose_x(n):
                for i in range(TT):
                    pe.wait_ge(sem(f"x_ready{n}"), i + 1)
                    if n == 3 and i == 0:
                        pe.wait_ge(sem("kTx_ready"), KT)
                    if i >= 2:
                        pe.wait_ge(sem(f"xT_ready{n}"), i - 1)
                    for c in range(DC):
                        mm = pe.transpose(bank(4 + i % 2)[:, c * P:(c + 1) * P], x_tok[n % 2][:, i, c * P:(c + 1) * P], ident[:])
                    mm.then_inc(sem("xT_ps"), 1)

            def tile_of(n, i):
                return lambda c: xT[n % 2][:, c, i * P:(i + 1) * P]

            def stage2():
                pe.wait_ge(sem("in_ctxT"), 16)
                for i in range(TT):
                    b = i // (TT // B)
                    pe.wait_ge(sem("kx_out"), KT)
                    pe.wait_ge(sem("xT_ready1"), i + 1)
                    dense(bank(i), tile_of(1, i), lambda c: ctxT[:, c, b * M:(b + 1) * M]).then_inc(sem("s2_ps"), 1)
                pe.wait_ge(sem("in_ctx"), 16)
                pe.wait_ge(sem("xT_ready1"), TT)
                for i in range(TT + 1):
                    if i < TT:
                        pe.wait_ge(sem("p2_ready"), i + 1)
                        if i >= 2:
                            pe.wait_ge(sem("pT2_ready"), i - 1)
                        for k in range(MT):
                            mm = pe.transpose(bank(4 + i % 2)[:, k * P:(k + 1) * P], p2[:, i, k * P:(k + 1) * P], ident[:])
                        mm.then_inc(sem("pT2_ps"), 1)
                    if i < NS // 512:
                        mix_atoms(i)
                    if i:
                        b = (i - 1) // (TT // B)
                        pe.wait_ge(sem("pT2_ready"), i)
                        for k in range(MT):
                            mm = pe.matmul(proj(i - 1), pT2[:, i - 1, k, :], ctx_tok[:, b * MT + k, :],
                                           start=k == 0, stop=k == MT - 1)
                        mm.then_inc(sem("proj2"), 1)

            def stage3():
                pe.wait_ge(sem("in_w_router0"), 16)
                pe.wait_ge(sem("in_w_ffn0"), 16)
                pe.wait_ge(sem("weighted_ready"), 1)
                for i in range(TT):
                    pe.wait_ge(sem("xT_ready2"), i + 1)
                    mm = dense(bank(0)[:, E0 * i:E0 * (i + 1)], tile_of(2, i), lambda c: w_router0[:, c, :])
                mm.then_inc(sem("logit0_ps"), 1)
                for i in range(TT):
                    dense(proj(i), tile_of(2, i), lambda c: w_ffn0[:, c, :], start=i % 2 == 0, stop=False,
                          skip_group_check=True)

                def gather(j):
                    if j >= 2:
                        pe.wait_ge(sem("prod_ready"), j - 1)
                    for c in range(DC):
                        for k, part in enumerate(x_parts):
                            pe.matmul(bank(2 if j % 2 else 1), col_hot[:, c, j:NS:SJ], part[:, c, :],
                                      start=c == 0 and k == 0, stop=c == DC - 1 and k == 2)

                def values(j):
                    if j >= 2:
                        pe.wait_ge(sem("vals_ready"), j - 1)
                    pe.matmul(bank(3 + j % 2 * 2), weighted[:, j:NS:SJ], gate0T, start=True, stop=True).then_inc(sem("vals_ps"), 1)

                def turn_keys(k):
                    pe.wait_ge(sem("kstack_ready"), k + 1)
                    if k:
                        pe.wait_ge(sem("kTx_ready"), k)
                    for c in range(HX // 2):
                        mm = pe.transpose(bank(4).bitcast(BF16)[:, c * P:(c + 1) * P], kstack[:, k % 2, c * P:(c + 1) * P], ident_b[:])
                    mm.then_inc(sem("kTx_ps"), 1)

                pe.wait_ge(sem("col_hot_ready"), DC)
                pe.wait_ge(sem("weighted_ready"), NS // 512)
                pe.wait_ge(sem("row_hot_ready"), DC)
                pe.wait_ge(sem("gate0_ready"), 1)
                for i in range(TT):
                    mm = pe.transpose(bank(0)[0:E0, i * P:(i + 1) * P], gate0[:, i, :], ident[:])
                mm.then_inc(sem("gate0T_ps"), 1)
                pe.wait_ge(sem("x_parts_ready"), 1)
                gather(0)
                pe.wait_ge(sem("gate0T_ready"), 1)
                values(0)
                gather(1)
                values(1)
                for j in range(SJ):
                    pe.wait_ge(sem("prod_ready"), j + 1)
                    for i in range(TT):
                        mm = pe.matmul(proj(i), prod[:, j % 2, i * P:(i + 1) * P], row_hot[:, j, :],
                                       start=False, stop=j == SJ - 1, skip_group_check=True)
                        if j == SJ - 1:
                            mm.then_inc(sem("proj3"), 1)
                    if j < SJ - 1:
                        mm.then_inc(sem("prod_used"), 1)
                    if j + 2 < SJ:
                        gather(j + 2)
                        values(j + 2)
                    if j >= TURN_AT and j % 2 == TURN_AT % 2:
                        turn_keys((j - TURN_AT) // 2)

            def stage4():
                pe.wait_ge(sem("in_stage4"), 4 * 16)
                pe.wait_ge(sem("xT_ready3"), TT)
                for c in range(DC):
                    for k, w in ((0, wq1), (1, wk1)):
                        dense(bank(2 * c + k), lambda d: w[:, d, c * P:(c + 1) * P], lambda d: xT[1][:, d, :]).then_inc(sem("qk1_ps"), 1)
                for i in range(TT):
                    dense(bank(4 + i // 2)[:, D * (i % 2):D * (i % 2) + D], tile_of(3, i), lambda d: wv1[:, d, :]).then_inc(sem("v1_ps"), 1)
                for c in range(DC):
                    for k in range(KT):
                        mm = pe.transpose(bank(6 + c).bitcast(BF16)[:, k * P:(k + 1) * P], ivT[:, c, k * P:(k + 1) * P], ident_b[:])
                    mm.then_inc(sem("iv_ps"), 1)
                units = TT * H1 // HU

                def scores(u):
                    i, g8 = divmod(u, H1 // HU)
                    if u >= 2:
                        pe.wait_ge(sem("max1_ready"), u - 1)
                    nk = 1 + i % 2
                    for b in range(nk):
                        kt = i - nk + 1 + b
                        dst = unit_s1(u)[:, b]
                        mm = pe.matmul(dst, qT1[:, g8, i * P:(i + 1) * P], kT1[:, g8 // UC, :, kt * P:(kt + 1) * P], start=True, stop=True)
                    mm.then_inc(sem("s1_ps"), 1)

                def turn(u):
                    i, g8 = divmod(u, H1 // HU)
                    nk = 1 + i % 2
                    pe.wait_ge(sem("p1_ready"), u + 1)
                    if u:
                        pe.wait_ge(sem("pT1_ready"), u)
                    for j in range(HU):
                        for b in range(nk):
                            at = (2 * j + b) * P
                            mm = pe.transpose(bank(4, 2)[:, at:at + P], unit_p1(u)[:, j, b, :], ident[:])
                    mm.then_inc(sem("pT1_ps"), 1)

                def apply(u):
                    i, g8 = divmod(u, H1 // HU)
                    nk = 1 + i % 2
                    pe.wait_ge(sem("pT1_ready"), u + 1)
                    if g8 == 0 and u:
                        pe.wait_ge(sem("sums1_out"), i)
                    if u == 0:
                        pe.wait_ge(sem("ivtok_ready"), DC)
                    g = g8 % UC
                    dst = bank(6)[g * HU * DH1:(g + 1) * HU * DH1, g8 // UC * P:(g8 // UC + 1) * P]
                    for j in range(HU):
                        for b in range(nk):
                            kt = i - nk + 1 + b
                            mm = pe.matmul(dst, v1[:, (kt * (H1 // HU) + g8) * HU + j, :], unit_pT1(u)[:, j, b, :],
                                           start=j == 0 and b == 0, stop=j == HU - 1 and b == nk - 1)
                    mm.then_inc(sem("o1_ps"), 1)

                def turn_z(i):
                    pe.wait_ge(sem("rz1_ready"), i + 1)
                    if i:
                        pe.wait_ge(sem("res4_ready"), i)
                    pe.transpose(bank(7)[0:H1, 0:P], rz1[:, i, :], ident[:]).then_inc(sem("rzT1_ps"), 1)

                def spread_z(i):
                    pe.wait_ge(sem("rzT1_ready"), i + 1)
                    for c in range(DC):
                        mm = pe.matmul(bank(7)[:, (1 + c) * P:(2 + c) * P], head_rows[:, c * P:(c + 1) * P], rzT1,
                                       start=True, stop=True)
                    mm.then_inc(sem("zf1_ps"), 1)

                def project(i):
                    pe.wait_ge(sem("att1_ready"), i + 1)
                    dense(bank(7)[:, 0:D], lambda c: attT1[:, i % 2, c, :], lambda c: wo1[:, c, :]).then_inc(sem("proj4"), 1)

                pe.wait_ge(sem("qT1_ready"), DC)
                pe.wait_ge(sem("kT1_ready"), DC)
                pe.wait_ge(sem("v1_ready"), TT // 2)
                per = H1 // HU
                scores(0)
                scores(1)
                for u in range(units + 1):
                    if u + 2 < units:
                        scores(u + 2)
                    if u < units:
                        turn(u)
                    if u % per == 1 and u > per:
                        turn_z(u // per - 1)
                    if u % per == 2 and u > per:
                        spread_z(u // per - 1)
                    if u % per == 4 and u > per:
                        project(u // per - 1)
                    if u:
                        apply(u - 1)
                turn_z(TT - 1)
                spread_z(TT - 1)
                project(TT - 1)

            def stage5():
                pe.wait_ge(sem("in_stage5"), 4 * 16)
                pe.wait_ge(sem("xT_ready4"), TT)
                for i in range(TT):
                    dense(bank(i // 2)[:, D * (i % 2):D * (i % 2) + D], tile_of(4, i), lambda d: wqx[:, d, :]).then_inc(sem("qx_ps"), 1)
                pe.wait_ge(sem("qstack_ready"), 1)
                pe.wait_ge(sem("qstack_filled"), 1)
                for c in range(HX // 2):
                    if c >= 2:
                        pe.wait_ge(sem("qTx_even"), c - 1)
                        pe.wait_ge(sem("qTx_odd"), c - 1)
                    for i in range(TT):
                        mm = pe.transpose(bank(6 + c % 2).bitcast(BF16)[:, i * P:(i + 1) * P],
                                          qstack[:, i, c * P:(c + 1) * P], ident_b[:])
                    mm.then_inc(sem("qTx_ps"), 1)
                pe.wait_ge(sem("qTx_even"), HX // 2)
                pe.wait_ge(sem("qTx_odd"), HX // 2)
                pe.wait_ge(sem("kTx_ready"), KT)
                pe.wait_ge(sem("qx_ready"), TT // 2)
                units = TT * HX

                def scores(u):
                    i, h = divmod(u, HX)
                    if u >= 2:
                        pe.wait_ge(sem("maxx_ready"), u - 1)
                    for half in range(2):
                        mm = pe.matmul(bank(2 * (u % 2) + half), qTx[:, h // 2, h % 2, i * P:(i + 1) * P],
                                       kTx[:, h // 2, half * 512:(half + 1) * 512], start=True, stop=True)
                    mm.then_inc(sem("sx_ps"), 1)

                def turn(u):
                    pe.wait_ge(sem("px_ready"), u + 1)
                    if u >= 2:
                        pTx_ready(pe, u - 2)
                    for k in range(KT):
                        mm = pe.transpose(bank(4 + u % 2).bitcast(BF16)[:, k * P:(k + 1) * P],
                                          px[:, u % PX, k * P:(k + 1) * P].bitcast(BF16), ident_b[:])
                    mm.then_inc(sem("pTx_ps"), 1)

                def apply(u):
                    i, h = divmod(u, HX)
                    pTx_ready(pe, u)
                    c, pair = divmod(h // 2, P // PAIR)
                    dst = bank(6 + i % 2)[pair * PAIR:(pair + 1) * PAIR, c * P:(c + 1) * P]
                    for k in range(KT):
                        mm = pe.matmul(dst, ivh[:, k * HX + h, :], pTx[:, u % 2, k * P:(k + 1) * P],
                                       start=h % 2 == 0 and k == 0, stop=h % 2 == 1 and k == KT - 1)
                    mm.then_inc(sem("ox_ps"), 1)

                def turn_z(i):
                    pe.wait_ge(sem("rzx_ready"), i + 1)
                    pe.wait_ge(sem("sumsx_out"), i + 1)
                    pe.transpose(bank(6 + i % 2)[0:HX, 0:P], rzx[:, i, :], ident[:]).then_inc(sem("rzTx_ps"), 1)

                def spread_z(i):
                    pe.wait_ge(sem("rzTx_ready"), i + 1)
                    for c in range(DC):
                        mm = pe.matmul(bank(6 + i % 2)[:, D + c * P:D + (c + 1) * P], pair_rows[:, c * P:(c + 1) * P], rzTx[:],
                                       start=True, stop=True)
                    mm.then_inc(sem("zfx_ps"), 1)

                def project(i):
                    pe.wait_ge(sem("attx_ready"), i + 1)
                    dense(bank(6 + i % 2)[:, 0:D], lambda c: attTx[:, i % 2, c, :], lambda c: wpx[:, c, :]).then_inc(sem("proj5"), 1)

                pe.wait_ge(sem("in_stage5"), 4 * 16)
                for u in range(3):
                    scores(u)
                for u in range(units + 1):
                    if u + 3 < units:
                        scores(u + 3)
                    if u < units:
                        turn(u)
                    if u > HX and u % HX == 3:
                        turn_z(u // HX - 1)
                    if u > HX and u % HX == 5:
                        spread_z(u // HX - 1)
                    if u > HX and u % HX == 7:
                        project(u // HX - 1)
                    if u % HX == 1 and u > 2 * HX:
                        pe.wait_ge(sem("res5_ready"), u // HX - 1)
                    if u:
                        apply(u - 1)
                turn_z(TT - 1)
                spread_z(TT - 1)
                project(TT - 1)

            def stage6():
                pe.wait_ge(sem("in_stage6"), 3 * 16)
                for i in range(TT):
                    pe.wait_ge(sem("xT_ready5"), i + 1)
                    mm = dense(bank(7)[:, E1 * i:E1 * (i + 1)], tile_of(5, i), lambda c: w_router1[:, c, :])
                mm.then_inc(sem("score1_ps"), 1)

                def up(g):
                    if g >= 2:
                        pe.wait_ge(sem("hidden_ready"), g - 1)
                    xs = lambda c: xT[1][:, c, :]
                    rows = slice(P * g, P * (g + 1))
                    dense(bank(g % 2), lambda c: w_up[:, c, 0, rows], xs)
                    dense(bank(2 + g % 2), lambda c: w_up[:, c, 1, rows], xs).then_inc(sem("up_ps"), 1)

                def spread_gates(g):
                    rows = slice(g * P, (g + 1) * P)
                    pe.matmul(bank(4 + g % 2), spread[:, rows], gate1S, start=True, stop=False)
                    pe.matmul(bank(4 + g % 2), spread[0:E1, rows], gate1L, start=False, stop=True).then_inc(sem("spread_even" if g % 2 == 0 else "spread_odd"), 1)

                pe.wait_ge(sem("in_w_up"), 16)
                up(0)
                up(1)
                pe.wait_ge(sem("picked_ready"), TT)
                for i in range(TT):
                    for k in range(i + 1):
                        mm = pe.matmul(bank(6)[:, E1 * i:E1 * (i + 1)], (tri_b if k == i else ones_b)[:], picked_b[:, k, :],
                                       start=k == 0, stop=k == i)
                mm.then_inc(sem("count_ps"), 1)
                pe.wait_ge(sem("gate1_ready"), 1)
                for i in range(TT):
                    mm = pe.transpose(bank(5)[0:E1, i * P:(i + 1) * P], gate1[:, i, :], ident[:])
                mm.then_inc(sem("gate1T_ps"), 1)

                def down(g):
                    pe.wait_ge(sem("hidden_ready"), g + 1)
                    for i in range(TT):
                        mm = pe.matmul(proj(i), hidden[:, g % 2, i * P:(i + 1) * P], w_down[:, g, :],
                                       start=g == 0 and i % 2 == 0, stop=g == NG - 1, skip_group_check=True)
                        if g == NG - 1:
                            mm.then_inc(sem("proj6"), 1)
                    if g < NG - 1:
                        mm.then_inc(sem("hidden_used"), 1)

                pe.wait_ge(sem("gate1T_ready"), 1)
                dense(bank(5), lambda c: w_su[:, c, :], lambda c: xT[1][:, c, :]).then_inc(sem("shared_ps"), 1)
                pe.wait_ge(sem("gate1S_ready"), 1)
                spread_gates(0)
                pe.wait_ge(sem("score1_ready"), 1)
                pe.wait_ge(sem("in_w_down"), 16)
                down(0)
                up(2)
                spread_gates(2)
                pe.wait_ge(sem("shared_ready"), 1)
                spread_gates(1)
                for i in range(TT):
                    pe.matmul(proj(i), shared[:, i * P:(i + 1) * P], w_sd[:], start=False, stop=False, skip_group_check=True)
                down(1)
                for g in range(2, NG):
                    if g + 1 < NG:
                        up(g + 1)
                        spread_gates(g + 1)
                    down(g)

            unit = [None, None, stage2, stage3, stage4, stage5, stage6]
            for n in range(1, STAGES + 1):
                if n > 1:
                    unit[n]()
                if n < STAGES:
                    transpose_x(n)

        @block.vector
        def _(dve):
            link = linker(dve, "dve_chain")
            TS, TTN, STT = dve.tensor_scalar, dve.tensor_tensor, dve.scalar_tensor_tensor

            dve.wait_ge(sem("in_mix"), 16)
            dve.tensor_reduce(mix_z[:, 0:1], mix, AX.X, ALU.max, negate=True).then_inc(sem("mixmax_ready"), 1)
            dve.wait_ge(sem("in_idx_col"), 16)
            link(TS(idx_col[:], idx_col[:], D.bit_length() - 1, None, ALU.logical_shift_right))
            dve.tensor_copy(row_id, idx_col[:]).then_inc(sem("row_id_ready"), 1)
            dve.wait_ge(sem("mixexp_ready"), 1)
            link(dve.reciprocal(mix_z[:, 2:3], mix_z[:, 1:2]))
            TS(mix, mix, mix_z[:, 2:3], None, ALU.mult).then_inc(sem("mix_ready"), 1)
            dve.wait_ge(sem("first_const_ready"), 1)
            dve.wait_ge(sem("in_idx_row"), 16)
            link(TS(idx_row, idx_row, D - 1, None, ALU.bitwise_and))
            for c in range(DC):
                TS(col_hot[:, c, :], idx_row, part_id[:, c:c + 1], None, ALU.is_equal).then_inc(sem("col_hot_ready"), 1)

            def mask_rows():
                dve.wait_ge(sem("in_mask"), 16)
                link(TS(mask_add[:], mask_u8[:], 1.0, None, ALU.min))
                link(dve.tensor_reduce(valid[:], mask_add[:], AX.X, ALU.max))
                link(TS(mask_add[:], mask_add[:], -1.0, -16 * MASKED, ALU.add, ALU.mult))

            def weigh_entries():
                dve.wait_ge(sem("imp_ready"), 1)
                for k in range(NS // 512):
                    dve.wait_ge(sem("delta_ps"), k + 1)
                    w = weighted[:, 512 * k:512 * (k + 1)]
                    TTN(out=w, in0=bank(k)[0:E0, :], in1=w, op=ALU.mult).then_inc(sem("weighted_ready"), 1)

            for c in range(DC):
                dve.wait_ge(sem("exp_ready"), 2 * c + 1)
                link(STT(out=phi_k, in0=exp_kq[:, 0, :], scalar=1.0, in1=relu_kq[:, 0, :], op0=ALU.min, op1=ALU.add))
                link(TTN(out=kv, in0=phi_k, in1=bank(3 * c + 1), op=ALU.mult))
                if c:
                    dve.wait_ge(sem("num_ready"), c)
                dve.tensor_tensor_scan(kv_sum, keep_state[:], kv, 0.0, ALU.mult, ALU.add)
                link(dve.tensor_tensor_scan(k_sum, keep_state[:], phi_k, 0.0, ALU.mult, ALU.add))
                dve.wait_ge(sem("exp_ready"), 2 * c + 2)
                STT(out=phi_q, in0=exp_kq[:, 1, :], scalar=1.0, in1=relu_kq[:, 1, :], op0=ALU.min,
                    op1=ALU.add).then_inc(sem("phi_ready"), 1)
                dve.wait_ge(sem("phi_ready"), c + 1)
                dve.sem_inc(sem("sums_ready"), 1)
                link(TTN(out=den, in0=phi_q, in1=k_sum, op=ALU.mult))
                link(TS(den, den, EPS_LIN, None, ALU.add))
                link(dve.reciprocal(den, den))
                dve.wait_ge(sem("num_ready"), c + 1)
                TTN(out=lin[:, c, :], in0=num, in1=den, op=ALU.mult).then_inc(sem("lin_ready"), 1)
            mask_rows()

            def norm_stats(n, i):
                link(dve.bn_stats(stats[:, i, :], res[:, i, :]))
                dve.bn_aggr(meanvar[:, i, :], stats[:, i, :]).then_inc(sem("var_ready"), 1)

            def norm_scale(n, i):
                dve.wait_ge(sem("rstd_ready"), nth(n, i))
                TS(x_tok[n % 2][:, i, :], res[:, i, :], meanvar[:, i, 0:1], rstd[:, i:i + 1],
                   ALU.subtract, ALU.mult).then_inc(sem(f"x_ready{n}"), 1)

            def norm(n, residual):
                for i in range(TT):
                    residual(i)
                    norm_stats(n, i)
                    if i:
                        norm_scale(n, i - 1)
                norm_scale(n, TT - 1)

            def projected(n, i):
                dve.wait_ge(sem(f"proj{n}"), 2 * (i // 2) + 2)

            def residual1(i):
                projected(1, i)
                dve.wait_ge(sem("in_x"), 16)
                link(STT(out=res[:, i, :], in0=proj(i), scalar=16 ** -0.5, in1=x_tok[0][:, i, :], op0=ALU.mult, op1=ALU.add))

            def stage2():
                for i in range(TT):
                    dve.wait_ge(sem("s2_ps"), i + 1)
                    link(dve.tensor_tensor_reduce(s2[:, i, :], bank(i), mask_add[:, i // (TT // B), :], 1.0, LOWEST,
                                                  ALU.add, ALU.max, mx2[:, i:i + 1]))
                    TS(nb2[:, i:i + 1], mx2[:, i:i + 1], -1.0 / 16, None, ALU.mult).then_inc(sem("nb2_ready"), 1)
                for i in range(TT):
                    dve.wait_ge(sem("p2_ready"), i + 1)
                    link(dve.reciprocal(rz2[:, i:i + 1], z2[:, i:i + 1]))
                    link(TS(rz2[:, i:i + 1], rz2[:, i:i + 1], valid[:, i // (TT // B):i // (TT // B) + 1], None, ALU.mult))

            def residual2(i):
                projected(2, i)
                link(STT(out=res[:, i, :], in0=proj(i), scalar=rz2[:, i:i + 1], in1=x_tok[1][:, i, :], op0=ALU.mult, op1=ALU.add))

            def residual(n):
                def add(i):
                    projected(n, i)
                    link(TTN(out=res[:, i, :], in0=proj(i), in1=x_tok[(n - 1) % 2][:, i, :], op=ALU.add))
                return add

            def stage3():
                weigh_entries()
                dve.wait_ge(sem("logit0_ps"), 1)
                link(TS(logit0.rearrange("p i e -> p (i e)"), bank(0)[:, 0:TT * E0], -50.0, 50.0, ALU.max, ALU.min))
                for i in range(TT):
                    last = dve.max(top0[:, i, :], logit0[:, i, :])
                link(last)
                for i in range(TT):
                    last = dve.max_index(idx0[:, i, :], top0[:, i, :], logit0[:, i, :])
                link(last)
                TTN(out=gap0, in0=top0[:, :, 1], in1=top0[:, :, 0], op=ALU.subtract).then_inc(sem("gap0_ready"), 1)
                link(dve.tensor_copy(idx0f, idx0))
                ids = iota_row[:, 0:E0].unsqueeze(1).broadcast_to([P, TT, E0])
                for k, hot_k in ((0, hot0), (1, hot1)):
                    link(TTN(out=hot_k, in0=idx0f[:, :, k:k + 1].broadcast_to([P, TT, E0]), in1=ids, op=ALU.is_equal))
                dve.wait_ge(sem("exp0_ready"), 1)
                link(TS(w10, exp0, 1.0, None, ALU.add))
                link(dve.reciprocal(w10, w10))
                link(TTN(out=w20, in0=w10, in1=exp0, op=ALU.mult))
                for hot_k, w in ((hot0, w10), (hot1, w20)):
                    link(TTN(out=hot_k, in0=hot_k, in1=w.unsqueeze(2).broadcast_to([P, TT, E0]), op=ALU.mult))
                TTN(out=gate0, in0=hot0, in1=hot1, op=ALU.add).then_inc(sem("gate0_ready"), 1)
                dve.wait_ge(sem("x_high_ready"), 1)
                link(TTN(out=x_rest, in0=xT[0][:], in1=x_parts[0], op=ALU.subtract))
                link(dve.tensor_copy(x_parts[1], x_rest))
                TTN(out=x_parts[2], in0=x_rest, in1=x_parts[1], op=ALU.subtract).then_inc(sem("x_parts_ready"), 1)

                def quantise(am, sc, rs):
                    link(TS(sc, am, 1.0 / 127, 1e-8, ALU.mult, ALU.max))
                    link(dve.reciprocal(rs, sc))

                def quantise_keys(k):
                    z = kx[:, k, :]
                    heads = z.rearrange("p (h d) -> p h d", h=HX)
                    dve.wait_ge(sem("kx_out"), k + 1)
                    link(TTN(out=z, in0=z, in1=bkx[:], op=ALU.add))
                    link(dve.tensor_reduce(kam[:, k, :], heads, AX.X, ALU.max, apply_absolute_value=True))
                    quantise(kam[:, k, :], ksc[:, k, :], krs[:, k, :])
                    if k >= 2:
                        dve.wait_ge(sem("ks_ready"), k - 1)
                    r = kr[:, k % 2, :]
                    link(TTN(out=r.rearrange("p (h d) -> p h d", h=HX), in0=heads,
                             in1=krs[:, k, :].unsqueeze(2).broadcast_to([P, HX, DHX]), op=ALU.mult))
                    link(TS(r, r, ROUND, ROUND, ALU.add, ALU.subtract))
                    TS(r, r, 127.0, -127.0, ALU.min, ALU.max).then_inc(sem("kr_ready"), 1)

                def quantise_values(c):
                    dve.wait_ge(sem("vTx_ready"), B * (c + 1))
                    link(dve.tensor_reduce(vam[:, c:c + 1], vTx[:, c, :], AX.X, ALU.max, apply_absolute_value=True))
                    quantise(vam[:, c:c + 1], vsc[:, c:c + 1], vrs[:, c:c + 1])
                    link(TS(vr, vTx[:, c, :], vrs[:, c:c + 1], ROUND, ALU.mult, ALU.add))
                    link(TS(vr, vr, ROUND, 127.0, ALU.subtract, ALU.min))
                    link(TS(ivT[:, c, :], vr, -127.0, None, ALU.max))

                quantise_keys(0)
                for j in range(SJ):
                    dve.wait_ge(sem("vals_ready"), j + 1)
                    if j >= 2:
                        dve.wait_ge(sem("prod_used"), j - 1)
                    TTN(out=prod[:, j % 2, :], in0=bank(2 if j % 2 else 1), in1=vals[:, j % 2, :],
                        op=ALU.mult).then_inc(sem("prod_ready"), 1)
                    if j % 2 == 0 and j // 2 + 1 < KT:
                        quantise_keys(j // 2 + 1)
                    if j in VALUES_AT:
                        quantise_values(VALUES_AT.index(j))

            def stage4():
                dve.wait_ge(sem("const_ready"), 1)
                link(dve.tensor_reduce(head_sel[:], head_of[:].rearrange("p g j -> p j g"), AX.X, ALU.add))
                dve.sem_inc(sem("head_sel_ready"), 1)
                link(dve.tensor_reduce(unit_sel[:], head_of[:], AX.X, ALU.add))
                link(TS(unit_sel[:], unit_sel[:], DH1 ** -0.5, None, ALU.mult))
                for c in range(DC):
                    dve.wait_ge(sem("qk1_ps"), 2 * c + 1)
                    for g in range(UC):
                        q = TS(qT1[:, c * UC + g, :], bank(2 * c), unit_sel[:, g:g + 1], None, ALU.mult)
                    q.then_inc(sem("qT1_ready"), 1)
                dve.wait_ge(sem("v1_cleared"), 1)
                units_v = v1.rearrange("p (t j) w -> p t j w", j=HU)
                for k in range(TT // 2):
                    dve.wait_ge(sem("v1_ps"), 2 * k + 2)
                    heads = bank(4 + k).rearrange("p (t j d) -> p t j d", j=HU, d=DH1)
                    for j in range(HU):
                        v = dve.tensor_copy(units_v[:, 2 * k * (H1 // HU):2 * (k + 1) * (H1 // HU), j, j * DH1:(j + 1) * DH1],
                                            heads[:, :, j, :])
                    v.then_inc(sem("v1_ready"), 1)

                def maxima(u):
                    nk = 1 + u // (H1 // HU) % 2
                    dve.wait_ge(sem("s1_ps"), u + 1)
                    if u >= 2:
                        dve.wait_ge(sem("p1_ready"), u - 1)
                    for j in range(HU):
                        m = dve.tensor_tensor_reduce(s1[u % 2][:, j, 0:nk * P].rearrange("p (b k) -> p b k", b=nk),
                                                     unit_s1(u)[:, 0:nk, j, :], window[:, 2 - nk:2, :], -1.0, -LOWEST,
                                                     ALU.add, ALU.min, nmx1[:, u % 2, j:j + 1])
                    m.then_inc(sem("max1_ready"), 1)

                def evacuate(u):
                    nk = 1 + u // (H1 // HU) % 2
                    dve.wait_ge(sem("pT1_ps"), u + 1)
                    if u >= 2:
                        dve.wait_ge(sem("o1_ps"), u - 1)
                    src = bank(4, 2).rearrange("p (j b q) -> p j b q", b=2, j=HU)[:, :, 0:nk, :]
                    dve.tensor_copy(unit_pT1(u)[:, :, 0:nk, :], src).then_inc(sem("pT1_ready"), 1)

                def invert_z(i):
                    dve.wait_ge(sem("p1_ready"), H1 // HU * (i + 1))
                    dve.reciprocal(rz1[:, i, :], z1[:, i, :]).then_inc(sem("rz1_ready"), 1)

                def take_sums(i):
                    dve.wait_ge(sem("o1_ps"), H1 // HU * (i + 1))
                    dve.tensor_copy(attT1[:, i % 2].rearrange("p c q -> p (c q)"), bank(6)[:, 0:D]).then_inc(sem("sums1_out"), 1)

                def take_z(i):
                    dve.wait_ge(sem("rzT1_ps"), i + 1)
                    dve.tensor_copy(rzT1, bank(7)[0:H1, 0:P]).then_inc(sem("rzT1_ready"), 1)

                def normalise(i):
                    dve.wait_ge(sem("zf1_ps"), i + 1)
                    dve.wait_ge(sem("sums1_out"), i + 1)
                    a = attT1[:, i % 2].rearrange("p c q -> p (c q)")
                    TTN(out=a, in0=bank(7)[:, P:P + D], in1=a, op=ALU.mult).then_inc(sem("att1_ready"), 1)

                def add(i):
                    dve.wait_ge(sem("proj4"), i + 1)
                    TTN(out=res[:, i, :], in0=bank(7)[:, 0:D], in1=x_tok[1][:, i, :], op=ALU.add).then_inc(sem("res4_ready"), 1)
                    dve.wait_ge(sem("res4_ready"), i + 1)

                per = H1 // HU
                units = TT * per
                maxima(0)
                dve.wait_ge(sem("iv_ps"), DC)
                maxima(1)
                dve.wait_ge(sem("ivh_cleared"), 1)
                for c in range(DC):
                    dve.wait_ge(sem("iv_ps"), c + 1)
                    src = bank(6 + c).bitcast(BF16).rearrange("p (k g j d) -> p k g j d", k=KT, j=2, d=DHX)
                    dst = ivh.rearrange("p (k c g j) (l d) -> p k c g j l d", k=KT, c=DC, j=2, l=2)
                    for j in range(2):
                        v = dve.tensor_copy(dst[:, :, c, :, j, j, :], src[:, :, :, j, :])
                    v.then_inc(sem("ivtok_ready"), 1)
                for u in range(units):
                    i = u // per - 1
                    if i >= 0 and u % per == 1:
                        take_sums(i)
                    if i >= 0 and u % per == 2:
                        take_z(i)
                    if i >= 0 and u % per == 3:
                        normalise(i)
                    if u + 2 < units:
                        maxima(u + 2)
                    evacuate(u)
                    if i >= 0 and u % per == 0:
                        invert_z(i)
                    if i >= 0 and u % per == 5:
                        add(i)
                        norm_stats(4, i)
                    if i >= 0 and u % per == 6:
                        norm_scale(4, i)
                invert_z(TT - 1)
                take_sums(TT - 1)
                take_z(TT - 1)
                normalise(TT - 1)
                add(TT - 1)
                norm_stats(4, TT - 1)
                norm_scale(4, TT - 1)

            def stage5():
                dve.wait_ge(sem("in_stage5"), 4 * 16)
                for i in range(0, TT, 2):
                    dve.wait_ge(sem("qx_ps"), i + 2)
                    TTN(out=qx[:, i:i + 2, :], in0=bank(i // 2).rearrange("p (i d) -> p i d", i=2),
                        in1=bqx[:].unsqueeze(1).broadcast_to([P, 2, D]), op=ALU.add).then_inc(sem("qx_ready"), 1)
                dve.wait_ge(sem("qx_ready"), TT // 2)
                scale = DHX ** -0.5
                flat = qx.rearrange("p i d -> p (i d)")
                heads = flat.rearrange("p (h d) -> p h d", d=DHX)
                qam_, qsc_, qrs_ = (z.rearrange("p i h -> p (i h)") for z in (qam, qsc, qrs))
                link(dve.tensor_reduce(qam_, heads, AX.X, ALU.max, apply_absolute_value=True))
                link(TS(qsc_, qam_, scale / 127, 1e-8, ALU.mult, ALU.max))
                link(dve.reciprocal(qrs_, qsc_))
                link(TTN(out=heads, in0=heads, in1=qrs_.unsqueeze(2).broadcast_to([P, TT * HX, DHX]), op=ALU.mult))
                link(TS(flat, flat, scale, ROUND, ALU.mult, ALU.add))
                TS(flat, flat, ROUND, 127.0, ALU.subtract, ALU.min).then_inc(sem("q_rounded"), 1)
                dve.wait_ge(sem("q_rounded"), 1)
                stack = qstack.rearrange("p i (h w) -> p (i h) w", w=KW)
                for k in range(3):
                    q = TS(stack[:, :, k * DHX:(k + 1) * DHX], heads, -127.0, None, ALU.max)
                q.then_inc(sem("qstack_ready"), 1)
                dve.wait_ge(sem("qTx_cleared"), 1)
                for c in range(HX // 2):
                    dve.wait_ge(sem("qTx_ps"), c + 1)
                    dve.tensor_copy(qTx[KW:2 * KW, c, 1, :], bank(6 + c % 2)[KW:2 * KW, 0:N // 2].bitcast(BF16)).then_inc(sem("qTx_odd"), 1)

                def maximum(u):
                    dve.wait_ge(sem("sx_ps"), u + 1)
                    if u >= 3:
                        dve.wait_ge(sem("px_ready"), u - 2)
                    dve.tensor_tensor_reduce(sx[:, u % 3, :], bank(2 * (u % 2), 2), zero[:].broadcast_to([P, B * M]),
                                             qsc[:, u // HX, u % HX:u % HX + 1], LOWEST, ALU.add, ALU.max,
                                             mxx[:, u:u + 1]).then_inc(sem("maxx_ready"), 1)

                def evacuate(u):
                    dve.wait_ge(sem("pTx_ps"), u + 1)
                    if u >= 2:
                        dve.wait_ge(sem("ox_ps"), u - 1)
                    dve.tensor_copy(pTx[:, u % 2, :], bank(4 + u % 2).bitcast(I16)).then_inc(sem("pTx_dve"), 1)

                def invert_z(i):
                    dve.wait_ge(sem("px_ready"), HX * (i + 1))
                    dve.reciprocal(rzx[:, i, :], zx[:, i, :]).then_inc(sem("rzx_ready"), 1)

                def normalise(i):
                    dve.wait_ge(sem("zfx_ps"), i + 1)
                    a = attTx[:, i % 2].rearrange("p c q -> p (c q)")
                    TTN(out=a, in0=bank(6 + i % 2)[:, D:2 * D], in1=a, op=ALU.mult).then_inc(sem("attx_ready"), 1)

                def add(i):
                    dve.wait_ge(sem("proj5"), i + 1)
                    dve.wait_ge(sem("bias_added"), 1)
                    TTN(out=res[:, i, :], in0=bank(6 + i % 2)[:, 0:D], in1=x_tok[0][:, i, :], op=ALU.add).then_inc(sem("res5_ready"), 1)
                    dve.wait_ge(sem("res5_ready"), i + 1)

                units = TT * HX
                maximum(0)
                maximum(1)
                for u in range(units):
                    if u + 2 < units:
                        maximum(u + 2)
                    if not by_scalar(u):
                        evacuate(u)
                    if u >= HX:
                        i = u // HX - 1
                        if u % HX == 1:
                            invert_z(i)
                        if u % HX == 6:
                            normalise(i)
                        if u % HX == 8:
                            add(i)
                            norm_stats(5, i)
                        if u % HX == NORM_AT:
                            norm_scale(5, i)
                invert_z(TT - 1)
                normalise(TT - 1)
                add(TT - 1)
                norm_stats(5, TT - 1)
                norm_scale(5, TT - 1)

            def stage6():
                dve.wait_ge(sem("score1_ready"), 1)
                ids = iota_row[:, 0:E1].unsqueeze(1).broadcast_to([P, TOPK, E1])
                for i in range(TT):
                    last = dve.max(top1[:, i, :], score1[:, i, :])
                link(last)
                for i in range(TT):
                    last = dve.max_index(idx1[:, i, :], top1[:, i, :], score1[:, i, :])
                link(last)
                link(dve.tensor_copy(idx1f, idx1))
                link(dve.tensor_reduce(sum1, top1[:, :, 0:TOPK], AX.X, ALU.add))
                link(dve.reciprocal(rsum1, sum1))
                for i in range(TT):
                    link(TTN(out=hot, in0=idx1f[:, i, 0:TOPK].unsqueeze(2).broadcast_to([P, TOPK, E1]), in1=ids, op=ALU.is_equal))
                    link(dve.tensor_reduce(picked[:, i, :], hot.rearrange("p k e -> p e k"), AX.X, ALU.add))
                    dve.tensor_copy(picked_b[:, i, :], picked[:, i, :]).then_inc(sem("picked_ready"), 1)
                link(TTN(out=gate1, in0=picked, in1=score1, op=ALU.mult))
                link(TTN(out=gate1, in0=gate1, in1=rsum1.unsqueeze(2).broadcast_to([P, TT, E1]), op=ALU.mult))
                dve.wait_ge(sem("count_ps"), 1)
                flat = gate1.rearrange("p i e -> p (i e)")
                STT(out=flat, in0=bank(6)[:, 0:TT * E1], scalar=float(CAP), in1=flat, op0=ALU.is_le, op1=ALU.mult).then_inc(sem("gate1_ready"), 1)
                dve.wait_ge(sem("gate1T_ready"), 1)
                high, middle = gate1S[0:E1, :], gate1S[E1:2 * E1, :]
                link(dve.tensor_copy(high, gate1T))
                link(TTN(out=gate1T, in0=gate1T, in1=high, op=ALU.subtract))
                link(dve.tensor_copy(middle, gate1T))
                TTN(out=gate1L, in0=gate1T, in1=middle, op=ALU.subtract).then_inc(sem("gate1S_ready"), 1)
                for g in range(NG):
                    s = g % 2
                    dve.wait_ge(sem("silu_ready"), g + 1)
                    link(TTN(out=gated[:, s, :], in0=bank(2 + s), in1=silu[:, s, :], op=ALU.mult))
                    if g >= 2:
                        dve.wait_ge(sem("hidden_used"), g - 1)
                    dve.wait_ge(sem("spread_odd" if s else "spread_even"), g // 2 + 1)
                    TTN(out=hidden[:, s, :], in0=bank(4 + s), in1=gated[:, s, :], op=ALU.mult).then_inc(sem("hidden_ready"), 1)
                    if g == 0:
                        dve.wait_ge(sem("silu_shared_ready"), 1)
                        TTN(out=shared, in0=bank(5)[0:HS, :], in1=silu_shared, op=ALU.mult).then_inc(sem("shared_ready"), 1)

            work = [None, None, stage2, stage3, stage4, stage5, stage6]
            adds = [None, residual1, residual2, residual(3), None, None, residual(6)]
            for n in range(1, STAGES + 1):
                if n > 1:
                    work[n]()
                if adds[n]:
                    norm(n, adds[n])


def _layout(a):
    def rows(v, shape):
        return np.broadcast_to(v, (P,) + shape)

    x = a["x"].reshape(N, D)
    ctx = a["ctx_2048"].reshape(B * M, D)
    idx = a["L0_ffn_mask_idx"]
    return {
        "x": x, "xT": x.T, "w_qkv0": a["L0_attn_W_qkv"].T, "w_out0": a["L0_attn_W_out"].T,
        "ctx": ctx, "ctxT": ctx.T, "mask": rows(a["mask_BxS2_bk0"], (B, M)),
        "w_router0": a["L0_ffn_gate_w"].T, "w_ffn0": a["L0_ffn_W"].T, "atoms": a["L0_ffn_atoms"],
        "mix": a["L0_ffn_expert_atom_weights"], "imp": a["L0_ffn_importance"],
        "idx": idx, "idx_row": rows(idx, (NS,)),
        "wq1": a["L1_attn_Wq"].T, "wk1": a["L1_attn_Wk"].T, "wv1": a["L1_attn_Wv"].T, "wo1": a["L1_attn_Wo"].T,
        "wqx": a["L1_xattn_Wq"], "wkvx": a["L1_xattn_Wkv"], "wpx": a["L1_xattn_Wp"],
        "bqx": rows(a["L1_xattn_bq"], (D,)), "bkx": rows(a["L1_xattn_bkv"][0:D], (D,)),
        "bvx": a["L1_xattn_bkv"][D:2 * D].reshape(DC, P).T, "bpx": rows(a["L1_xattn_bp"], (D,)),
        "w_router1": a["L1_ffn_w_gate"], "w_su": a["L1_ffn_w_shared_up"], "w_sd": a["L1_ffn_w_shared_down"],
        "w_up": a["L1_ffn_w_up"].reshape(E1, DC, P, 2, HE).transpose(2, 1, 3, 0, 4).reshape(P, -1), "w_down": a["L1_ffn_w_down"].reshape(E1 * HE, D),
    }


def kernel(**inputs):
    import numpy as _np
    import concourse.bacc as _bacc
    from concourse import mybir as _mybir
    from concourse.bass_utils import run_bass_kernel_spmd as _run

    nc = _bacc.Bacc("TRN2", target_bir_lowering=False, num_devices=1)
    arrays, tensors = {}, {}
    for name, a in _layout({k: _np.asarray(v) for k, v in inputs.items()}).items():
        a = _np.ascontiguousarray(a)
        arrays[f"in_{name}_dram"] = a
        tensors[name] = nc.dram_tensor(f"in_{name}_dram", a.shape, _mybir.dt.from_np(a.dtype), kind="ExternalInput").ap()
    out = nc.dram_tensor("out_0_dram", (N, D), _mybir.dt.float32, kind="ExternalOutput").ap()
    build(nc, tensors, out)
    r = _run(nc, [arrays], core_ids=[0])
    return r.results[0]["out_0_dram"].reshape(B, S, D)
```
